# Optimizing a Trainium2 kernel written in Bass

```python
import numpy as np
import jax
import jax.numpy as jnp

def _softmax(x, axis=-1):
    return jax.nn.softmax(x, axis=axis)

def _gelu(x):
    return jax.nn.gelu(x, approximate=True)

def _silu(x):
    return jax.nn.silu(x)

def _sigmoid(x):
    return jax.nn.sigmoid(x)

def _layernorm(x, axis=-1, eps=1e-05):
    m = jnp.mean(x, axis=axis, keepdims=True)
    v = jnp.var(x, axis=axis, keepdims=True)
    return (x - m) / jnp.sqrt(v + eps)

def _scatter_add(tgt, idx, src, axis=0):
    return tgt.at[idx].add(src)

def _segment_sum(src, seg, n):
    return jax.ops.segment_sum(src, seg, n)
kernel_name = 'mk_seq_postln_d1_jaxref_r8_859f54'

def setup_inputs(seed: int=0):
    np.random.seed(seed)
    _w = jnp.asarray

    def _L0_attn_setup():
        import jax, jax.numpy as jnp
        import numpy as np
        H = 8
        D = 64
        E = 128

        def sinusoidal_pe(T, d, dtype=jnp.float32):
            pos = jnp.arange(T, dtype=jnp.float32)[:, None]
            div = jnp.exp(jnp.arange(0, d, 2, dtype=jnp.float32) * (-np.log(10000.0) / d))
            ang = pos * div
            pe = jnp.stack([jnp.sin(ang), jnp.cos(ang)], axis=-1).reshape(T, d)
            return pe.astype(dtype)
        key = jax.random.key(seed)
        k1, k2, k3 = jax.random.split(key, 3)
        B, T = (2, 256)
        x = jax.random.normal(k1, (B, T, E), dtype=jnp.float32)
        Wqkv = jax.random.normal(k2, (3 * H * D, E), dtype=jnp.float32) * (1.0 / np.sqrt(E))
        Wo = jax.random.normal(k3, (E, H * D), dtype=jnp.float32) * (1.0 / np.sqrt(H * D))
        return {'x': x, 'Wqkv': Wqkv, 'Wo': Wo}
    _L0_attn_in = _L0_attn_setup()

    def _L0_ffn_setup():
        import jax, jax.numpy as jnp
        import numpy as np
        from jax.scipy.linalg import expm
        D = 128
        E = 6
        K = 2
        H = 2 * D
        A4 = 4 * D
        NROT = 4
        LN_EPS = 1e-05

        def _xavier(key, shape):
            fan_in, fan_out = (shape[-2], shape[-1])
            lim = np.sqrt(6.0 / (fan_in + fan_out))
            return jax.random.uniform(key, shape, jnp.float32, -lim, lim)

        def _layernorm(x, g, b):
            mu = jnp.mean(x, axis=-1, keepdims=True)
            var = jnp.var(x, axis=-1, keepdims=True)
            return (x - mu) * jax.lax.rsqrt(var + LN_EPS) * g + b

        def _moe(xn, gate_w, gate_b, ew1, eb1, ew2, eb2):
            logits = xn @ gate_w + gate_b
            tw, ti = jax.lax.top_k(logits, K)
            tw = jax.nn.softmax(tw, axis=-1)
            w_full = jnp.sum(tw[..., None] * jax.nn.one_hot(ti, E, dtype=tw.dtype), axis=-2)
            h = jax.nn.gelu(jnp.einsum('bsd,edh->besh', xn, ew1) + eb1[None, :, None, :], approximate=False)
            eo = jnp.einsum('besh,ehd->besd', h, ew2) + eb2[None, :, None, :]
            return jnp.einsum('bse,besd->bsd', w_full, eo)

        def _rotate(x, gens):
            for i in range(NROT):
                x = x @ expm(gens[i])
            return x
        key = jax.random.key(seed)
        ks = jax.random.split(key, 16)
        x = jax.random.normal(ks[0], (4, 256, D), jnp.float32)
        gens_raw = _xavier(ks[1], (NROT, D, D))
        gens = 0.5 * (gens_raw - jnp.swapaxes(gens_raw, -1, -2))
        return {'x': x, 'ln_g': jnp.ones((D,), jnp.float32), 'ln_b': jnp.zeros((D,), jnp.float32), 'aw1': _xavier(ks[2], (D, A4)), 'ab1': jnp.zeros((A4,), jnp.float32), 'aw2': _xavier(ks[3], (A4, D)), 'ab2': jnp.zeros((D,), jnp.float32), 'gate_w': _xavier(ks[4], (D, E)), 'gate_b': jnp.zeros((E,), jnp.float32), 'ew1': _xavier(ks[5], (E, D, H)), 'eb1': jnp.zeros((E, H), jnp.float32), 'ew2': _xavier(ks[6], (E, H, D)), 'eb2': jnp.zeros((E, D), jnp.float32), 'gens': gens, 'gc_w': _xavier(ks[7], (2 * D, 1)), 'gc_b': jnp.zeros((1,), jnp.float32)}
    _L0_ffn_in = _L0_ffn_setup()
    _d = {'L0_attn_x': _L0_attn_in['x'], 'L0_attn_Wqkv': _L0_attn_in['Wqkv'], 'L0_attn_Wo': _L0_attn_in['Wo'], 'L0_ffn_ln_g': _L0_ffn_in['ln_g'], 'L0_ffn_ln_b': _L0_ffn_in['ln_b'], 'L0_ffn_aw1': _L0_ffn_in['aw1'], 'L0_ffn_ab1': _L0_ffn_in['ab1'], 'L0_ffn_aw2': _L0_ffn_in['aw2'], 'L0_ffn_ab2': _L0_ffn_in['ab2'], 'L0_ffn_gate_w': _L0_ffn_in['gate_w'], 'L0_ffn_gate_b': _L0_ffn_in['gate_b'], 'L0_ffn_ew1': _L0_ffn_in['ew1'], 'L0_ffn_eb1': _L0_ffn_in['eb1'], 'L0_ffn_ew2': _L0_ffn_in['ew2'], 'L0_ffn_eb2': _L0_ffn_in['eb2'], 'L0_ffn_gens': _L0_ffn_in['gens'], 'L0_ffn_gc_w': _L0_ffn_in['gc_w'], 'L0_ffn_gc_b': _L0_ffn_in['gc_b']}
    _x0 = _d['L0_attn_x']
    _d['L0_attn_x'] = jax.random.normal(jax.random.fold_in(jax.random.key(seed), 1), (1, 2048, 128), dtype=_x0.dtype)
    del _x0
    return _d

def reference(L0_attn_x, L0_attn_Wqkv, L0_attn_Wo, L0_ffn_ln_g, L0_ffn_ln_b, L0_ffn_aw1, L0_ffn_ab1, L0_ffn_aw2, L0_ffn_ab2, L0_ffn_gate_w, L0_ffn_gate_b, L0_ffn_ew1, L0_ffn_eb1, L0_ffn_ew2, L0_ffn_eb2, L0_ffn_gens, L0_ffn_gc_w, L0_ffn_gc_b):

    def _L0_attn_ref(x, Wqkv, Wo):
        import jax, jax.numpy as jnp
        import numpy as np
        H = 8
        D = 64
        E = 128

        def sinusoidal_pe(T, d, dtype=jnp.float32):
            pos = jnp.arange(T, dtype=jnp.float32)[:, None]
            div = jnp.exp(jnp.arange(0, d, 2, dtype=jnp.float32) * (-np.log(10000.0) / d))
            ang = pos * div
            pe = jnp.stack([jnp.sin(ang), jnp.cos(ang)], axis=-1).reshape(T, d)
            return pe.astype(dtype)
        B, T, _ = x.shape
        qkv = jnp.einsum('bte,fe->btf', x, Wqkv)
        qkv = qkv.reshape(B, T, H, 3 * D)
        q, k, v = jnp.split(qkv, 3, axis=-1)
        q = q.transpose(0, 2, 1, 3)
        k = k.transpose(0, 2, 1, 3)
        v = v.transpose(0, 2, 1, 3)
        pe = sinusoidal_pe(T, D, q.dtype)
        q = q + pe[None, None]
        k = k + pe[None, None]
        causal = jnp.tril(jnp.ones((T, T), dtype=bool))
        scores = jnp.einsum('bhtd,bhsd->bhts', q, k) / jnp.sqrt(jnp.asarray(D, q.dtype))
        scores = jnp.where(causal[None, None], scores, jnp.asarray(-jnp.inf, q.dtype))
        probs = jax.nn.softmax(scores, axis=-1)
        attn = jnp.einsum('bhts,bhsd->bhtd', probs, v)
        out = attn.transpose(0, 2, 1, 3).reshape(B, T, H * D)
        out = jnp.einsum('btf,ef->bte', out, Wo)
        return out

    def _L0_ffn_ref(x, ln_g, ln_b, aw1, ab1, aw2, ab2, gate_w, gate_b, ew1, eb1, ew2, eb2, gens, gc_w, gc_b):
        import jax, jax.numpy as jnp
        import numpy as np
        from jax.scipy.linalg import expm
        D = 128
        E = 6
        K = 2
        H = 2 * D
        A4 = 4 * D
        NROT = 4
        LN_EPS = 1e-05

        def _xavier(key, shape):
            fan_in, fan_out = (shape[-2], shape[-1])
            lim = np.sqrt(6.0 / (fan_in + fan_out))
            return jax.random.uniform(key, shape, jnp.float32, -lim, lim)

        def _layernorm(x, g, b):
            mu = jnp.mean(x, axis=-1, keepdims=True)
            var = jnp.var(x, axis=-1, keepdims=True)
            return (x - mu) * jax.lax.rsqrt(var + LN_EPS) * g + b

        def _moe(xn, gate_w, gate_b, ew1, eb1, ew2, eb2):
            logits = xn @ gate_w + gate_b
            tw, ti = jax.lax.top_k(logits, K)
            tw = jax.nn.softmax(tw, axis=-1)
            w_full = jnp.sum(tw[..., None] * jax.nn.one_hot(ti, E, dtype=tw.dtype), axis=-2)
            h = jax.nn.gelu(jnp.einsum('bsd,edh->besh', xn, ew1) + eb1[None, :, None, :], approximate=False)
            eo = jnp.einsum('besh,ehd->besd', h, ew2) + eb2[None, :, None, :]
            return jnp.einsum('bse,besd->bsd', w_full, eo)

        def _rotate(x, gens):
            for i in range(NROT):
                x = x @ expm(gens[i])
            return x
        residual = x
        xn = _layernorm(x, ln_g, ln_b)
        abel = jax.nn.gelu(xn @ aw1 + ab1, approximate=False) @ aw2 + ab2
        nonabel = _rotate(_moe(xn, gate_w, gate_b, ew1, eb1, ew2, eb2), gens)
        combined = jnp.concatenate([abel, nonabel], axis=-1)
        gate = jax.nn.sigmoid(combined @ gc_w + gc_b)
        mixed = abel * (1.0 - gate) + nonabel * gate
        return residual + mixed
    x = L0_attn_x
    x = _layernorm(x + _L0_attn_ref(x, L0_attn_Wqkv, L0_attn_Wo), axis=-1)
    x = _layernorm(x + _L0_ffn_ref(x, L0_ffn_ln_g, L0_ffn_ln_b, L0_ffn_aw1, L0_ffn_ab1, L0_ffn_aw2, L0_ffn_ab2, L0_ffn_gate_w, L0_ffn_gate_b, L0_ffn_ew1, L0_ffn_eb1, L0_ffn_ew2, L0_ffn_eb2, L0_ffn_gens, L0_ffn_gc_w, L0_ffn_gc_b), axis=-1)
    return x

_drawn_inputs = setup_inputs


def setup_inputs(seed=0):
    import zlib

    import numpy as np

    out = dict(_drawn_inputs(seed))
    spreads = {'L0_ffn_ln_g': (1.0, 0.2),
     'L0_ffn_ln_b': (0.0, 0.1),
     'L0_ffn_ab1': (0.0, 0.411),
     'L0_ffn_ab2': (0.0, 0.297),
     'L0_ffn_gate_b': (0.0, 0.336),
     'L0_ffn_eb1': (0.0, 0.549),
     'L0_ffn_eb2': (0.0, 0.411)}
    factors = {}
    for name, (base, spread) in spreads.items():
        noise = np.random.default_rng([zlib.crc32(name.encode()), seed]).standard_normal(out[name].shape)
        drawn = base * np.exp(spread * noise) if base else spread * noise
        out[name] = jnp.asarray(drawn.astype(out[name].dtype))
    for name, factor in factors.items():
        out[name] = (out[name] * factor).astype(out[name].dtype)
    return out
```

```python
from contextlib import ExitStack

import concourse.bass as bass
from concourse import mybir

F32 = mybir.dt.float32
F32R = mybir.dt.float32r
BF16 = mybir.dt.bfloat16
ALU = mybir.AluOpType
ACT = mybir.ActivationFunctionType
AX = mybir.AxisListType

P = 128
T = 2048
E = 128
H = 8
D = 64
CH = 512
NC = T // CH
NT = T // P
TPC = CH // P
NEG = -1e30
LEAD = 20

PAIRS = [2 * (c + 1) for c in range(NC)]
PAIR0 = [sum(PAIRS[:c]) for c in range(NC + 1)]
NP = PAIR0[NC]
UNIT0 = [sum(TPC * (b + 1) for b in range(c)) for c in range(NC + 1)]
NU = UNIT0[NC]
I32 = mybir.dt.int32

EPS = 1e-5

NA = 4
NX = 6
NXB = 2
NB = NA + NX * NXB
N_VEC = 5 + NB
NROT = 4
TAYLOR = 8
HALVINGS = 8
LAG = 3
RING = 4
LN_STEPS = 17
NORM_STEPS = (2, 2, 7, 6)

LAYER1 = [P * j if j < NA else 2 * NA * P + P * (j - NA) for j in range(NB)]
LAYER2 = [NA * P + P * j if j < NA else 2 * NA * P + NX * NXB * P + P * (j - NA) for j in range(NB)]
W_COLS = 2 * NB * P
W_PARTS = 4

T_ABEL, T_SPLIT, T_ROTATE, T_NONABEL, T_GATE, T_TANH, T_MIX, T_TURN, T_NORM = 1, 3, 5, 6, 7, 8, 9, 11, 12


def chunk_of(starts, n):
    return max(c for c in range(NC) if starts[c] <= n)


def at(g, per, local):
    i, offset = g
    return i * (2 * per) + (offset * per + local)


def plus(g, n):
    return (g[0], g[1] + n)


def index(g):
    return g[0] * 2 + g[1]


def wait(eng, sem, value):
    if not isinstance(value, int) or value > 0:
        eng.wait_ge(sem, value)


PROJECT_Q = {4: (0, 1), 7: (1, 1), 13: (2, 1), 19: (3, 1)}
PROJECT_K = {5: (0, 1), 8: (1, 1), 14: (2, 1), 17: (3, 1)}
TURN = {2: (2, 0), 10: (3, 0), 12: (0, 1), 16: (1, 1)}
OUTPUT = {6: (3, -1), 9: (0, 0), 15: (1, 0), 18: (2, 0)}


def due(table, p, after, cur, nxt, prev):
    for slot, (c, ahead) in table.items():
        if (slot + after) % NP == p:
            ahead -= (slot + after) // NP
            if (nxt if ahead > 0 else prev if ahead < 0 else cur):
                return [(c, ahead)]
    return []


DONE = {PAIR0[c + 1] + 2: (c, 0) for c in range(NC)}


def attention(nc, acc, ident, x, w_qkv, w_o, pe2):
    with ExitStack() as ctx:
        def sb(name, shape, dt=F32):
            return ctx.enter_context(nc.sbuf_tensor(name, shape, dt))

        def psum(name, shape, dt=F32):
            return ctx.enter_context(nc.psum_tensor(name, shape, dt))

        def sem(name):
            return ctx.enter_context(nc.semaphore(name))

        xh = sb("xh", [P, T], F32R)
        xl = sb("xl", [P, T], F32R)
        wth = sb("wth", [P, H, 2, D], F32R)
        wtl = sb("wtl", [P, H, 2, D], F32R)
        woh = sb("woh", [P, H, E], F32R)
        wol = sb("wol", [P, H, E], F32R)
        w_head = sb("w_head", [P, 4, P], F32R)
        wo_head = sb("wo_head", [P, 2, 2, E], F32R)
        v_all = sb("v_all", [P, H, NT, D])
        v1 = sb("v1", [P, 2, NT, 2 * D], F32R)
        v2 = sb("v2", [P, 2, NT, D], F32R)
        q1 = sb("q1", [P, T], F32R)
        q2 = sb("q2", [P, T], F32R)
        k1 = sb("k1", [P, 2, T], F32R)
        k2 = sb("k2", [P, 2, T], F32R)
        probs = sb("probs", [P, 2, 2, CH])
        probs_h = sb("probs_h", [P, 4, 2, CH], F32R)
        probs_l = sb("probs_l", [P, 2, 2, CH], F32R)
        oh = sb("oh", [P, 2, CH], F32R)
        pos = sb("pos", [P, T])
        tq = sb("tq", [P, CH])
        tk = sb("tk", [P, CH])
        o_sum = sb("o_sum", [D, CH])
        l_both = sb("l_both", [P, CH])
        l_rows, l_cols = l_both[0:D, :], l_both[D:P, :]
        l_inv = sb("l_inv", [P, CH // 32])
        o_norm = sb("o_norm", [D, 2, CH])
        m_part = sb("m_part", [P, TPC, NC])
        m_max = sb("m_max", [P, 2, TPC])
        m_row = sb("m_row", [TPC, P], F32R)
        ident_b = sb("ident_b", [P, P], BF16)
        mask_kq = sb("mask_kq", [P, 2 * P], BF16)
        mask_qk = sb("mask_qk", [P, P], BF16)
        wvh, wvl = k1[:, 1, 0:CH], k1[:, 1, CH:2 * CH]
        x_tok = probs[:].rearrange("p b j q -> p (b j q)").rearrange("p (n e) -> p n e", e=E)
        wq_raw = acc[:, 0:12 * P].rearrange("p (n e) -> p n e", n=12)
        wo_raw = v_all[:, 0, :, :].rearrange("p t d -> p (t d)").rearrange("p (h r d) -> p h r d", h=H, r=2)

        scores = psum("scores", [P, 2, 2, CH])
        o_ps = psum("o_ps", [P, CH])
        max_ps = psum("max_ps", [P, 2, CH])
        side_ps = psum("side_ps", [P, CH])

        names = """ld_w ld_wo ld_x ld_pos c_ident c_masks c_v c_q2
            p_wt a_wt d_wt p_xt a_xt d_xt p_v a_v
            p_q p_k p_max p_turn p_out p_score p_pv
            a_exp a_expr a_k1 a_q1 a_q2 a_w a_wo a_vh a_oh
            g_pl g_vl
            d_q d_k d_ql d_kl d_max d_mx d_row d_lt d_o d_inv d_bc d_lr d_on d_oh d_acc
            s_m""".split()
        S = {n: sem(n) for n in names}
        block = ctx.enter_context(nc.Block())

        def units(p, cur, nxt):
            for n in (2 * p + LEAD, 2 * p + LEAD + 1):
                if n < NU and cur:
                    yield 0, n
                if n >= NU and nxt:
                    yield 1, n - NU

        def unit_place(u):
            c = chunk_of(UNIT0, u)
            r, j = divmod(u - UNIT0[c], c + 1)
            return c, r, j, (CH if j < c else P * (r + 1))

        def group(n, hi):
            if n < 3:
                if n == 2:
                    return wvh if hi else wvl
                return (wth if hi else wtl)[:, 4 * n:4 * (n + 1), :, :].rearrange("p h s d -> p (h s d)")
            if n < 5:
                return (woh if hi else wol)[:, 4 * (n - 3):4 * (n - 2), :].rearrange("p h e -> p (h e)")
            return (xh if hi else xl)[:, (n - 5) * CH:(n - 4) * CH]

        def high(n):
            return group(n, True)

        GROUPS = 3 + 2 + 4

        @block.sync
        def _(sp):
            w_rows = w_qkv.rearrange("(h s d) e -> s d h e", h=H, s=3)
            for s in range(2):
                sp.dma_start(wq_raw[s * D:(s + 1) * D, 0:H, :], w_rows[s]).then_inc(S["ld_w"], 16)
            v_rows = w_rows[2].rearrange("d (n r) e -> r d n e", r=2)
            for r in range(2):
                sp.dma_start(wq_raw[r * D:(r + 1) * D, H:H + H // 2, :], v_rows[r]).then_inc(S["ld_w"], 16)
            sp.dma_start(x_tok, x.rearrange("b (n p) e -> p (b n) e", p=P)).then_inc(S["ld_x"], 16)
            for r in range(2):
                sp.dma_start(wo_raw[:, :, r, :], w_o.rearrange("e (h d) -> e h d", d=D)).then_inc(S["ld_wo"], 16)
            sp.dma_start(pos[:], pe2).then_inc(S["ld_pos"], 16)

            def section(g, cur, nxt):
                for p in range(NP):
                    for c, ahead in due(TURN, p, 0, cur, nxt, False):
                        h = plus(g, ahead)
                        wait(sp, S["d_row"], at(h, NC, c + 1))
                        sp.dma_start(q2[D:D + 1, c * CH:(c + 1) * CH].bitcast(F32), m_row[:].bitcast(F32)).then_inc(S["s_m"], 16)

            section((0, -1), False, True)
            section((0, 0), True, True)
            with sp.Fori(0,(H - 2) // 2) as i:
                for o in (1, 2):
                    section((i, o), True, True)
            section((0, H - 1), True, False)

        @block.gpsimd
        def _(pool):
            pool.memset(ident[:], 0.0).then_inc(S["c_ident"], 1)
            pool.wait_ge(S["c_ident"], 1)
            pool.affine_select(out=ident[:], in_=ident[:], compare_op=ALU.not_equal, fill=1.0, base=0,
                               pattern=[[-1, P]], channel_multiplier=1).then_inc(S["c_ident"], 1)
            pool.memset(ident_b[:], 0.0).then_inc(S["c_masks"], 1)
            pool.memset(mask_kq[:], 0.0).then_inc(S["c_masks"], 1)
            pool.memset(mask_qk[:], 0.0).then_inc(S["c_masks"], 1)
            pool.wait_ge(S["c_masks"], 3)
            pool.affine_select(out=ident_b[:], in_=ident_b[:], compare_op=ALU.not_equal, fill=1.0, base=0,
                               pattern=[[-1, P]], channel_multiplier=1).then_inc(S["c_masks"], 1)
            pool.affine_select(out=mask_kq[:], in_=mask_kq[:], compare_op=ALU.is_ge, fill=NEG, base=-P,
                               pattern=[[1, 2 * P]], channel_multiplier=-1).then_inc(S["c_masks"], 1)
            pool.affine_select(out=mask_qk[:], in_=mask_qk[:], compare_op=ALU.is_ge, fill=NEG, base=0,
                               pattern=[[-1, P]], channel_multiplier=1).then_inc(S["c_masks"], 1)
            for b in range(2):
                pool.memset(v1[:, b, :, D:2 * D].bitcast(F32), 1.0).then_inc(S["c_v"], 1)

            def v_low(g):
                pool.wait_ge(S["a_vh"], at(g, 1, 1))
                b = g[1] % 2
                pool.tensor_tensor(v2[:, b, :, :], v_all[:, bass.ds(index(g), 1), :, :].rearrange("p h t d -> p (h t) d"),
                                   v1[:, b, :, 0:D], ALU.subtract).then_inc(S["g_vl"], 1)

            def section(g, cur, nxt):
                for p in range(NP):
                    if cur:
                        c = chunk_of(PAIR0, p)
                        lo = CH // 2 if p == PAIR0[c + 1] - 1 else 0
                        wait(pool, S["a_expr"], at(g, NP, p + 1))
                        wait(pool, S["p_pv"], at(g, NP, p - 1))
                        pool.tensor_tensor(probs_l[:, p % 2, :, lo:CH], probs[:, p % 2, :, lo:CH],
                                           probs_h[:, p % 4, :, lo:CH], ALU.subtract).then_inc(S["g_pl"], 1)
                    if p == 12 and nxt:
                        v_low(plus(g, 1))

            section((0, -1), False, True)
            section((0, 0), True, True)
            with pool.Fori(0,(H - 2) // 2) as i:
                for o in (1, 2):
                    section((i, o), True, True)
            section((0, H - 1), True, False)

        @block.scalar
        def _(act):
            for n in range(GROUPS):
                act.wait_ge(S["p_wt"], n + 1)
                act.activation(high(n), scores[:, n % 4 // 2, n % 2, :], ACT.Copy).then_inc(S["a_wt"], 1)

            def w_copy(g):
                wait(act, S["p_q"], at(g, NC, 0))
                for part, w in enumerate((wth, wtl)):
                    src = w[:, bass.ds(index(g), 1), :, :]
                    src = src.rearrange("p h s d -> p (h s) d").unsqueeze(2).to_broadcast([P, 2, 2, D])
                    act.activation(w_head[:, 2 * part:2 * part + 2, :].rearrange("p s (r d) -> p s r d", r=2),
                                   src, ACT.Copy).then_inc(S["a_w"], 1)

            def wo_copy(g):
                wait(act, S["p_out"], at(g, NC, -NC))
                for part, w in enumerate((woh, wol)):
                    act.activation(wo_head[:, g[1] % 2, part, :], w[:, bass.ds(index(g), 1), :].rearrange("p h e -> p (h e)"),
                                   ACT.Copy).then_inc(S["a_wo"], 1)

            def v_high(g):
                b = g[1] % 2
                wait(act, S["p_pv"], at(g, NP, -NP))
                act.activation(v1[:, b, :, 0:D], v_all[:, bass.ds(index(g), 1), :, :].rearrange("p h t d -> p (h t) d"),
                               ACT.Copy).then_inc(S["a_vh"], 1)

            def section(g, cur, nxt, prev):
                for p in range(NP):
                    if cur:
                        c = chunk_of(PAIR0, p)
                        lo = CH // 2 if p == PAIR0[c + 1] - 1 else 0
                        act.wait_ge(S["p_score"], at(g, NP, p + 1))
                        wait(act, S["g_pl"], at(g, NP, p - 1))
                        act.activation(probs[:, p % 2, :, lo:CH], scores[:, p % 2, :, lo:CH], ACT.Exp,
                                       scale=D ** -0.5).then_inc(S["a_exp"], 1)
                        wait(act, S["p_pv"], at(g, NP, p - 3))
                        act.activation(probs_h[:, p % 4, :, lo:CH], scores[:, p % 2, :, lo:CH], ACT.Exp,
                                       scale=D ** -0.5).then_inc(S["a_expr"], 1)
                    if p == 1 and nxt:
                        w_copy(plus(g, 1))
                    for c, ahead in due(PROJECT_K, p, 1, cur, nxt, prev):
                        h = plus(g, ahead)
                        act.wait_ge(S["d_k"], at(h, NC, c + 1))
                        act.activation(k1[:, h[1] % 2, c * CH:(c + 1) * CH], tk[:], ACT.Copy).then_inc(S["a_k1"], 1)
                    for c, ahead in due(PROJECT_Q, p, 1, cur, nxt, prev):
                        h = plus(g, ahead)
                        qs = slice(c * CH, (c + 1) * CH)
                        act.wait_ge(S["d_q"], at(h, NC, c + 1))
                        wait(act, S["p_score"], at(h, NP, PAIR0[c + 1] - NP))
                        act.activation(q1[:, qs], tq[:], ACT.Copy).then_inc(S["a_q1"], 1)
                        act.activation(q2[0:D, qs], tq[0:D, :], ACT.Copy).then_inc(S["a_q2"], 1)
                    if p == 9 and nxt:
                        wo_copy(plus(g, 1))
                    if p == 11 and nxt:
                        v_high(plus(g, 1))
                    for c, ahead in due(DONE, p, 2, cur, nxt, prev):
                        h = plus(g, ahead)
                        act.wait_ge(S["d_on"], at(h, NC, c + 1))
                        wait(act, S["p_out"], at(h, NC, c - 1))
                        act.activation(oh[0:D, c % 2, :], o_norm[:, c % 2, :], ACT.Copy).then_inc(S["a_oh"], 1)

            for n in range(NT):
                act.wait_ge(S["p_v"], n + 1)
                act.activation(v_all[:, :, n, :], scores[:, n % 4 // 2, n % 2, :].rearrange("p (h d) -> p h d", h=H),
                               ACT.Copy).then_inc(S["a_v"], 1)
            section((0, -1), False, True, False)
            section((0, 0), True, True, False)
            with act.Fori(0,(H - 2) // 2) as i:
                for o in (1, 2):
                    section((i, o), True, True, True)
            section((0, H - 1), True, False, True)
            section((0, H), False, False, True)

        @block.vector
        def _(dve):
            dve.memset(q2[D:P, :].bitcast(F32), 0.0).then_inc(S["c_q2"], 1)
            dve.memset(k2[D:P, :, :].bitcast(F32), 0.0).then_inc(S["c_q2"], 1)
            dve.wait_ge(S["c_q2"], 2)
            dve.memset(k2[D:D + 1, :, :].bitcast(F32), 1.0).then_inc(S["c_q2"], 1)
            for n in range(GROUPS):
                dve.wait_ge(S["a_wt"], n + 1)
                dve.tensor_tensor(group(n, False), scores[:, n % 4 // 2, n % 2, :], high(n), ALU.subtract).then_inc(S["d_wt"], 1)
            dve.memset(acc[:], 0.0).then_inc(S["c_q2"], 1)

            def section(g, cur, nxt, prev):
                for p in range(NP):
                    for c, ahead in due(OUTPUT, p, 0, cur, nxt, prev):
                        h = plus(g, ahead)
                        qs = slice(c * CH, (c + 1) * CH)
                        wait(dve, S["d_acc"], at(h, NC, c - NC + 1))
                        dve.wait_ge(S["p_out"], at(h, NC, c + 1))
                        dve.tensor_tensor(acc[:, qs], acc[:, qs], side_ps[:], ALU.add).then_inc(S["d_acc"], 1)
                    for c, ahead in due(TURN, p, 0, cur, nxt, prev):
                        h = plus(g, ahead)
                        wait(dve, S["p_score"], at(h, NP, PAIR0[c + 1] - NP))
                        wait(dve, S["s_m"], at(h, 16 * NC, 16 * c))
                        dve.wait_ge(S["p_turn"], at(h, NC, c + 1))
                        dve.tensor_scalar(m_row[:], side_ps[0:TPC, 0:P], -1.0, None, ALU.mult).then_inc(S["d_row"], 1)
                    for c, ahead in due(PROJECT_Q, p, 0, cur, nxt, prev):
                        h = plus(g, ahead)
                        wait(dve, S["d_ql"], at(h, NC, c))
                        dve.wait_ge(S["p_q"], at(h, NC, c + 1))
                        dve.tensor_tensor(tq[:], side_ps[:], pos[:, c * CH:(c + 1) * CH], ALU.add).then_inc(S["d_q"], 1)
                    for c, ahead in due(PROJECT_K, p, 0, cur, nxt, prev):
                        h = plus(g, ahead)
                        wait(dve, S["d_kl"], at(h, NC, c))
                        dve.wait_ge(S["p_k"], at(h, NC, c + 1))
                        dve.tensor_tensor(tk[:], side_ps[:], pos[:, c * CH:(c + 1) * CH], ALU.add).then_inc(S["d_k"], 1)
                    for c, ahead in due(DONE, p, 0, cur, nxt, prev):
                        h = plus(g, ahead)
                        wait(dve, S["d_lr"], at(h, NC, c))
                        wait(dve, S["d_on"], at(h, NC, c))
                        dve.wait_ge(S["p_pv"], at(h, NP, PAIR0[c + 1]))
                        dve.transpose(l_cols, o_ps[D:P, :]).then_inc(S["d_lt"], 1)
                        dve.tensor_copy(o_sum[:], o_ps[0:D, :]).then_inc(S["d_o"], 1)
                    for ahead, u in units(p, cur, nxt):
                        h = plus(g, ahead)
                        c, r, j, width = unit_place(u)
                        if u == UNIT0[c]:
                            wait(dve, S["d_mx"], at(h, NC, c))
                        dve.wait_ge(S["p_max"], at(h, NU, u + 1))
                        dve.tensor_reduce(m_part[:, r, j:j + 1], max_ps[:, u % 2, 0:width], AX.X, ALU.max).then_inc(S["d_max"], 1)
                        if u + 1 == UNIT0[c + 1]:
                            dve.wait_ge(S["d_max"], at(h, NU, u + 1))
                            wait(dve, S["p_turn"], at(h, NC, c - 1))
                            dve.tensor_reduce(m_max[:, c % 2, :], m_part[:, :, 0:c + 1], AX.X, ALU.max).then_inc(S["d_mx"], 1)
                    for c, ahead in due(PROJECT_Q, p, 2, cur, nxt, prev):
                        h = plus(g, ahead)
                        qs = slice(c * CH, (c + 1) * CH)
                        dve.wait_ge(S["a_q2"], at(h, NC, c + 1))
                        dve.tensor_tensor(q1[D:P, qs], tq[D:P, :], q1[D:P, qs], ALU.subtract).then_inc(S["d_ql"], 1)
                    for c, ahead in due(PROJECT_K, p, 2, cur, nxt, prev):
                        h = plus(g, ahead)
                        b, ks = h[1] % 2, slice(c * CH, (c + 1) * CH)
                        dve.wait_ge(S["a_k1"], at(h, NC, c + 1))
                        dve.tensor_tensor(k2[0:D, b, ks], tk[0:D, :], k1[0:D, b, ks], ALU.subtract).then_inc(S["d_kl"], 1)
                    for c, ahead in due(DONE, p, 0, cur, nxt, prev):
                        h = plus(g, ahead)
                        dve.wait_ge(S["d_lt"], at(h, NC, c + 1))
                        dve.reciprocal(l_inv[D:P, :], l_cols.rearrange("p (b j) -> p b j", j=32)[:, :, 0]).then_inc(S["d_inv"], 1)
                        dve.wait_ge(S["d_inv"], at(h, NC, c + 1))
                        dve.tensor_copy(l_cols.rearrange("p (b j) -> p b j", j=32),
                                        l_inv[D:P, :].unsqueeze(2).to_broadcast([D, CH // 32, 32])).then_inc(S["d_bc"], 1)
                        dve.wait_ge(S["d_bc"], at(h, NC, c + 1))
                        wait(dve, S["d_on"], at(h, NC, c))
                        dve.transpose(l_rows, l_cols).then_inc(S["d_lr"], 1)
                    for c, ahead in due(DONE, p, 1, cur, nxt, prev):
                        h = plus(g, ahead)
                        dve.wait_ge(S["d_lr"], at(h, NC, c + 1))
                        wait(dve, S["d_oh"], at(h, NC, c - 1))
                        dve.tensor_tensor(o_norm[:, c % 2, :], o_sum[:], l_rows, ALU.mult).then_inc(S["d_on"], 1)
                    for c, ahead in due(DONE, p, 3, cur, nxt, prev):
                        h = plus(g, ahead)
                        dve.wait_ge(S["a_oh"], at(h, NC, c + 1))
                        dve.tensor_tensor(oh[D:P, c % 2, :], o_norm[:, c % 2, :], oh[0:D, c % 2, :], ALU.subtract).then_inc(S["d_oh"], 1)

            dve.wait_ge(S["ld_pos"], 16)
            section((0, -1), False, True, False)
            section((0, 0), True, True, False)
            with dve.Fori(0,(H - 2) // 2) as i:
                for o in (1, 2):
                    section((i, o), True, True, True)
            section((0, H - 1), True, False, True)
            section((0, H), False, False, True)

        @block.tensor
        def _(pe):
            pe.wait_ge(S["c_ident"], 2)
            for n in range(GROUPS):
                if n >= 4:
                    pe.wait_ge(S["d_wt"], n - 3)
                if n == 0:
                    pe.wait_ge(S["ld_w"], 64)
                if n == 3:
                    pe.wait_ge(S["ld_wo"], 32)
                if n == 5:
                    pe.wait_ge(S["ld_x"], 16)
                for j in range(4):
                    if n < 3:
                        src = wq_raw[:, 4 * n + j, :]
                    elif n < 5:
                        src = wo_raw[:, 4 * (n - 3) + j, :, :].rearrange("p r d -> p (r d)")
                    else:
                        src = x_tok[:, 4 * (n - 5) + j, :]
                    last = pe.transpose(scores[:, n % 4 // 2, n % 2, j * P:(j + 1) * P], src, ident[:])
                last.then_inc(S["p_wt"], 1)
            for n in range(NT):
                pe.wait_ge(S["d_wt"], GROUPS if n == 0 else GROUPS)
                if n >= 4:
                    pe.wait_ge(S["a_v"], n - 3)
                ts = slice(n * P, (n + 1) * P)
                for k, (a, w) in enumerate(((xh, wvh), (xh, wvl), (xl, wvh))):
                    last = pe.matmul(scores[:, n % 4 // 2, n % 2, :], a[:, ts], w, start=(k == 0), stop=(k == 2))
                last.then_inc(S["p_v"], 1)

            def project(h, c, which):
                xs = slice(c * CH, (c + 1) * CH)
                for k, (w, a) in enumerate(((0, xh), (0, xl), (2, xh))):
                    last = pe.matmul(side_ps[:], w_head[:, w + which, :], a[:, xs], start=(k == 0), stop=(k == 2))
                last.then_inc(S["p_k" if which else "p_q"], 1)

            def maximum(h, u):
                c, r, j, width = unit_place(u)
                b = h[1] % 2
                if u == UNIT0[c]:
                    pe.wait_ge(S["d_ql"], at(h, NC, c + 1))
                    pe.wait_ge(S["a_k1"], at(h, NC, c + 1))
                wait(pe, S["d_max"], at(h, NU, u - 1))
                n = max(width, 2 * P)
                ks = slice(j * CH, j * CH + n)
                tile = (c * TPC + r) * P
                last = pe.matmul(max_ps[:, u % 2, 0:n], q1[:, tile:tile + P], k1[:, b, ks], start=True, stop=(j < c))
                if j == c:
                    last = pe.matmul(max_ps[:, u % 2, width - P:width], ident_b[:], mask_qk[:], start=False, stop=True)
                last.then_inc(S["p_max"], 1)

            def turn(h, c):
                pe.wait_ge(S["d_mx"], at(h, NC, c + 1))
                pe.transpose(side_ps[0:TPC, 0:P], m_max[:, c % 2, :], ident[:]).then_inc(S["p_turn"], 1)

            def output(h, c):
                pe.wait_ge(S["d_oh"], at(h, NC, c + 1))
                if c == 0:
                    pe.wait_ge(S["a_wo"], at(h, 2, 2))
                for part in range(2):
                    last = pe.matmul(side_ps[:], wo_head[:, h[1] % 2, part, :], oh[:, c % 2, :], start=(part == 0), stop=(part == 1))
                last.then_inc(S["p_out"], 1)

            def score_pair(h, p):
                c = chunk_of(PAIR0, p)
                b = h[1] % 2
                if p == PAIR0[c]:
                    pe.wait_ge(S["s_m"], at(h, 16 * NC, 16 * (c + 1)))
                    pe.wait_ge(S["d_kl"], at(h, NC, c + 1))
                wait(pe, S["a_expr"], at(h, NP, p - 1))
                for j in range(2):
                    kb = 2 * (p - PAIR0[c]) + j
                    diag = kb - TPC * c
                    lo = CH // 2 if diag >= 2 else 0
                    ks = slice(kb * P, (kb + 1) * P)
                    qs = slice(c * CH + lo, (c + 1) * CH)
                    into = scores[:, p % 2, j, lo:CH]
                    pe.matmul(into, k1[:, b, ks], q1[:, qs], start=True, stop=False)
                    last = pe.matmul(into, k2[:, b, ks], q2[:, qs], start=False, stop=(diag < 0))
                    if diag >= 0:
                        m0 = 0 if diag == 3 else P
                        last = pe.matmul(scores[:, p % 2, j, (diag + 1) * P - (2 * P - m0):(diag + 1) * P], ident_b[:],
                                         mask_kq[:, m0:2 * P], start=False, stop=True)
                last.then_inc(S["p_score"], 1)

            def pv_pair(h, p):
                c = chunk_of(PAIR0, p)
                b = h[1] % 2
                pe.wait_ge(S["g_pl"], at(h, NP, p + 1))
                if p == PAIR0[c]:
                    wait(pe, S["d_o"], at(h, NC, c))
                if p == 0:
                    pe.wait_ge(S["g_vl"], at(h, 1, 1))
                for j in range(2):
                    kb = 2 * (p - PAIR0[c]) + j
                    diag = kb - TPC * c
                    lo = P * min(diag, 2) if diag > 0 else 0
                    hi_v = v1[:, b, kb, :]
                    lo_v = v2[:, b, kb, :]
                    for k, (v, rows, pr) in enumerate(((hi_v, P, probs_h[:, p % 4, j, lo:CH]),
                                                       (lo_v, D, probs_h[:, p % 4, j, lo:CH]),
                                                       (hi_v, P, probs_l[:, p % 2, j, lo:CH]))):
                        last = pe.matmul(o_ps[0:rows, lo:CH], v, pr, start=(p == PAIR0[c] and j == 0 and k == 0),
                                         stop=(p == PAIR0[c + 1] - 1 and j == 1 and k == 2))
                last.then_inc(S["p_pv"], 1)

            def section(g, cur, nxt, prev):
                before = [("d_q", at(g, NC, NC))] if cur else []

                def side_bank(evacuated, value):
                    if before:
                        wait(pe, S[before[0][0]], before[0][1])
                    before[:] = [(evacuated, value)]

                for p in range(NP):
                    if cur:
                        score_pair(g, p)
                    for ahead, u in units(p, cur, nxt):
                        maximum(plus(g, ahead), u)
                    for c, ahead in due(OUTPUT, p, 0, cur, nxt, prev):
                        side_bank("d_acc", at(plus(g, ahead), NC, c + 1))
                        output(plus(g, ahead), c)
                    for c, ahead in due(TURN, p, 0, cur, nxt, prev):
                        side_bank("d_row", at(plus(g, ahead), NC, c + 1))
                        turn(plus(g, ahead), c)
                    for c, ahead in due(PROJECT_Q, p, 0, cur, nxt, prev):
                        if c == 0:
                            pe.wait_ge(S["a_w"], at(plus(g, ahead), 2, 2))
                        side_bank("d_q", at(plus(g, ahead), NC, c + 1))
                        project(plus(g, ahead), c, 0)
                    for c, ahead in due(PROJECT_K, p, 0, cur, nxt, prev):
                        side_bank("d_k", at(plus(g, ahead), NC, c + 1))
                        project(plus(g, ahead), c, 1)
                    if p >= 2 and cur:
                        pv_pair(g, p - 2)
                    if p < 2 and prev:
                        pv_pair(plus(g, -1), NP - 2 + p)

            pe.wait_ge(S["c_masks"], 6)
            pe.wait_ge(S["c_v"], 2)
            pe.wait_ge(S["c_q2"], 4)
            section((0, -1), False, True, False)
            section((0, 0), True, True, False)
            with pe.Fori(0,(H - 2) // 2) as i:
                for o in (1, 2):
                    section((i, o), True, True, True)
            section((0, H - 1), True, False, True)
            section((0, H), False, False, True)


def layer_norm(dve, sem, base, src, dst, buf):
    cen, sq, s = buf
    total, var, half, guess, t, bits = (s[:, i, :] for i in range(6))

    def spread(a):
        return a.unsqueeze(2).to_broadcast([P, TPC, E])

    if not isinstance(base, int) or base > 0:
        dve.wait_ge(sem, base)
    dve.tensor_reduce(total, src, AX.X, ALU.add).then_inc(sem, 1)
    yield
    dve.wait_ge(sem, base + 1)
    dve.scalar_tensor_tensor(cen, spread(total), -1.0 / E, src, ALU.mult, ALU.add).then_inc(sem, 1)
    yield
    dve.wait_ge(sem, base + 2)
    dve.tensor_tensor(sq, cen, cen, ALU.mult).then_inc(sem, 1)
    yield
    dve.wait_ge(sem, base + 3)
    dve.tensor_reduce(total, sq, AX.X, ALU.add).then_inc(sem, 1)
    yield
    dve.wait_ge(sem, base + 4)
    dve.tensor_scalar(var, total, 1.0 / E, EPS, ALU.mult, ALU.add).then_inc(sem, 1)
    yield
    dve.wait_ge(sem, base + 5)
    dve.tensor_scalar(bits.bitcast(I32), var.bitcast(I32), 1, None, ALU.logical_shift_right).then_inc(sem, 1)
    yield
    dve.wait_ge(sem, base + 6)
    dve.tensor_scalar(guess.bitcast(I32), bits.bitcast(I32), -1, 0x5F3759DF, ALU.mult, ALU.add).then_inc(sem, 1)
    yield
    for k in range(3):
        dve.wait_ge(sem, base + 7 + 3 * k)
        dve.tensor_tensor(t, guess, guess, ALU.mult).then_inc(sem, 1)
        yield
        dve.wait_ge(sem, base + 8 + 3 * k)
        dve.scalar_tensor_tensor(half, var, -0.5, t, ALU.mult, ALU.mult).then_inc(sem, 1)
        yield
        dve.wait_ge(sem, base + 9 + 3 * k)
        dve.scalar_tensor_tensor(guess, half, 1.5, guess, ALU.add, ALU.mult).then_inc(sem, 1)
        yield
    dve.wait_ge(sem, base + 16)
    dve.tensor_tensor(dst, cen, spread(guess), ALU.mult).then_inc(sem, 1)
    yield


def feed_forward(nc, acc, ident, x, ln_g, ln_b, aw1, ab1, aw2, ab2, gate_w, gate_b, ew1, eb1, ew2, eb2, gens, gc_w, gc_b, out):
    with ExitStack() as ctx:
        def sb(name, shape, dt=F32):
            return ctx.enter_context(nc.sbuf_tensor(name, shape, dt))

        def sem(name):
            return ctx.enter_context(nc.semaphore(name))

        w_raw = sb("w_raw", [P, W_COLS])
        w_hi = sb("w_hi", [P, W_COLS], F32R)
        w_lo = sb("w_lo", [P, W_COLS], F32R)
        x_in = sb("x_in", [P, NT, E])
        y1 = sb("y1", [P, NT, E])
        u = sb("u", [P, TPC, E])
        n2 = sb("n2", [P, 2, TPC, E])
        ln_buf = (sb("ln_cen", [P, TPC, E])[:], sb("ln_sq", [P, TPC, E])[:], sb("ln_small", [P, 6, TPC]))
        xn = sb("xn", [P, T])
        xn_hi = sb("xn_hi", [P, T], F32R)
        xn_lo = sb("xn_lo", [P, T], F32R)
        gens_sb = sb("gens_sb", [P, NROT, P])
        gens_t = sb("gens_t", [P, NROT, P])
        e_pow = sb("e_pow", [P, 2, NROT, P])
        e_sum = sb("e_sum", [P, NROT, P])
        e_turn = sb("e_turn", [P, NROT, P])
        rot = sb("rot", [P, 2, P])
        rot_hi = sb("rot_hi", [P, P], F32R)
        rot_lo = sb("rot_lo", [P, P], F32R)
        gw = sb("gw", [P, NX])
        gb = sb("gb", [P, NX])
        vec_rows = sb("vec_rows", [N_VEC, P])
        vec_cols = sb("vec_cols", [P, N_VEC])
        g_col, b_col, ab2_col, gc_col = (vec_cols[:, a:b] for a, b in ((0, 1), (1, 2), (2, 3), (3, 5)))
        ab1_col, eb1_col = vec_cols[:, 5:5 + NA], vec_cols[:, 5 + NA:N_VEC]
        eb2_rows = sb("eb2_rows", [P, E])
        eb2_hi = sb("eb2_hi", [P, E], F32R)
        eb2_lo = sb("eb2_lo", [P, E], F32R)
        gc_wide = sb("gc_wide", [P, 2, P])
        gcb = sb("gcb", [P, 1])
        gcb_half = sb("gcb_half", [P, 1])
        pick = sb("pick", [P, NX, P], F32R)
        logits = sb("logits", [P, NT, NX])
        before = sb("before", [P, NX, NX])
        gt = sb("gt", [P, NT, NX, NX])
        eq = sb("eq", [P, NT, NX, NX])
        rank = sb("rank", [P, NT, NX])
        first = sb("first", [P, NT, NX])
        second = sb("second", [P, NT, NX])
        diff_m = sb("diff_m", [P, NT, NX])
        gap = sb("gap", [P, NT])
        gap_t = sb("gap_t", [P, NT])
        mix_w = sb("mix_w", [P, NT, NX])
        w_pad = sb("w_pad", [P, NT, 64])
        wt = sb("wt", [P, T], F32R)
        hid = sb("hid", [P, RING, CH])
        hid_hi = sb("hid_hi", [P, RING, CH], F32R)
        hid_lo = sb("hid_lo", [P, RING, CH], F32R)
        abel = sb("abel", [P, CH])
        moe_hi = sb("moe_hi", [P, CH], F32R)
        moe_lo = sb("moe_lo", [P, CH], F32R)
        nonabel = sb("nonabel", [P, CH])
        gate = sb("gate", [P, CH])
        delta = sb("delta", [P, CH])
        mixed = sb("mixed", [P, CH])
        last_sum = sb("last_sum", [P, TPC, E])
        y2 = sb("y2", [P, NT, E])

        ps = ctx.enter_context(nc.psum_tensor("ps_ffn", [P, 8, CH], F32))

        names = """l_gens l_x l_small l_wa l_we1 l_we2 c_k c_pick c_bef f_vec a_vec
            f_u f_gt f_tay f_sq f_sqt f_n f_log f_wt f_r
            f_h f_wb f_y f_ym f_ya f_rot f_gate f_out
            a_gt a_tay a_sq a_wh a_x a_wth a_r a_rh a_tanh a_eb
            a_g a_hh a_ab a_mh a_no a_th
            d_u d_ln d_sqt d_xl d_log d_top d_wl d_rl d_gc d_m
            d_hw d_ml d_mix d_v d_ln3 d_pad
            g_wl g_sum g_hl
            s_y""".split()
        S = {n: sem("ffn_" + n) for n in names}
        block = ctx.enter_context(nc.Block())

        N_SMALL = 11

        @block.sync
        def _(sp):
            sp.dma_start(gens_sb[:], gens.rearrange("r i j -> i r j")).then_inc(S["l_gens"], 16)
            sp.dma_start(x_in[:], x.rearrange("b (n p) e -> p (b n) e", p=P)).then_inc(S["l_x"], 16)
            def row(a, n=1):
                return vec_rows[a:a + n, :]

            small = [(gw[:], gate_w), (gb[:], gate_b.partition_broadcast(P)), (gcb[:], gc_b.partition_broadcast(P)),
                     (row(0), ln_g.rearrange("(o d) -> o d", o=1)), (row(1), ln_b.rearrange("(o d) -> o d", o=1)),
                     (row(2), ab2.rearrange("(o d) -> o d", o=1)), (row(3, 2), gc_w.rearrange("(o d) u -> o (d u)", o=2)),
                     (row(5, NA), ab1.rearrange("(m p) -> m p", p=P)),
                     (row(5 + NA, NX * NXB), eb1.rearrange("e (k p) -> (e k) p", p=P))]
            for dst, src in small:
                sp.dma_start(dst, src).then_inc(S["l_small"], 16)
            sp.wait_ge(S["c_k"], 1)
            for row in (0, 32):
                sp.dma_start(eb2_rows[row:row + NX, :], eb2).then_inc(S["l_small"], 16)
            A = NA * P
            sp.dma_start(w_raw[:, 0:A], aw1).then_inc(S["l_wa"], 16)
            sp.dma_start(w_raw[:, A:2 * A].rearrange("p (m d) -> p m d", m=NA), aw2.rearrange("(m p) d -> p m d", p=P)).then_inc(S["l_wa"], 16)
            X = NX * NXB * P
            sp.dma_start(w_raw[:, 2 * A:2 * A + X].rearrange("p (e h) -> p e h", e=NX), ew1.rearrange("e d h -> d e h")).then_inc(S["l_we1"], 16)
            sp.dma_start(w_raw[:, 2 * A + X:].rearrange("p (e k d) -> p e k d", e=NX, k=NXB),
                         ew2.rearrange("e (k p) d -> p e k d", p=P)).then_inc(S["l_we2"], 16)
            o_v = out.rearrange("b (n p) e -> p (b n) e", p=P)
            for c in range(NC):
                sp.wait_ge(S["d_ln3"], LN_STEPS * (c + 1))
                sp.dma_start(o_v[:, TPC * c:TPC * (c + 1), :], y2[:, TPC * c:TPC * (c + 1), :]).then_inc(S["s_y"], 16)
            sp.wait_ge(S["s_y"], 16 * NC)

        PART = W_COLS // W_PARTS

        def weights_loaded(eng, part):
            if part == 0:
                eng.wait_ge(S["l_wa"], 32)
            if part == 1:
                eng.wait_ge(S["l_we1"], 16)
            if part >= 2:
                eng.wait_ge(S["l_we1"], 16)
                eng.wait_ge(S["l_we2"], 16)

        @block.gpsimd
        def _(pool):
            pool.tensor_tensor(pick[:], ident[:, 0:NX].unsqueeze(2).to_broadcast([P, NX, P]),
                               ident[:, 32:32 + NX].unsqueeze(2).to_broadcast([P, NX, P]), ALU.add).then_inc(S["c_pick"], 1)
            pool.memset(before[:], 1.0).then_inc(S["c_bef"], 1)
            pool.wait_ge(S["c_bef"], 1)
            pool.affine_select(out=before[:], in_=before[:], compare_op=ALU.is_gt, fill=0.0, base=0,
                               pattern=[[1, NX], [-1, NX]], channel_multiplier=0).then_inc(S["c_bef"], 1)
            for j in range(2, TAYLOR + 1):
                pool.wait_ge(S["a_tay"], j)
                if j > 2:
                    pool.wait_ge(S["g_sum"], j - 2)
                src = e_pow[:, 1, :, :] if j == 2 else e_sum[:]
                pool.tensor_tensor(e_sum[:], src, e_pow[:, j % 2, :, :], ALU.add).then_inc(S["g_sum"], 1)
            for part in range(W_PARTS):
                cols = slice(part * PART, (part + 1) * PART)
                pool.wait_ge(S["a_wh"], part + 1)
                pool.tensor_tensor(w_lo[:, cols], w_raw[:, cols], w_hi[:, cols], ALU.subtract).then_inc(S["g_wl"], 1)

            def section(c):
                for j in range(NB):
                    pool.wait_ge(S["a_hh"], c * NB + (j + 1))
                    wait(pool, S["f_y"], c * NB + (j - RING + 1))
                    r = j % RING
                    pool.tensor_tensor(hid_lo[:, r, :], hid[:, r, :], hid_hi[:, r, :], ALU.subtract).then_inc(S["g_hl"], 1)

            section(0)
            with pool.Fori(1, NC) as c:
                section(c)

        @block.scalar
        def _(act):
            act.wait_ge(S["f_vec"], 1)
            act.activation(vec_cols[:], ps[:, 6, 0:N_VEC], ACT.Copy).then_inc(S["a_vec"], 1)
            act.wait_ge(S["l_gens"], 16)
            act.activation(e_pow[:, 1, :, :], gens_sb[:], ACT.Copy, scale=2.0 ** -HALVINGS).then_inc(S["a_tay"], 1)
            act.wait_ge(S["f_gt"], 1)
            act.activation(gens_t[:], ps[:, 4, :], ACT.Copy, scale=2.0 ** -HALVINGS).then_inc(S["a_gt"], 1)
            for j in range(2, TAYLOR + 1):
                act.wait_ge(S["f_tay"], j - 1)
                if j > 2:
                    act.wait_ge(S["g_sum"], max(1, j - 3))
                act.activation(e_pow[:, j % 2, :, :], ps[:, 4, :], ACT.Copy, scale=1.0 / j).then_inc(S["a_tay"], 1)

            def squaring(k):
                act.wait_ge(S["f_sq"], k + 1)
                act.activation(e_sum[:], ps[:, 4, :], ACT.Copy).then_inc(S["a_sq"], 1)

            def weight_high(part):
                cols = slice(part * PART, (part + 1) * PART)
                weights_loaded(act, part)
                act.activation(w_hi[:, cols], w_raw[:, cols], ACT.Copy).then_inc(S["a_wh"], 1)

            for c in range(NC):
                for k in range(2 * c, 2 * c + 2):
                    squaring(k)
                weight_high(c)
                cs = slice(c * CH, (c + 1) * CH)
                act.wait_ge(S["f_n"], c + 1)
                act.activation(xn[:, cs], ps[:, c, :], ACT.Identity, scale=g_col, bias=b_col).then_inc(S["a_x"], 1)
                act.activation(xn_hi[:, cs], ps[:, c, :], ACT.Identity, scale=g_col, bias=b_col).then_inc(S["a_x"], 1)
            for k in range(3):
                act.wait_ge(S["f_r"], k + 1)
                if k < 2:
                    act.activation(rot[:, k, :], ps[:, 5, 0:P], ACT.Copy).then_inc(S["a_r"], 1)
            act.activation(rot_hi[:], ps[:, 5, 0:P], ACT.Copy).then_inc(S["a_rh"], 1)
            act.wait_ge(S["l_small"], 16 * N_SMALL)
            act.activation(eb2_hi[:], eb2_rows[:], ACT.Copy).then_inc(S["a_eb"], 1)
            act.wait_ge(S["d_top"], 9)
            act.activation(gap_t[:], gap[:], ACT.Tanh, scale=0.5).then_inc(S["a_tanh"], 1)
            for c in range(NC):
                act.wait_ge(S["f_wt"], c + 1)
                act.activation(wt[0:64, c * CH:(c + 1) * CH], ps[0:64, c, :], ACT.Copy).then_inc(S["a_wth"], 1)
            def high(c, j):
                r = j % RING
                wait(act, S["f_y"], c * NB + (j - RING + 1))
                if j < NA:
                    act.activation(hid_hi[:, r, :], ps[:, j % 2, :], ACT.Gelu, bias=ab1_col[:, j:j + 1]).then_inc(S["a_hh"], 1)
                else:
                    act.wait_ge(S["d_hw"], c * (NB - NA) + (j - NA + 1))
                    act.activation(hid_hi[:, r, :], hid[:, r, :], ACT.Copy).then_inc(S["a_hh"], 1)

            def section(c, cur, prev):
                for j in range(NB):
                    if cur:
                        bias = ab1_col[:, j:j + 1] if j < NA else eb1_col[:, j - NA:j - NA + 1]
                        act.wait_ge(S["f_h"], c * NB + (j + 1))
                        wait(act, S["g_hl"], c * NB + (j - RING + 1))
                        act.activation(hid[:, j % RING, :], ps[:, j % 2, :], ACT.Gelu, bias=bias).then_inc(S["a_g"], 1)
                        if j < NA:
                            high(c, j)
                        elif j > NA:
                            high(c, j - 1)
                    if prev and j == T_ABEL:
                        act.wait_ge(S["f_y"], (c - 1) * NB + NA)
                        wait(act, S["d_mix"], (c - 1) * 3)
                        act.activation(abel[:], ps[:, 4, :], ACT.Identity, bias=ab2_col).then_inc(S["a_ab"], 1)
                    if prev and j == T_SPLIT:
                        act.wait_ge(S["f_ym"], c)
                        wait(act, S["f_rot"], c - 1)
                        act.activation(moe_hi[:], ps[:, 5, :], ACT.Copy).then_inc(S["a_mh"], 1)
                    if prev and j == T_NONABEL:
                        act.wait_ge(S["f_rot"], c)
                        wait(act, S["f_gate"], c - 1)
                        wait(act, S["d_mix"], (c - 1) * 3)
                        act.activation(nonabel[:], ps[:, 6, :], ACT.Copy).then_inc(S["a_no"], 1)
                    if prev and j == T_TANH:
                        act.wait_ge(S["f_gate"], c)
                        wait(act, S["d_mix"], (c - 1) * 3)
                        act.activation(gate[:], ps[:, 7, :], ACT.Tanh, scale=0.5, bias=gcb_half[:]).then_inc(S["a_th"], 1)
                if cur:
                    high(c, NB - 1)

            act.wait_ge(S["d_gc"], 2)
            section(0, True, False)
            section(1, True, True)
            with act.Fori(2, NC) as c:
                section(c, True, True)
            section(NC, False, True)

        @block.vector
        def _(dve):
            dve.memset(eb2_rows[:], 0.0).then_inc(S["c_k"], 1)
            dve.memset(w_pad[:], 0.0).then_inc(S["d_pad"], 1)
            dve.memset(wt[64:P, :].bitcast(F32), 0.0).then_inc(S["d_pad"], 1)
            dve.wait_ge(S["l_small"], 16 * N_SMALL)
            dve.tensor_scalar(gcb_half[:], gcb[:], 0.5, None, ALU.mult).then_inc(S["d_gc"], 1)
            dve.wait_ge(S["a_vec"], 1)
            dve.tensor_copy(gc_wide[:], gc_col.unsqueeze(2).to_broadcast([P, 2, P])).then_inc(S["d_gc"], 1)
            dve.wait_ge(S["l_x"], 16)

            def turned(k):
                dve.wait_ge(S["f_sqt"], k + 1)
                dve.scalar_tensor_tensor(e_turn[:], ident[:].unsqueeze(1).to_broadcast([P, NROT, P]), 2.0,
                                         ps[:, 5, :].rearrange("p (r j) -> p r j", r=NROT), ALU.mult, ALU.add).then_inc(S["d_sqt"], 1)

            for c in range(NC):
                ts = slice(TPC * c, TPC * (c + 1))
                dve.wait_ge(S["f_u"], c + 1)
                wait(dve, S["d_ln"], 2 * LN_STEPS * c)
                dve.tensor_tensor(u[:], ps[:, c, :].rearrange("p (t e) -> p t e", e=E), x_in[:, ts, :], ALU.add).then_inc(S["d_u"], 1)
                dve.wait_ge(S["d_u"], c + 1)
                for _ in layer_norm(dve, S["d_ln"], 2 * LN_STEPS * c, u[:], y1[:, ts, :], ln_buf):
                    pass
                turned(2 * c)
                wait(dve, S["f_n"], c - 1)
                for _ in layer_norm(dve, S["d_ln"], 2 * LN_STEPS * c + LN_STEPS, y1[:, ts, :], n2[:, c % 2, :, :], ln_buf):
                    pass
                turned(2 * c + 1)
                if c > 0:
                    low = slice((c - 1) * CH, c * CH)
                    dve.wait_ge(S["a_x"], 2 * c)
                    dve.tensor_tensor(xn_lo[:, low], xn[:, low], xn_hi[:, low], ALU.subtract).then_inc(S["d_xl"], 1)
            dve.wait_ge(S["a_x"], 2 * NC)
            low = slice((NC - 1) * CH, NC * CH)
            dve.tensor_tensor(xn_lo[:, low], xn[:, low], xn_hi[:, low], ALU.subtract).then_inc(S["d_xl"], 1)

            dve.wait_ge(S["a_sq"], HALVINGS)
            dve.tensor_tensor(e_pow[:, 0, 0, :], e_sum[:, NROT - 1, :], ident[:], ALU.add).then_inc(S["d_m"], 1)
            dve.wait_ge(S["f_sqt"], HALVINGS + 1)
            dve.tensor_tensor(e_turn[:], ps[:, 5, :].rearrange("p (r j) -> p r j", r=NROT),
                              ident[:].unsqueeze(1).to_broadcast([P, NROT, P]), ALU.add).then_inc(S["d_m"], 1)
            dve.wait_ge(S["f_log"], NC)
            dve.wait_ge(S["c_bef"], 2)
            dve.tensor_tensor(logits[:], ps[:, 6, 0:NT * NX].rearrange("p (t e) -> p t e", e=NX),
                              gb[:].unsqueeze(1).to_broadcast([P, NT, NX]), ALU.add).then_inc(S["d_log"], 1)
            dve.wait_ge(S["d_log"], 1)
            full = [P, NT, NX, NX]
            other, own = logits[:].unsqueeze(2).to_broadcast(full), logits[:].unsqueeze(3).to_broadcast(full)
            dve.tensor_tensor(gt[:], other, own, ALU.is_gt).then_inc(S["d_top"], 1)
            dve.tensor_tensor(eq[:], other, own, ALU.is_equal).then_inc(S["d_top"], 1)
            dve.wait_ge(S["d_top"], 2)
            dve.tensor_tensor(eq[:], eq[:], before[:].unsqueeze(1).to_broadcast(full), ALU.mult).then_inc(S["d_top"], 1)
            dve.wait_ge(S["d_top"], 3)
            dve.tensor_tensor(gt[:], gt[:], eq[:], ALU.add).then_inc(S["d_top"], 1)
            dve.wait_ge(S["d_top"], 4)
            dve.tensor_reduce(rank[:], gt[:], AX.X, ALU.add).then_inc(S["d_top"], 1)
            dve.wait_ge(S["d_top"], 5)
            dve.tensor_scalar(first[:], rank[:], 0.0, None, ALU.is_equal).then_inc(S["d_top"], 1)
            dve.wait_ge(S["d_top"], 6)
            dve.scalar_tensor_tensor(diff_m[:], rank[:], 1.0, first[:], ALU.is_equal, ALU.subtract).then_inc(S["d_top"], 1)
            dve.wait_ge(S["d_top"], 7)
            dve.scalar_tensor_tensor(second[:], diff_m[:], -1.0, logits[:], ALU.mult, ALU.mult).then_inc(S["d_top"], 1)
            dve.wait_ge(S["d_top"], 8)
            dve.tensor_reduce(gap[:], second[:], AX.X, ALU.add).then_inc(S["d_top"], 1)
            dve.wait_ge(S["a_tanh"], 1)
            dve.tensor_tensor(mix_w[:], diff_m[:], gap_t[:].unsqueeze(2).to_broadcast([P, NT, NX]), ALU.mult).then_inc(S["d_top"], 1)
            dve.tensor_scalar(second[:], rank[:], 1.5, None, ALU.is_lt).then_inc(S["d_top"], 1)
            dve.wait_ge(S["d_top"], 11)
            dve.tensor_tensor(mix_w[:], second[:], mix_w[:], ALU.subtract).then_inc(S["d_top"], 1)
            dve.wait_ge(S["d_top"], 12)
            dve.wait_ge(S["d_pad"], 1)
            for col in (0, 32):
                dve.tensor_scalar(w_pad[:, :, col:col + NX], mix_w[:], 0.5, None, ALU.mult).then_inc(S["d_pad"], 1)
            dve.wait_ge(S["a_eb"], 1)
            dve.tensor_tensor(eb2_lo[:], eb2_rows[:], eb2_hi[:], ALU.subtract).then_inc(S["d_wl"], 1)
            for c in range(NC):
                cs = slice(c * CH, (c + 1) * CH)
                dve.wait_ge(S["a_wth"], c + 1)
                dve.tensor_tensor(wt[32:64, cs], ps[32:64, c, :], wt[32:64, cs], ALU.subtract).then_inc(S["d_wl"], 1)
            dve.wait_ge(S["a_rh"], 1)
            dve.tensor_tensor(rot_lo[:], ps[:, 5, 0:P], rot_hi[:], ALU.subtract).then_inc(S["d_rl"], 1)

            def section(c, cur, prev):
                for j in range(NB):
                    if cur and j >= NA:
                        n = j - NA
                        dve.wait_ge(S["a_g"], c * NB + (j + 1))
                        dve.wait_ge(S["f_wb"], c * NX + (n // NXB + 1))
                        dve.tensor_tensor(hid[:, j % RING, :], hid[:, j % RING, :], ps[:, 2 + n // NXB % 2, :], ALU.mult).then_inc(S["d_hw"], 1)
                    if prev and j == T_SPLIT:
                        dve.wait_ge(S["a_mh"], c)
                        dve.tensor_tensor(moe_lo[:], ps[:, 5, :], moe_hi[:], ALU.subtract).then_inc(S["d_ml"], 1)
                    if prev and j == T_MIX:
                        base = (c - 1) * 3
                        dve.wait_ge(S["a_no"], c)
                        dve.wait_ge(S["a_ab"], c)
                        wait(dve, S["d_mix"], base)
                        dve.tensor_tensor(delta[:], nonabel[:], abel[:], ALU.subtract).then_inc(S["d_mix"], 1)
                        dve.wait_ge(S["a_th"], c)
                        dve.wait_ge(S["d_mix"], base + 1)
                        dve.scalar_tensor_tensor(delta[:], gate[:], 1.0, delta[:], ALU.add, ALU.mult).then_inc(S["d_mix"], 1)
                        dve.wait_ge(S["d_mix"], base + 2)
                        wait(dve, S["f_out"], c - 1)
                        dve.scalar_tensor_tensor(mixed[:], delta[:], 0.5, abel[:], ALU.mult, ALU.add).then_inc(S["d_mix"], 1)
                    if prev and j == T_NORM:
                        dve.wait_ge(S["f_out"], c)
                        ts = bass.ds((c - 1) * TPC, TPC)
                        wait(dve, S["d_ln3"], LN_STEPS * (c - 1))
                        dve.scalar_tensor_tensor(last_sum[:], y1[:, ts, :], 2.0, ps[:, 6, :].rearrange("p (t e) -> p t e", e=E),
                                                 ALU.mult, ALU.add).then_inc(S["d_v"], 1)
                        dve.wait_ge(S["d_v"], c)
                        norm = layer_norm(dve, S["d_ln3"], LN_STEPS * (c - 1), last_sum[:], y2[:, ts, :], ln_buf)
                    if prev and j >= T_NORM:
                        for _ in range(NORM_STEPS[j - T_NORM]):
                            next(norm)

            section(0, True, False)
            section(1, True, True)
            with dve.Fori(2, NC) as c:
                section(c, True, True)
            section(NC, False, True)

        @block.tensor
        def _(pe):
            for c in range(NC):
                for t in range(TPC):
                    last = pe.transpose(ps[:, c, t * P:(t + 1) * P], acc[:, (c * TPC + t) * P:(c * TPC + t + 1) * P], ident[:])
                last.then_inc(S["f_u"], 1)
            pe.wait_ge(S["l_small"], 16 * N_SMALL)
            pe.transpose(ps[:, 6, 0:N_VEC], vec_rows[:], ident[0:N_VEC, 0:N_VEC]).then_inc(S["f_vec"], 1)
            pe.wait_ge(S["l_gens"], 16)
            for r in range(NROT):
                last = pe.transpose(ps[:, 4, r * P:(r + 1) * P], gens_sb[:, r, :], ident[:])
            last.then_inc(S["f_gt"], 1)
            pe.wait_ge(S["a_gt"], 1)
            for j in range(2, TAYLOR + 1):
                pe.wait_ge(S["a_tay"], j - 1)
                for r in range(NROT):
                    last = pe.matmul(ps[:, 4, r * P:(r + 1) * P], gens_t[:, r, :], e_pow[:, (j - 1) % 2, r, :], start=True, stop=True)
                last.then_inc(S["f_tay"], 1)

            def turn():
                for r in range(NROT):
                    last = pe.transpose(ps[:, 5, r * P:(r + 1) * P], e_sum[:, r, :], ident[:])
                last.then_inc(S["f_sqt"], 1)

            def squaring(k):
                if k == 0:
                    pe.wait_ge(S["g_sum"], TAYLOR - 1)
                    pe.wait_ge(S["a_tay"], TAYLOR)
                    turn()
                pe.wait_ge(S["d_sqt"], k + 1)
                for r in range(NROT):
                    last = pe.matmul(ps[:, 4, r * P:(r + 1) * P], e_turn[:, r, :], e_sum[:, r, :], start=True, stop=True)
                last.then_inc(S["f_sq"], 1)
                pe.wait_ge(S["a_sq"], k + 1)
                turn()

            for c in range(NC):
                squaring(2 * c)
                squaring(2 * c + 1)
                pe.wait_ge(S["d_ln"], 2 * LN_STEPS * (c + 1))
                for t in range(TPC):
                    last = pe.transpose(ps[:, c, t * P:(t + 1) * P], n2[:, c % 2, t, :], ident[:])
                last.then_inc(S["f_n"], 1)
                pe.wait_ge(S["a_x"], 2 * c + 1)
                if c == 0:
                    pe.wait_ge(S["a_vec"], 1)
                for t in range(c * TPC, (c + 1) * TPC):
                    last = pe.matmul(ps[:, 6, t * NX:(t + 1) * NX], xn[:, t * P:(t + 1) * P], gw[:], start=True, stop=True)
                last.then_inc(S["f_log"], 1)
            pe.wait_ge(S["d_m"], 2)
            for k, r in enumerate((2, 1, 0)):
                if k > 0:
                    pe.wait_ge(S["a_r"], k)
                pe.matmul(ps[:, 5, 0:P], e_turn[:, r, :], rot[:, k - 1, :] if k else e_pow[:, 0, 0, :], start=True, stop=True).then_inc(S["f_r"], 1)
            pe.wait_ge(S["d_pad"], 4)
            pe.wait_ge(S["a_x"], 2 * NC)
            for c in range(NC):
                for t in range(TPC):
                    last = pe.transpose(ps[0:64, c, t * P:(t + 1) * P], w_pad[:, c * TPC + t, :], ident[:])
                last.then_inc(S["f_wt"], 1)

            def chunk(a, c):
                return a[:, bass.ds(c * CH, CH)]

            def layer2(c, j):
                into = ps[:, 4 if j < NA else 5, :]
                pe.wait_ge(S["g_hl"], c * NB + (j + 1))
                if j == 0:
                    wait(pe, S["a_ab"], c)
                if j == NA:
                    wait(pe, S["d_ml"], c)
                w = slice(LAYER2[j], LAYER2[j] + P)
                r = j % RING
                end = j in (NA - 1, NB - 1)
                for k, (a, h) in enumerate(((w_hi, hid_hi), (w_lo, hid_hi), (w_hi, hid_lo))):
                    last = pe.matmul(into, a[:, w], h[:, r, :], start=(k == 0 and j in (0, NA)), stop=(end and k == 2 and j < NA))
                last.then_inc(S["f_y"], 1)

            def section(c, cur, prev):
                for j in range(NB):
                    if cur:
                        wait(pe, S["a_hh"] if j in range(2, NA + 2) else S["a_g"], c * NB + (j - 1))
                        w = slice(LAYER1[j], LAYER1[j] + P)
                        for k, (a, h) in enumerate(((w_hi, xn_hi), (w_lo, xn_hi), (w_hi, xn_lo))):
                            last = pe.matmul(ps[:, j % 2, :], a[:, w], chunk(h, c), start=(k == 0), stop=(k == 2))
                        last.then_inc(S["f_h"], 1)
                        if j >= NA and (j - NA) % NXB == 0:
                            e = (j - NA) // NXB
                            wait(pe, S["d_hw"], c * (NB - NA) + NXB * (e - 1))
                            pe.matmul(ps[:, 2 + e % 2, :], pick[:, e, :], chunk(wt, c), start=True, stop=True).then_inc(S["f_wb"], 1)
                    if cur and j >= LAG:
                        layer2(c, j - LAG)
                    if prev and j < LAG:
                        layer2(c - 1, NB - LAG + j)
                        if j == LAG - 1:
                            pe.matmul(ps[:, 5, :], eb2_hi[:], chunk(wt, c - 1), start=False, stop=False)
                            pe.matmul(ps[:, 5, :], eb2_lo[:], chunk(wt, c - 1), start=False, stop=True).then_inc(S["f_ym"], 1)
                    if prev and j == T_ROTATE:
                        pe.wait_ge(S["d_ml"], c)
                        wait(pe, S["d_v"], c - 1)
                        for k, (a, m) in enumerate(((rot_hi, moe_hi), (rot_lo, moe_hi), (rot_hi, moe_lo))):
                            last = pe.matmul(ps[:, 6, :], a[:], m[:], start=(k == 0), stop=(k == 2))
                        last.then_inc(S["f_rot"], 1)
                    if prev and j == T_GATE:
                        pe.wait_ge(S["a_no"], c)
                        pe.wait_ge(S["a_ab"], c)
                        wait(pe, S["a_th"], c - 1)
                        pe.matmul(ps[:, 7, :], gc_wide[:, 0, :], abel[:], start=True, stop=False)
                        pe.matmul(ps[:, 7, :], gc_wide[:, 1, :], nonabel[:], start=False, stop=True).then_inc(S["f_gate"], 1)
                    if prev and j == T_TURN:
                        pe.wait_ge(S["d_mix"], 3 * c)
                        for t in range(TPC):
                            last = pe.transpose(ps[:, 6, t * P:(t + 1) * P], mixed[:, t * P:(t + 1) * P], ident[:])
                        last.then_inc(S["f_out"], 1)

            pe.wait_ge(S["d_wl"], 1 + NC)
            pe.wait_ge(S["d_xl"], NC)
            pe.wait_ge(S["g_wl"], W_PARTS)
            pe.wait_ge(S["d_rl"], 1)
            pe.wait_ge(S["d_log"], 1)
            pe.wait_ge(S["c_pick"], 1)
            section(0, True, False)
            section(1, True, True)
            with pe.Fori(2, NC) as c:
                section(c, True, True)
            section(NC, False, True)


def transformer_block(nc, x, w_qkv, w_o, ln_g, ln_b, aw1, ab1, aw2, ab2, gate_w, gate_b, ew1, eb1, ew2, eb2,
                      gens, gc_w, gc_b, pe2, out):
    with nc.sbuf_tensor("acc", [P, T], F32) as acc, nc.sbuf_tensor("ident", [P, P], F32) as ident:
        attention(nc, acc, ident, x, w_qkv, w_o, pe2)
        feed_forward(nc, acc, ident, x, ln_g, ln_b, aw1, ab1, aw2, ab2, gate_w, gate_b, ew1, eb1, ew2, eb2, gens,
                     gc_w, gc_b, out)


_INS = ["L0_attn_x", "L0_attn_Wqkv", "L0_attn_Wo", "L0_ffn_ln_g", "L0_ffn_ln_b", "L0_ffn_aw1", "L0_ffn_ab1",
        "L0_ffn_aw2", "L0_ffn_ab2", "L0_ffn_gate_w", "L0_ffn_gate_b", "L0_ffn_ew1", "L0_ffn_eb1", "L0_ffn_ew2",
        "L0_ffn_eb2", "L0_ffn_gens", "L0_ffn_gc_w", "L0_ffn_gc_b"]


def position_table():
    import numpy as np

    pos = np.arange(T, dtype=np.float32)[:, None]
    div = np.exp(np.arange(0, D, 2, dtype=np.float32) * np.float32(-np.log(10000.0) / D))
    angle = pos * div
    table = np.stack([np.sin(angle), np.cos(angle)], axis=-1).reshape(T, D).astype(np.float32)
    return np.ascontiguousarray(np.concatenate([table.T, table.T], axis=0))


def kernel(**inputs):
    import concourse.bacc as bacc
    import numpy as np
    from concourse.bass_utils import run_bass_kernel_spmd

    nc = bacc.Bacc("TRN2", target_bir_lowering=False, num_devices=1)
    arrays = {name: np.ascontiguousarray(inputs[name]) for name in _INS}
    arrays["positions"] = position_table()
    args = [nc.dram_tensor(name, a.shape, F32, kind="ExternalInput").ap() for name, a in arrays.items()]
    args.append(nc.dram_tensor("out", (1, T, E), F32, kind="ExternalOutput").ap())
    transformer_block(nc, *args)
    result = run_bass_kernel_spmd(nc, [arrays], core_ids=[0])
    return result.results[0]["out"]
```

```python
from contextlib import ExitStack

import concourse.bass as bass
from concourse import mybir

F32 = mybir.dt.float32
F32R = mybir.dt.float32r
BF16 = mybir.dt.bfloat16
ALU = mybir.AluOpType
ACT = mybir.ActivationFunctionType
AX = mybir.AxisListType

P = 128
T = 2048
E = 128
H = 8
D = 64
CH = 512
NC = T // CH
NT = T // P
TPC = CH // P
NEG = -1e30
LEAD = 20

PAIRS = [2 * (c + 1) for c in range(NC)]
PAIR0 = [sum(PAIRS[:c]) for c in range(NC + 1)]
NP = PAIR0[NC]
UNIT0 = [sum(TPC * (b + 1) for b in range(c)) for c in range(NC + 1)]
NU = UNIT0[NC]
I32 = mybir.dt.int32

EPS = 1e-5

NA = 4
NX = 6
NXB = 2
NB = NA + NX * NXB
N_SMALL = 9
N_VEC = 5 + NB
NROT = 4
SQUARINGS = 10
HALF = NROT // 2
EARLY = 7
CHOOSE = 12
LOGIT_BANK = (5, 7)
EARLY_FEATURES = 3
LAG = 3
RING = 4
NORM_STEPS = (6, 6, 6, 7)

LAYER1 = [P * j if j < NA else 2 * NA * P + P * (j - NA) for j in range(NB)]
LAYER2 = [NA * P + P * j if j < NA else 2 * NA * P + NX * NXB * P + P * (j - NA) for j in range(NB)]
W_COLS = 2 * NB * P
W_PARTS = 8

TURN_AT = {1: 7, 3: 8, 5: 9, 7: 10}
SQUARE_AT = {2: 7, 4: 8, 6: 9}
PRODUCT_AT = {9: 0, 10: 1, 11: 2}
FEATURES_AT = {0: 2, 2: 3}
LOW_AT = {1: 2, 3: 3}
LOGITS_AT, CHOOSE_AT = 4, 5
CHOOSE_STEPS = (3, 3, 3, 0, 2, 3)
WEIGHTS_AT = {12: 2, 14: 3}
WEIGHTS_LOW_AT = {13: 2, 15: 3}
T_ABEL, T_SPLIT, T_ROTATE, T_NONABEL, T_GATE, T_TANH, T_MIX, T_TURN, T_NORM = 1, 3, 5, 6, 7, 8, 9, 11, 12

def ln_steps(n):
    return 3 * n + 13


def chunk_of(starts, n):
    return max(c for c in range(NC) if starts[c] <= n)


def at(g, per, local):
    i, offset = g
    return i * (2 * per) + (offset * per + local)


def plus(g, n):
    return (g[0], g[1] + n)


def index(g):
    return g[0] * 2 + g[1]


def wait(eng, sem, value):
    if not isinstance(value, int) or value > 0:
        eng.wait_ge(sem, value)


PROJECT = {4: (0, 1), 8: (1, 1), 11: (2, 1), 17: (3, 1)}
TURN = {2: (2, 0), 10: (3, 0), 12: (0, 1), 16: (1, 1)}
OUTPUT = {7: (3, -1), 9: (0, 0), 15: (1, 0), 19: (2, 0)}


def due(table, p, after, cur, nxt, prev):
    for slot, (c, ahead) in table.items():
        if (slot + after) % NP == p:
            ahead -= (slot + after) // NP
            if (nxt if ahead > 0 else prev if ahead < 0 else cur):
                return [(c, ahead)]
    return []


V_LOW = (16, 18)

V_TILES = [range(2 * p, 2 * p + 2) if p < 4 else range(p + 4, p + 5) if p < 12 else () for p in range(NP)]

DONE = {PAIR0[c + 1] + 2: (c, 0) for c in range(NC)}


def attention(nc, acc, ident, pos, qk, v_all, x, w_qkv, w_o, pe2, load_early):
    with ExitStack() as ctx:
        def sb(name, shape, dt=F32):
            return ctx.enter_context(nc.sbuf_tensor(name, shape, dt))

        def psum(name, shape, dt=F32):
            return ctx.enter_context(nc.psum_tensor(name, shape, dt))

        def sem(name):
            return ctx.enter_context(nc.semaphore(name))

        xh = sb("xh", [P, T], F32R)
        xl = sb("xl", [P, T], F32R)
        wth = sb("wth", [P, H, 2, D], F32R)
        wtl = sb("wtl", [P, H, 2, D], F32R)
        woh = sb("woh", [P, H, E], F32R)
        wol = sb("wol", [P, H, E], F32R)
        w_head = sb("w_head", [P, 2, P], F32R)
        wo_head = sb("wo_head", [P, 2, 2, E], F32R)
        v1 = sb("v1", [P, 2, NT, 2 * D], F32R)
        v2 = sb("v2", [P, 2, NT, D], F32R)
        q1 = sb("q1", [P, T], F32R)
        q2 = sb("q2", [P, T], F32R)
        k1 = sb("k1", [P, 2, T], F32R)
        k2 = sb("k2", [P, 2, T], F32R)
        probs = sb("probs", [P, 2, 2, CH])
        probs_h = sb("probs_h", [P, 4, 2, CH], F32R)
        probs_l = sb("probs_l", [P, 2, 2, CH], F32R)
        oh = sb("oh", [P, 2, CH], F32R)
        o_sum = sb("o_sum", [P, CH])
        l_both = sb("l_both", [P, CH])
        l_rows, l_cols = l_both[0:D, :], l_both[D:P, :]
        l_inv = sb("l_inv", [P, CH // 32])
        o_norm = sb("o_norm", [D, 2, CH])
        m_part = sb("m_part", [P, TPC, NC])
        m_max = sb("m_max", [P, 2, TPC])
        m_row = sb("m_row", [TPC, P], F32R)
        ident_b = sb("ident_b", [P, P], BF16)
        mask_kq = sb("mask_kq", [P, 2 * P], BF16)
        mask_qk = sb("mask_qk", [P, P], BF16)
        wvh, wvl = k1[:, 1, 0:CH], k1[:, 1, CH:2 * CH]
        x_tok = probs[:].rearrange("p b j q -> p (b j q)").rearrange("p (n e) -> p n e", e=E)
        wq_raw = acc[:, 0:12 * P].rearrange("p (n e) -> p n e", n=12)
        wo_raw = v_all[:, 0, :, :].rearrange("p t d -> p (t d)").rearrange("p (h r d) -> p h r d", h=H, r=2)

        scores = psum("scores", [P, 2, 2, CH])
        o_ps = psum("o_ps", [P, CH])
        max_ps = psum("max_ps", [P, 2, CH])
        side_ps = psum("side_ps", [P, CH])

        names = """ld_w ld_wo ld_x ld_pos c_ident c_masks c_v c_q2 c_acc
            p_wt a_wt d_wt p_xt a_xt d_xt p_v a_v
            p_q p_max p_turn p_out p_score p_pv
            a_exp a_expr a_k1 a_q1 a_q2 a_w a_wo a_vh a_oh a_o
            g_pl
            d_q d_ql d_kl d_max d_mx d_row d_lt d_inv d_bc d_lr d_on d_oh d_acc d_vl
            s_m""".split()
        S = {n: sem(n) for n in names}
        block = ctx.enter_context(nc.Block())

        def units(p, cur, nxt):
            for n in (2 * p + LEAD, 2 * p + LEAD + 1):
                if n < NU and cur:
                    yield 0, n
                if n >= NU and nxt:
                    yield 1, n - NU

        def unit_place(u):
            c = chunk_of(UNIT0, u)
            r, j = divmod(u - UNIT0[c], c + 1)
            return c, r, j, (CH if j < c else P * (r + 1))

        def group(n, hi):
            if n < 3:
                if n == 2:
                    return wvh if hi else wvl
                return (wth if hi else wtl)[:, 4 * n:4 * (n + 1), :, :].rearrange("p h s d -> p (h s d)")
            if n < 7:
                return (xh if hi else xl)[:, (n - 3) * CH:(n - 2) * CH]
            return (woh if hi else wol)[:, 4 * (n - 7):4 * (n - 6), :].rearrange("p h e -> p (h e)")

        def high(n):
            return group(n, True)

        GROUPS = 3 + 4 + 2

        @block.sync
        def _(sp):
            w_rows = w_qkv.rearrange("(h s d) e -> s d h e", h=H, s=3)
            for s in range(2):
                sp.dma_start(wq_raw[s * D:(s + 1) * D, 0:H, :], w_rows[s]).then_inc(S["ld_w"], 16)
            v_rows = w_rows[2].rearrange("d (n r) e -> r d n e", r=2)
            for r in range(2):
                sp.dma_start(wq_raw[r * D:(r + 1) * D, H:H + H // 2, :], v_rows[r]).then_inc(S["ld_w"], 16)
            sp.dma_start(x_tok, x.rearrange("b (n p) e -> p (b n) e", p=P)).then_inc(S["ld_x"], 16)
            for r in range(2):
                sp.dma_start(wo_raw[:, :, r, :], w_o.rearrange("e (h d) -> e h d", d=D)).then_inc(S["ld_wo"], 16)
            sp.dma_start(pos[:], pe2).then_inc(S["ld_pos"], 16)

            def section(g, cur, nxt):
                for p in range(NP):
                    for c, ahead in due(TURN, p, 0, cur, nxt, False):
                        h = plus(g, ahead)
                        wait(sp, S["d_row"], at(h, NC, c + 1))
                        sp.dma_start(q2[D:D + 1, c * CH:(c + 1) * CH].bitcast(F32), m_row[:].bitcast(F32)).then_inc(S["s_m"], 16)

            sp.wait_ge(S["c_q2"], 3)
            section((0, -1), False, True)
            section((0, 0), True, True)
            with sp.Fori(0,(H - 2) // 2) as i:
                for o in (1, 2):
                    section((i, o), True, True)
            section((0, H - 1), True, False)
            for signal, per_head in (("d_q", NC), ("d_ql", NC), ("d_kl", NC), ("a_q2", NC), ("a_k1", 2 * NC), ("d_vl", 2)):
                sp.wait_ge(S[signal], H * per_head)
            load_early(sp)

        @block.gpsimd
        def _(pool):
            pool.memset(ident[:], 0.0).then_inc(S["c_ident"], 1)
            pool.wait_ge(S["c_ident"], 1)
            pool.affine_select(out=ident[:], in_=ident[:], compare_op=ALU.not_equal, fill=1.0, base=0,
                               pattern=[[-1, P]], channel_multiplier=1).then_inc(S["c_ident"], 1)
            pool.memset(ident_b[:], 0.0).then_inc(S["c_masks"], 1)
            pool.memset(mask_kq[:], 0.0).then_inc(S["c_masks"], 1)
            pool.memset(mask_qk[:], 0.0).then_inc(S["c_masks"], 1)
            pool.wait_ge(S["c_masks"], 3)
            pool.affine_select(out=ident_b[:], in_=ident_b[:], compare_op=ALU.not_equal, fill=1.0, base=0,
                               pattern=[[-1, P]], channel_multiplier=1).then_inc(S["c_masks"], 1)
            pool.affine_select(out=mask_kq[:], in_=mask_kq[:], compare_op=ALU.is_ge, fill=NEG, base=-P,
                               pattern=[[1, 2 * P]], channel_multiplier=-1).then_inc(S["c_masks"], 1)
            pool.affine_select(out=mask_qk[:], in_=mask_qk[:], compare_op=ALU.is_ge, fill=NEG, base=0,
                               pattern=[[-1, P]], channel_multiplier=1).then_inc(S["c_masks"], 1)
            pool.wait_ge(S["c_masks"], 6)
            pool.memset(q2[D:P, :].bitcast(F32), 0.0).then_inc(S["c_q2"], 1)
            pool.memset(k2[D:P, :, :].bitcast(F32), 0.0).then_inc(S["c_q2"], 1)
            pool.wait_ge(S["c_q2"], 2)
            pool.memset(k2[D:D + 1, :, :].bitcast(F32), 1.0).then_inc(S["c_q2"], 1)
            pool.wait_ge(S["c_q2"], 3)
            for b in range(2):
                pool.memset(v1[:, b, :, D:2 * D].bitcast(F32), 1.0).then_inc(S["c_v"], 1)

            def section(g, cur, nxt):
                for p in range(NP):
                    if cur:
                        c = chunk_of(PAIR0, p)
                        lo = CH // 2 if p == PAIR0[c + 1] - 1 else 0
                        wait(pool, S["a_expr"], at(g, NP, p + 1))
                        wait(pool, S["p_pv"], at(g, NP, p - 1))
                        pool.tensor_tensor(probs_l[:, p % 2, :, lo:CH], probs[:, p % 2, :, lo:CH],
                                           probs_h[:, p % 4, :, lo:CH], ALU.subtract).then_inc(S["g_pl"], 1)

            section((0, -1), False, True)
            section((0, 0), True, True)
            with pool.Fori(0,(H - 2) // 2) as i:
                for o in (1, 2):
                    section((i, o), True, True)
            section((0, H - 1), True, False)

        @block.scalar
        def _(act):
            for n in range(GROUPS):
                act.wait_ge(S["p_wt"], n + 1)
                act.activation(high(n), scores[:, n % 4 // 2, n % 2, :], ACT.Copy).then_inc(S["a_wt"], 1)

            def w_copy(g):
                wait(act, S["p_q"], at(g, NC, 0))
                for part, w in enumerate((wth, wtl)):
                    act.activation(w_head[:, part, :], w[:, bass.ds(index(g), 1), :, :].rearrange("p h s d -> p (h s d)"),
                                   ACT.Copy).then_inc(S["a_w"], 1)

            def wo_copy(g):
                wait(act, S["p_out"], at(g, NC, -NC))
                for part, w in enumerate((woh, wol)):
                    act.activation(wo_head[:, g[1] % 2, part, :], w[:, bass.ds(index(g), 1), :].rearrange("p h e -> p (h e)"),
                                   ACT.Copy).then_inc(S["a_wo"], 1)

            def v_high(g):
                b = g[1] % 2
                wait(act, S["p_pv"], at(g, NP, -NP))
                act.wait_ge(S["a_v"], NT)
                act.activation(v1[:, b, :, 0:D], v_all[:, bass.ds(index(g), 1), :, :].rearrange("p h t d -> p (h t) d"),
                               ACT.Copy).then_inc(S["a_vh"], 1)

            def section(g, cur, nxt, prev, first=False):
                for p in range(NP):
                    for c, ahead in due(DONE, p, 0, cur, nxt, prev):
                        h = plus(g, ahead)
                        act.wait_ge(S["p_pv"], at(h, NP, PAIR0[c + 1]))
                        wait(act, S["d_on"], at(h, NC, c))
                        act.activation(o_sum[:], o_ps[:], ACT.Copy).then_inc(S["a_o"], 1)
                    if cur:
                        c = chunk_of(PAIR0, p)
                        lo = CH // 2 if p == PAIR0[c + 1] - 1 else 0
                        act.wait_ge(S["p_score"], at(g, NP, p + 1))
                        wait(act, S["g_pl"], at(g, NP, p - 1))
                        act.activation(probs[:, p % 2, :, lo:CH], scores[:, p % 2, :, lo:CH], ACT.Exp,
                                       scale=D ** -0.5).then_inc(S["a_exp"], 1)
                        wait(act, S["p_pv"], at(g, NP, p - 3))
                        act.activation(probs_h[:, p % 4, :, lo:CH], scores[:, p % 2, :, lo:CH], ACT.Exp,
                                       scale=D ** -0.5).then_inc(S["a_expr"], 1)
                    if p == 1 and nxt:
                        w_copy(plus(g, 1))
                    for c, ahead in due(PROJECT, p, 1, cur, nxt, prev):
                        h = plus(g, ahead)
                        ks = slice(c * CH, (c + 1) * CH)
                        act.wait_ge(S["d_q"], at(h, NC, c + 1))
                        for rows in (slice(0, D), slice(D, P)):
                            act.activation(k1[rows, h[1] % 2, ks], qk[D:P, c % 2, :], ACT.Copy).then_inc(S["a_k1"], 1)
                    for c, ahead in due(PROJECT, p, 2, cur, nxt, prev):
                        h = plus(g, ahead)
                        qs = slice(c * CH, (c + 1) * CH)
                        wait(act, S["p_score"], at(h, NP, PAIR0[c + 1] - NP))
                        act.activation(q1[0:D, qs], qk[0:D, c % 2, :], ACT.Copy).then_inc(S["a_q1"], 1)
                        act.activation(q2[0:D, qs], qk[0:D, c % 2, :], ACT.Copy).then_inc(S["a_q2"], 1)
                    for n in V_TILES[p] if first else ():
                        act.wait_ge(S["p_v"], n + 1)
                        act.activation(v_all[:, :, n, :], scores[:, n % 4 // 2, n % 2, :].rearrange("p (h d) -> p h d", h=H),
                                       ACT.Copy).then_inc(S["a_v"], 1)
                    if p == 9 and nxt:
                        wo_copy(plus(g, 1))
                    if p == 15 and nxt:
                        v_high(plus(g, 1))
                    for c, ahead in due(DONE, p, 2, cur, nxt, prev):
                        h = plus(g, ahead)
                        act.wait_ge(S["d_on"], at(h, NC, c + 1))
                        wait(act, S["p_out"], at(h, NC, c - 1))
                        act.activation(oh[0:D, c % 2, :], o_norm[:, c % 2, :], ACT.Copy).then_inc(S["a_oh"], 1)

            section((0, -1), False, True, False, first=True)
            section((0, 0), True, True, False)
            with act.Fori(0,(H - 2) // 2) as i:
                for o in (1, 2):
                    section((i, o), True, True, True)
            section((0, H - 1), True, False, True)
            section((0, H), False, False, True)

        @block.vector
        def _(dve):
            for n in range(GROUPS):
                dve.wait_ge(S["a_wt"], n + 1)
                dve.tensor_tensor(group(n, False), scores[:, n % 4 // 2, n % 2, :], high(n), ALU.subtract).then_inc(S["d_wt"], 1)
            dve.memset(acc[:], 0.0).then_inc(S["c_acc"], 1)
            dve.wait_ge(S["c_acc"], 1)

            def v_low(g, part):
                dve.wait_ge(S["a_vh"], at(g, 1, 1))
                b, ts = g[1] % 2, slice(part * NT // 2, (part + 1) * NT // 2)
                dve.tensor_tensor(v2[:, b, ts, :], v_all[:, bass.ds(index(g), 1), ts, :].rearrange("p h t d -> p (h t) d"),
                                  v1[:, b, ts, 0:D], ALU.subtract).then_inc(S["d_vl"], 1)

            def section(g, cur, nxt, prev):
                for p in range(NP):
                    for ahead, u in units(p, cur, nxt):
                        h = plus(g, ahead)
                        c, r, j, width = unit_place(u)
                        if u == UNIT0[c]:
                            wait(dve, S["d_mx"], at(h, NC, c))
                        dve.wait_ge(S["p_max"], at(h, NU, u + 1))
                        dve.tensor_reduce(m_part[:, r, j:j + 1], max_ps[:, u % 2, 0:width], AX.X, ALU.max).then_inc(S["d_max"], 1)
                        if u + 1 == UNIT0[c + 1]:
                            dve.wait_ge(S["d_max"], at(h, NU, u + 1))
                            wait(dve, S["p_turn"], at(h, NC, c - 1))
                            dve.tensor_reduce(m_max[:, c % 2, :], m_part[:, :, 0:c + 1], AX.X, ALU.max).then_inc(S["d_mx"], 1)
                    for c, ahead in due(OUTPUT, p, 0, cur, nxt, prev):
                        h = plus(g, ahead)
                        qs = slice(c * CH, (c + 1) * CH)
                        wait(dve, S["d_acc"], at(h, NC, c - NC + 1))
                        dve.wait_ge(S["p_out"], at(h, NC, c + 1))
                        dve.tensor_tensor(acc[:, qs], acc[:, qs], side_ps[:], ALU.add).then_inc(S["d_acc"], 1)
                    for c, ahead in due(TURN, p, 0, cur, nxt, prev):
                        h = plus(g, ahead)
                        wait(dve, S["p_score"], at(h, NP, PAIR0[c + 1] - NP))
                        wait(dve, S["s_m"], at(h, 16 * NC, 16 * c))
                        dve.wait_ge(S["p_turn"], at(h, NC, c + 1))
                        dve.tensor_scalar(m_row[:], side_ps[0:TPC, 0:P], -1.0, None, ALU.mult).then_inc(S["d_row"], 1)
                    for c, ahead in due(PROJECT, p, 0, cur, nxt, prev):
                        h = plus(g, ahead)
                        wait(dve, S["d_ql"], at(h, NC, c - 1))
                        wait(dve, S["d_kl"], at(h, NC, c - 1))
                        wait(dve, S["a_q2"], at(h, NC, c - 1))
                        wait(dve, S["a_k1"], at(h, 2 * NC, 2 * (c - 1)))
                        dve.wait_ge(S["p_q"], at(h, NC, c + 1))
                        dve.tensor_tensor(qk[:, c % 2, :], side_ps[:], pos[:, c * CH:(c + 1) * CH], ALU.add).then_inc(S["d_q"], 1)
                    for c, ahead in due(DONE, p, 0, cur, nxt, prev):
                        h = plus(g, ahead)
                        wait(dve, S["d_lr"], at(h, NC, c))
                        dve.wait_ge(S["a_o"], at(h, NC, c + 1))
                        dve.transpose(l_cols, o_sum[D:P, :]).then_inc(S["d_lt"], 1)
                    for c, ahead in due(PROJECT, p, 2, cur, nxt, prev):
                        h = plus(g, ahead)
                        b, ks = h[1] % 2, slice(c * CH, (c + 1) * CH)
                        dve.wait_ge(S["a_k1"], at(h, 2 * NC, 2 * (c + 1)))
                        dve.tensor_tensor(k2[0:D, b, ks], qk[D:P, c % 2, :], k1[D:P, b, ks], ALU.subtract).then_inc(S["d_kl"], 1)
                    for c, ahead in due(PROJECT, p, 3, cur, nxt, prev):
                        h = plus(g, ahead)
                        qs = slice(c * CH, (c + 1) * CH)
                        dve.wait_ge(S["a_q2"], at(h, NC, c + 1))
                        dve.tensor_tensor(q1[D:P, qs], qk[0:D, c % 2, :], q1[0:D, qs], ALU.subtract).then_inc(S["d_ql"], 1)
                    for c, ahead in due(DONE, p, 0, cur, nxt, prev):
                        h = plus(g, ahead)
                        dve.wait_ge(S["d_lt"], at(h, NC, c + 1))
                        dve.reciprocal(l_inv[D:P, :], l_cols.rearrange("p (b j) -> p b j", j=32)[:, :, 0]).then_inc(S["d_inv"], 1)
                        dve.wait_ge(S["d_inv"], at(h, NC, c + 1))
                        dve.tensor_copy(l_cols.rearrange("p (b j) -> p b j", j=32),
                                        l_inv[D:P, :].unsqueeze(2).to_broadcast([D, CH // 32, 32])).then_inc(S["d_bc"], 1)
                        dve.wait_ge(S["d_bc"], at(h, NC, c + 1))
                        wait(dve, S["d_on"], at(h, NC, c))
                        dve.transpose(l_rows, l_cols).then_inc(S["d_lr"], 1)
                    for c, ahead in due(DONE, p, 1, cur, nxt, prev):
                        h = plus(g, ahead)
                        dve.wait_ge(S["d_lr"], at(h, NC, c + 1))
                        wait(dve, S["d_oh"], at(h, NC, c - 1))
                        dve.tensor_tensor(o_norm[:, c % 2, :], o_sum[0:D, :], l_rows, ALU.mult).then_inc(S["d_on"], 1)
                    if p in V_LOW and nxt:
                        v_low(plus(g, 1), V_LOW.index(p))
                    for c, ahead in due(DONE, p, 3, cur, nxt, prev):
                        h = plus(g, ahead)
                        dve.wait_ge(S["a_oh"], at(h, NC, c + 1))
                        dve.tensor_tensor(oh[D:P, c % 2, :], o_norm[:, c % 2, :], oh[0:D, c % 2, :], ALU.subtract).then_inc(S["d_oh"], 1)

            dve.wait_ge(S["ld_pos"], 16)
            section((0, -1), False, True, False)
            section((0, 0), True, True, False)
            with dve.Fori(0,(H - 2) // 2) as i:
                for o in (1, 2):
                    section((i, o), True, True, True)
            section((0, H - 1), True, False, True)
            section((0, H), False, False, True)

        @block.tensor
        def _(pe):
            pe.wait_ge(S["c_ident"], 2)
            for n in range(GROUPS):
                if n >= 4:
                    pe.wait_ge(S["d_wt"], n - 3)
                if n == 0:
                    pe.wait_ge(S["ld_w"], 64)
                if n == 3:
                    pe.wait_ge(S["ld_x"], 16)
                if n == 7:
                    pe.wait_ge(S["ld_wo"], 32)
                for j in range(4):
                    if n < 3:
                        src = wq_raw[:, 4 * n + j, :]
                    elif n < 7:
                        src = x_tok[:, 4 * (n - 3) + j, :]
                    else:
                        src = wo_raw[:, 4 * (n - 7) + j, :, :].rearrange("p r d -> p (r d)")
                    last = pe.transpose(scores[:, n % 4 // 2, n % 2, j * P:(j + 1) * P], src, ident[:])
                last.then_inc(S["p_wt"], 1)
            def v_tile(n):
                if n == 0:
                    pe.wait_ge(S["d_wt"], GROUPS)
                if n >= 4:
                    pe.wait_ge(S["a_v"], n - 3)
                ts = slice(n * P, (n + 1) * P)
                for k, (a, w) in enumerate(((xh, wvh), (xh, wvl), (xl, wvh))):
                    last = pe.matmul(scores[:, n % 4 // 2, n % 2, :], a[:, ts], w, start=(k == 0), stop=(k == 2))
                last.then_inc(S["p_v"], 1)

            def project(h, c):
                xs = slice(c * CH, (c + 1) * CH)
                for k, (w, a) in enumerate(((0, xh), (0, xl), (1, xh))):
                    last = pe.matmul(side_ps[:], w_head[:, w, :], a[:, xs], start=(k == 0), stop=(k == 2))
                last.then_inc(S["p_q"], 1)

            def maximum(h, u):
                c, r, j, width = unit_place(u)
                b = h[1] % 2
                if u == UNIT0[c]:
                    pe.wait_ge(S["d_ql"], at(h, NC, c + 1))
                    pe.wait_ge(S["a_k1"], at(h, 2 * NC, 2 * (c + 1)))
                wait(pe, S["d_max"], at(h, NU, u - 1))
                n = max(width, 2 * P)
                ks = slice(j * CH, j * CH + n)
                tile = (c * TPC + r) * P
                last = pe.matmul(max_ps[:, u % 2, 0:n], q1[:, tile:tile + P], k1[:, b, ks], start=True, stop=(j < c))
                if j == c:
                    last = pe.matmul(max_ps[:, u % 2, width - P:width], ident_b[:], mask_qk[:], start=False, stop=True)
                last.then_inc(S["p_max"], 1)

            def turn(h, c):
                pe.wait_ge(S["d_mx"], at(h, NC, c + 1))
                pe.transpose(side_ps[0:TPC, 0:P], m_max[:, c % 2, :], ident[:]).then_inc(S["p_turn"], 1)

            def output(h, c):
                pe.wait_ge(S["d_oh"], at(h, NC, c + 1))
                if c == 0:
                    pe.wait_ge(S["a_wo"], at(h, 2, 2))
                for part in range(2):
                    last = pe.matmul(side_ps[:], wo_head[:, h[1] % 2, part, :], oh[:, c % 2, :], start=(part == 0), stop=(part == 1))
                last.then_inc(S["p_out"], 1)

            def score_pair(h, p):
                c = chunk_of(PAIR0, p)
                b = h[1] % 2
                if p == PAIR0[c]:
                    pe.wait_ge(S["s_m"], at(h, 16 * NC, 16 * (c + 1)))
                    pe.wait_ge(S["d_kl"], at(h, NC, c + 1))
                wait(pe, S["a_expr"], at(h, NP, p - 1))
                for j in range(2):
                    kb = 2 * (p - PAIR0[c]) + j
                    diag = kb - TPC * c
                    lo = CH // 2 if diag >= 2 else 0
                    ks = slice(kb * P, (kb + 1) * P)
                    qs = slice(c * CH + lo, (c + 1) * CH)
                    into = scores[:, p % 2, j, lo:CH]
                    pe.matmul(into, k1[:, b, ks], q1[:, qs], start=True, stop=False)
                    last = pe.matmul(into, k2[:, b, ks], q2[:, qs], start=False, stop=(diag < 0))
                    if diag >= 0:
                        m0 = 0 if diag == 3 else P
                        last = pe.matmul(scores[:, p % 2, j, (diag + 1) * P - (2 * P - m0):(diag + 1) * P], ident_b[:],
                                         mask_kq[:, m0:2 * P], start=False, stop=True)
                last.then_inc(S["p_score"], 1)

            def pv_pair(h, p):
                c = chunk_of(PAIR0, p)
                b = h[1] % 2
                pe.wait_ge(S["g_pl"], at(h, NP, p + 1))
                if p == PAIR0[c]:
                    wait(pe, S["a_o"], at(h, NC, c))
                if p == 0:
                    pe.wait_ge(S["d_vl"], at(h, 2, 2))
                for j in range(2):
                    kb = 2 * (p - PAIR0[c]) + j
                    diag = kb - TPC * c
                    lo = P * min(diag, 2) if diag > 0 else 0
                    hi_v = v1[:, b, kb, :]
                    lo_v = v2[:, b, kb, :]
                    for k, (v, rows, pr) in enumerate(((hi_v, P, probs_h[:, p % 4, j, lo:CH]),
                                                       (lo_v, D, probs_h[:, p % 4, j, lo:CH]),
                                                       (hi_v, P, probs_l[:, p % 2, j, lo:CH]))):
                        last = pe.matmul(o_ps[0:rows, lo:CH], v, pr, start=(p == PAIR0[c] and j == 0 and k == 0),
                                         stop=(p == PAIR0[c + 1] - 1 and j == 1 and k == 2))
                last.then_inc(S["p_pv"], 1)

            def section(g, cur, nxt, prev, first=False):
                before = [("d_acc", at(plus(g, -1), NC, NC - 1))] if prev else [("d_q", at(g, NC, NC))] if cur else []

                def side_bank(evacuated, value):
                    if before:
                        wait(pe, S[before[0][0]], before[0][1])
                    before[:] = [(evacuated, value)]

                for p in range(NP):
                    if cur:
                        score_pair(g, p)
                    for ahead, u in units(p, cur, nxt):
                        maximum(plus(g, ahead), u)
                    for c, ahead in due(OUTPUT, p, 0, cur, nxt, prev):
                        side_bank("d_acc", at(plus(g, ahead), NC, c + 1))
                        output(plus(g, ahead), c)
                    for c, ahead in due(TURN, p, 0, cur, nxt, prev):
                        side_bank("d_row", at(plus(g, ahead), NC, c + 1))
                        turn(plus(g, ahead), c)
                    for c, ahead in due(PROJECT, p, 0, cur, nxt, prev):
                        if c == 0:
                            pe.wait_ge(S["a_w"], at(plus(g, ahead), 2, 2))
                        side_bank("d_q", at(plus(g, ahead), NC, c + 1))
                        project(plus(g, ahead), c)
                    for n in V_TILES[p] if first else ():
                        v_tile(n)
                    if p >= 2 and cur:
                        pv_pair(g, p - 2)
                    if p < 2 and prev:
                        pv_pair(plus(g, -1), NP - 2 + p)

            pe.wait_ge(S["c_masks"], 6)
            section((0, -1), False, True, False, first=True)
            pe.wait_ge(S["c_v"], 2)
            pe.wait_ge(S["c_q2"], 3)
            section((0, 0), True, True, False)
            with pe.Fori(0,(H - 2) // 2) as i:
                for o in (1, 2):
                    section((i, o), True, True, True)
            section((0, H - 1), True, False, True)
            section((0, H), False, False, True)


def layer_norm(dve, sem, base, src, dst, buf, n):
    stats, mean_var, s, pause = buf
    var, half, guess, t, bits = (s[:, i, 0:n] for i in range(5))
    if not isinstance(base, int) or base > 0:
        dve.wait_ge(sem, base)
    for i in range(n):
        dve.bn_stats(stats[:, i, :], src[:, i, :]).then_inc(sem, 1)
        yield
    dve.wait_ge(sem, base + n)
    dve.memset(pause, 0.0).then_inc(sem, 1)
    yield
    base = base + 1
    for i in range(n):
        dve.bn_aggr(mean_var[:, i, :], stats[:, i, :]).then_inc(sem, 1)
        yield
    dve.wait_ge(sem, base + 2 * n)
    dve.tensor_scalar(var, mean_var[:, 0:n, 1], EPS, None, ALU.add).then_inc(sem, 1)
    yield
    base = base + 2 * n
    dve.wait_ge(sem, base + 1)
    dve.tensor_scalar(bits.bitcast(I32), var.bitcast(I32), 1, None, ALU.logical_shift_right).then_inc(sem, 1)
    yield
    dve.wait_ge(sem, base + 2)
    dve.tensor_scalar(guess.bitcast(I32), bits.bitcast(I32), -1, 0x5F3759DF, ALU.mult, ALU.add).then_inc(sem, 1)
    yield
    for k in range(3):
        dve.wait_ge(sem, base + 3 + 3 * k)
        dve.tensor_tensor(t, guess, guess, ALU.mult).then_inc(sem, 1)
        yield
        dve.wait_ge(sem, base + 4 + 3 * k)
        dve.scalar_tensor_tensor(half, var, -0.5, t, ALU.mult, ALU.mult).then_inc(sem, 1)
        yield
        dve.wait_ge(sem, base + 5 + 3 * k)
        dve.scalar_tensor_tensor(guess, half, 1.5, guess, ALU.add, ALU.mult).then_inc(sem, 1)
        yield
    dve.wait_ge(sem, base + 12)
    for i in range(n):
        dve.tensor_scalar(dst[:, i, :], src[:, i, :], mean_var[:, i, 0:1], guess[:, i:i + 1],
                          ALU.subtract, ALU.mult).then_inc(sem, 1)
        yield


class Early:

    def __init__(self, pos, qk, v_all, sems):
        self.x_in = pos[:].rearrange("p (n e) -> p n e", e=E)
        self.gens = qk[:, 0, :].rearrange("p (r j) -> p r j", r=NROT)
        small = qk[:, 1, :]
        self.vec_rows = small[0:N_VEC, 0:P]
        self.gw, self.gb, self.gcb = small[:, P:P + NX], small[:, P + NX:P + 2 * NX], small[:, P + 2 * NX:P + 2 * NX + 1]
        free = v_all[:].rearrange("p h t d -> p (h t d)")
        self.w_raw = free[:, 0:W_COLS]
        self.n2, self.y2 = (free[:, a:a + T].rearrange("p (n e) -> p n e", e=E) for a in (W_COLS, W_COLS + T))
        self.sems = sems

    def load(self, sp, x, ln_g, ln_b, aw1, ab1, aw2, ab2, gate_w, gate_b, ew1, eb1, ew2, eb2, gens, gc_w, gc_b):
        S = self.sems

        def row(a, n=1):
            return self.vec_rows[a:a + n, :]

        sp.dma_start(self.x_in, x.rearrange("b (n p) e -> p (b n) e", p=P)).then_inc(S["l_x"], 16)
        sp.dma_start(self.gens, gens.rearrange("r i j -> i r j")).then_inc(S["l_gens"], 16)
        small = [(self.gw, gate_w), (self.gb, gate_b.partition_broadcast(P)), (self.gcb, gc_b.partition_broadcast(P)),
                 (row(0), ln_g.rearrange("(o d) -> o d", o=1)), (row(1), ln_b.rearrange("(o d) -> o d", o=1)),
                 (row(2), ab2.rearrange("(o d) -> o d", o=1)), (row(3, 2), gc_w.rearrange("(o d) u -> o (d u)", o=2)),
                 (row(5, NA), ab1.rearrange("(m p) -> m p", p=P)),
                 (row(5 + NA, NX * NXB), eb1.rearrange("e (k p) -> (e k) p", p=P))]
        assert len(small) == N_SMALL
        for dst, src in small:
            sp.dma_start(dst, src).then_inc(S["l_small"], 16)
        A, X = NA * P, NX * NXB * P
        sp.dma_start(self.w_raw[:, 0:A], aw1).then_inc(S["l_w"], 16)
        sp.dma_start(self.w_raw[:, A:2 * A].rearrange("p (m d) -> p m d", m=NA), aw2.rearrange("(m p) d -> p m d", p=P)).then_inc(S["l_w"], 16)
        sp.dma_start(self.w_raw[:, 2 * A:2 * A + X].rearrange("p (e h) -> p e h", e=NX), ew1.rearrange("e d h -> d e h")).then_inc(S["l_w"], 16)
        sp.dma_start(self.w_raw[:, 2 * A + X:].rearrange("p (e k d) -> p e k d", e=NX, k=NXB),
                     ew2.rearrange("e (k p) d -> p e k d", p=P)).then_inc(S["l_w"], 16)


def feed_forward(nc, early, acc, ident, eb2, out):
    with ExitStack() as ctx:
        def sb(name, shape, dt=F32):
            return ctx.enter_context(nc.sbuf_tensor(name, shape, dt))

        def sem(name):
            return ctx.enter_context(nc.semaphore(name))

        w_hi = sb("w_hi", [P, W_COLS], F32R)
        w_lo = sb("w_lo", [P, W_COLS], F32R)
        x_in, gens_sb, vec_rows, w_raw = early.x_in, early.gens, early.vec_rows, early.w_raw
        n2, y2 = early.n2, early.y2
        gw, gb, gcb = early.gw, early.gb, early.gcb
        y1 = sb("y1", [P, NT, E])
        u = sb("u", [P, NT, E])
        ln_buf = (sb("ln_stats", [P, NT // 2, 6])[:], sb("ln_mean_var", [P, NT // 2, 2])[:], sb("ln_small", [P, 5, NT // 2])[:],
                  sb("ln_pause", [P, 1])[:])
        xn = sb("xn", [P, T])
        xn_hi = sb("xn_hi", [P, T], F32R)
        xn_lo = sb("xn_lo", [P, T], F32R)
        gen = sb("gen", [P, NROT, P])
        gen_t = sb("gen_t", [P, NROT, P])
        gen2_t = sb("gen2_t", [P, NROT, P])
        series = sb("series", [P, NROT, P])
        e_sum = sb("e_sum", [P, NROT, P])
        e_turn = sb("e_turn", [P, NROT, P])
        e_last = sb("e_last", [P, P])
        half_eye = sb("half_eye", [P, P])
        eyes = sb("eyes", [P, 2, P], BF16)
        rot = sb("rot", [P, 2, P])
        rot_hi = sb("rot_hi", [P, P], F32R)
        rot_lo = sb("rot_lo", [P, P], F32R)
        vec_cols = sb("vec_cols", [P, N_VEC])
        g_col, b_col, ab2_col, gc_col = (vec_cols[:, a:b] for a, b in ((0, 1), (1, 2), (2, 3), (3, 5)))
        ab1_col, eb1_col = vec_cols[:, 5:5 + NA], vec_cols[:, 5 + NA:N_VEC]
        eb2_rows = sb("eb2_rows", [P, E])
        eb2_hi = sb("eb2_hi", [P, E], F32R)
        eb2_lo = sb("eb2_lo", [P, E], F32R)
        gc_wide = sb("gc_wide", [P, 2, P])
        gcb_half = sb("gcb_half", [P, 1])
        pick = sb("pick", [P, NX, P], F32R)
        logits = sb("logits", [P, NT, NX])
        before = sb("before", [P, NX, NX])
        gt = sb("gt", [P, NT // 2, NX, NX])
        eq = sb("eq", [P, NT // 2, NX, NX])
        rank = sb("rank", [P, NT // 2, NX])
        first = sb("first", [P, NT // 2, NX])
        second_first = sb("second_first", [P, NT // 2, NX])
        chosen = sb("chosen", [P, NT // 2, NX])
        gap = sb("gap", [P, NT])
        gap_t = sb("gap_t", [P, NT])
        mix_w = sb("mix_w", [P, NT // 2, NX])
        w_pad = sb("w_pad", [P, NT, 64])
        wt = sb("wt", [P, T], F32R)
        hid = sb("hid", [P, RING, CH])
        hid_hi = sb("hid_hi", [P, RING, CH], F32R)
        hid_lo = sb("hid_lo", [P, RING, CH], F32R)
        abel = sb("abel", [P, CH])
        moe_hi = sb("moe_hi", [P, CH], F32R)
        moe_lo = sb("moe_lo", [P, CH], F32R)
        nonabel = sb("nonabel", [P, CH])
        gate = sb("gate", [P, CH])
        delta = sb("delta", [P, CH])
        mixed = sb("mixed", [P, CH])
        last_sum = sb("last_sum", [P, TPC, E])

        ps = ctx.enter_context(nc.psum_tensor("ps_ffn", [P, 8, CH], F32))

        names = """l_eb2 c_k c_pick c_bef c_eye c_wt
            f_u f_gt f_b2 f_e f_sq f_sqt f_vec f_n f_log f_wt f_r
            f_h f_wb f_y f_ym f_rot f_gate f_out
            a_b a_gt a_b2t a_e a_t a_sq a_vec a_wh a_x a_wth a_r a_rh a_tanh a_eb
            a_g a_hh a_ab a_mh a_no a_th
            d_u d_ln d_xl d_log d_top d_wl d_gc d_hw d_ml d_mix d_v d_ln3 d_pad
            d_rl g_q g_m g_wl g_hl
            s_y""".split()
        S = {n: sem("ffn_" + n) for n in names}
        S.update(early.sems)
        block = ctx.enter_context(nc.Block())

        def tiles(h):
            return slice(h * NT // 2, (h + 1) * NT // 2)

        def half(h):
            return slice(HALF * h, HALF * (h + 1))

        def product(h):
            return ps[:, 6 + h, 0:HALF * P].rearrange("p (r j) -> p r j", r=HALF)

        def turn_bank(h):
            return ps[:, 6 + h, HALF * P:2 * HALF * P].rearrange("p (r j) -> p r j", r=HALF)

        @block.sync
        def _(sp):
            sp.wait_ge(S["c_k"], 1)
            for row in (0, 32):
                sp.dma_start(eb2_rows[row:row + NX, :], eb2).then_inc(S["l_eb2"], 16)
            o_v = out.rearrange("b (n p) e -> p (b n) e", p=P)
            for c in range(NC):
                sp.wait_ge(S["d_ln3"], ln_steps(TPC) * (c + 1))
                sp.dma_start(o_v[:, TPC * c:TPC * (c + 1), :], y2[:, TPC * c:TPC * (c + 1), :]).then_inc(S["s_y"], 16)
            sp.wait_ge(S["s_y"], 16 * NC)

        PART = W_COLS // W_PARTS

        @block.gpsimd
        def _(pool):
            pool.tensor_scalar(half_eye[:], ident[:], 0.5, None, ALU.mult).then_inc(S["c_eye"], 1)
            for n in range(2):
                pool.tensor_scalar(eyes[:, n, :], ident[:], n + 1.0, None, ALU.mult).then_inc(S["c_eye"], 1)

            pool.wait_ge(S["c_eye"], 1)
            pool.wait_ge(S["a_b"], 2)
            pool.tensor_tensor(series[:], series[:], half_eye[:].unsqueeze(1).to_broadcast([P, NROT, P]), ALU.add).then_inc(S["g_q"], 1)
            for h in range(2):
                hs = half(h)
                pool.wait_ge(S["g_q"], h + 1)
                pool.wait_ge(S["a_b2t"], 2 * (h + 1))
                pool.tensor_tensor(series[:, hs, :], series[:, hs, :], e_turn[:, hs, :], ALU.add).then_inc(S["g_q"], 1)
            pool.tensor_tensor(pick[:], ident[:, 0:NX].unsqueeze(2).to_broadcast([P, NX, P]),
                               ident[:, 32:32 + NX].unsqueeze(2).to_broadcast([P, NX, P]), ALU.add).then_inc(S["c_pick"], 1)
            pool.memset(before[:], 1.0).then_inc(S["c_bef"], 1)
            pool.wait_ge(S["c_bef"], 1)
            pool.affine_select(out=before[:], in_=before[:], compare_op=ALU.is_gt, fill=0.0, base=0,
                               pattern=[[1, NX], [-1, NX]], channel_multiplier=0).then_inc(S["c_bef"], 1)

            for k in range(W_PARTS):
                cols = slice(k * PART, (k + 1) * PART)
                pool.wait_ge(S["a_wh"], k + 1)
                pool.tensor_tensor(w_lo[:, cols], w_raw[:, cols], w_hi[:, cols], ALU.subtract).then_inc(S["g_wl"], 1)

            def section(c, first=False):
                for j in range(NB):
                    if first and j + 1 == min(PRODUCT_AT):
                        pool.wait_ge(S["a_sq"], 2 * SQUARINGS)
                        pool.tensor_tensor(e_last[:], e_sum[:, NROT - 1, :], ident[:], ALU.add).then_inc(S["g_m"], 1)
                    pool.wait_ge(S["a_hh"], c * NB + (j + 1))
                    wait(pool, S["f_y"], c * NB + (j - RING + 1))
                    r = j % RING
                    pool.tensor_tensor(hid_lo[:, r, :], hid[:, r, :], hid_hi[:, r, :], ALU.subtract).then_inc(S["g_hl"], 1)

            section(0, first=True)
            with pool.Fori(1, NC) as c:
                section(c)

        @block.scalar
        def _(act):
            scale = 2.0 ** -SQUARINGS
            act.wait_ge(S["l_gens"], 16)
            act.activation(gen[:], gens_sb, ACT.Copy, scale=scale).then_inc(S["a_b"], 1)
            act.activation(series[:], gens_sb, ACT.Copy, scale=scale / 6).then_inc(S["a_b"], 1)
            for h in range(2):
                act.wait_ge(S["f_gt"], h + 1)
                act.activation(gen_t[:, half(h), :], turn_bank(h), ACT.Copy, scale=scale).then_inc(S["a_gt"], 1)
            for h in range(2):
                act.wait_ge(S["f_b2"], h + 1)
                act.activation(gen2_t[:, half(h), :], turn_bank(h), ACT.Copy).then_inc(S["a_b2t"], 1)
                act.activation(e_turn[:, half(h), :], product(h), ACT.Copy, scale=1 / 24).then_inc(S["a_b2t"], 1)

            for h in range(2):
                act.wait_ge(S["f_e"], h + 1)
                act.activation(e_sum[:, half(h), :], product(h), ACT.Copy).then_inc(S["a_e"], 1)

            def turned(k):
                for h in range(2):
                    act.wait_ge(S["f_sqt"], 2 * k + h + 1)
                    act.activation(e_turn[:, half(h), :], turn_bank(h), ACT.Copy).then_inc(S["a_t"], 1)

            def squared(k):
                for h in range(2):
                    act.wait_ge(S["f_sq"], 2 * k + h + 1)
                    act.activation(e_sum[:, half(h), :], product(h), ACT.Copy).then_inc(S["a_sq"], 1)

            def to_features(c):
                cs = slice(c * CH, (c + 1) * CH)
                act.wait_ge(S["a_vec"], 1)
                act.wait_ge(S["f_n"], c + 1)
                src = ps[:, c if c < 2 else 7, :]
                act.activation(xn[:, cs], src, ACT.Identity, scale=g_col, bias=b_col).then_inc(S["a_x"], 1)
                act.activation(xn_hi[:, cs], src, ACT.Identity, scale=g_col, bias=b_col).then_inc(S["a_x"], 1)

            def gap_tanh(h):
                act.wait_ge(S["d_top"], CHOOSE * h + 9)
                act.activation(gap_t[:, tiles(h)], gap[:, tiles(h)], ACT.Tanh, scale=0.5).then_inc(S["a_tanh"], 1)

            def weights_high(c):
                act.wait_ge(S["f_wt"], c + 1)
                act.activation(wt[0:64, c * CH:(c + 1) * CH], ps[0:64, c if c < 2 else 7, :], ACT.Copy).then_inc(S["a_wth"], 1)

            def weight_high(part):
                cols = slice(part * PART, (part + 1) * PART)
                act.wait_ge(S["l_w"], 16 * 4)
                act.activation(w_hi[:, cols], w_raw[:, cols], ACT.Copy).then_inc(S["a_wh"], 1)

            weight_high(0)
            for k in range(EARLY):
                turned(k)
                squared(k)
                weight_high(k + 1)
                if k == 0:
                    act.wait_ge(S["f_vec"], 1)
                    act.activation(vec_cols[:], ps[:, 5, P:P + N_VEC], ACT.Copy).then_inc(S["a_vec"], 1)
                if k == EARLY_FEATURES:
                    to_features(0)
                    to_features(1)
            act.wait_ge(S["l_eb2"], 32)
            act.activation(eb2_hi[:], eb2_rows[:], ACT.Copy).then_inc(S["a_eb"], 1)
            gap_tanh(0)
            for c in range(2):
                weights_high(c)

            def high(c, j):
                r = j % RING
                wait(act, S["f_y"], c * NB + (j - RING + 1))
                if j < NA:
                    act.activation(hid_hi[:, r, :], ps[:, j % 2, :], ACT.Gelu, bias=ab1_col[:, j:j + 1]).then_inc(S["a_hh"], 1)
                else:
                    act.wait_ge(S["d_hw"], c * (NB - NA) + (j - NA + 1))
                    act.activation(hid_hi[:, r, :], hid[:, r, :], ACT.Copy).then_inc(S["a_hh"], 1)

            def section(c, cur, prev, first=False, second=False):
                for j in range(NB):
                    if cur:
                        bias = ab1_col[:, j:j + 1] if j < NA else eb1_col[:, j - NA:j - NA + 1]
                        act.wait_ge(S["f_h"], c * NB + (j + 1))
                        wait(act, S["g_hl"], c * NB + (j - RING + 1))
                        act.activation(hid[:, j % RING, :], ps[:, j % 2, :], ACT.Gelu, bias=bias).then_inc(S["a_g"], 1)
                        if j < NA:
                            high(c, j)
                        elif j > NA:
                            high(c, j - 1)
                    if second and j in FEATURES_AT:
                        to_features(FEATURES_AT[j])
                    if second and j == CHOOSE_AT + 3:
                        gap_tanh(1)
                    if second and j in WEIGHTS_AT:
                        weights_high(WEIGHTS_AT[j])
                    if first and j in TURN_AT:
                        turned(TURN_AT[j])
                    if first and j in SQUARE_AT:
                        squared(SQUARE_AT[j])
                    if first and j in PRODUCT_AT:
                        k = PRODUCT_AT[j]
                        act.wait_ge(S["f_r"], k + 1)
                        if k < HALF:
                            act.activation(rot[:, k, :], product(0)[:, 0, :], ACT.Copy).then_inc(S["a_r"], 1)
                        else:
                            act.activation(rot_hi[:], product(0)[:, 0, :], ACT.Copy).then_inc(S["a_rh"], 1)
                    if prev and j == T_ABEL:
                        act.wait_ge(S["f_y"], (c - 1) * NB + NA)
                        wait(act, S["d_mix"], (c - 1) * 3)
                        act.activation(abel[:], ps[:, 4, :], ACT.Identity, bias=ab2_col).then_inc(S["a_ab"], 1)
                    if prev and j == T_SPLIT:
                        act.wait_ge(S["f_ym"], c)
                        wait(act, S["f_rot"], c - 1)
                        act.activation(moe_hi[:], ps[:, 5, :], ACT.Copy).then_inc(S["a_mh"], 1)
                    if prev and j == T_NONABEL:
                        act.wait_ge(S["f_rot"], c)
                        wait(act, S["f_gate"], c - 1)
                        wait(act, S["d_mix"], (c - 1) * 3)
                        act.activation(nonabel[:], ps[:, 6, :], ACT.Copy).then_inc(S["a_no"], 1)
                    if prev and j == T_TANH:
                        act.wait_ge(S["f_gate"], c)
                        wait(act, S["d_mix"], (c - 1) * 3)
                        act.activation(gate[:], ps[:, 7, :], ACT.Tanh, scale=0.5, bias=gcb_half[:]).then_inc(S["a_th"], 1)
                if cur:
                    high(c, NB - 1)

            act.wait_ge(S["d_gc"], 2)
            section(0, True, False, first=True)
            section(1, True, True, second=True)
            with act.Fori(2, NC) as c:
                section(c, True, True)
            section(NC, False, True)

        @block.vector
        def _(dve):
            dve.memset(eb2_rows[:], 0.0).then_inc(S["c_k"], 1)
            dve.memset(wt[64:P, :].bitcast(F32), 0.0).then_inc(S["c_wt"], 1)
            def residual(c):
                dve.wait_ge(S["f_u"], c + 1)
                dve.tensor_tensor(u[:, TPC * c:TPC * (c + 1), :], ps[:, c, :].rearrange("p (t e) -> p t e", e=E),
                                  x_in[:, TPC * c:TPC * (c + 1), :], ALU.add).then_inc(S["d_u"], 1)

            def norms(h):
                n = NT // 2
                dve.wait_ge(S["d_u"], 2 * h + 2)
                yield from layer_norm(dve, S["d_ln"], 2 * h * ln_steps(n), u[:, tiles(h), :], y1[:, tiles(h), :], ln_buf, n)
                yield from layer_norm(dve, S["d_ln"], (2 * h + 1) * ln_steps(n), y1[:, tiles(h), :], n2[:, tiles(h), :], ln_buf, n)

            def input_low(c):
                cs = slice(c * CH, (c + 1) * CH)
                dve.wait_ge(S["a_x"], 2 * (c + 1))
                dve.tensor_tensor(xn_lo[:, cs], xn[:, cs], xn_hi[:, cs], ALU.subtract).then_inc(S["d_xl"], 1)

            def add_gate_bias(h):
                n = NT // 2
                dve.wait_ge(S["f_log"], 2 * h + 2)
                dve.tensor_tensor(logits[:, tiles(h), :],
                                  ps[:, LOGIT_BANK[h], h * n * NX:(h + 1) * n * NX].rearrange("p (t e) -> p t e", e=NX),
                                  gb.unsqueeze(1).to_broadcast([P, n, NX]), ALU.add).then_inc(S["d_log"], 1)

            def choose(h):
                n, ts, base = NT // 2, tiles(h), CHOOSE * h
                full, part = [P, n, NX, NX], [P, n, NX]
                values = logits[:, ts, :]
                other, own = values.unsqueeze(2).to_broadcast(full), values.unsqueeze(3).to_broadcast(full)
                dve.wait_ge(S["d_log"], h + 1)
                if h:
                    dve.wait_ge(S["d_top"], base)
                dve.tensor_tensor(gt[:], other, own, ALU.is_gt).then_inc(S["d_top"], 1)
                yield
                dve.tensor_tensor(eq[:], other, own, ALU.is_equal).then_inc(S["d_top"], 1)
                yield
                dve.wait_ge(S["d_top"], base + 2)
                dve.tensor_tensor(eq[:], eq[:], before[:].unsqueeze(1).to_broadcast(full), ALU.mult).then_inc(S["d_top"], 1)
                yield
                dve.wait_ge(S["d_top"], base + 3)
                dve.tensor_tensor(gt[:], gt[:], eq[:], ALU.add).then_inc(S["d_top"], 1)
                yield
                dve.wait_ge(S["d_top"], base + 4)
                dve.tensor_reduce(rank[:], gt[:], AX.X, ALU.add).then_inc(S["d_top"], 1)
                yield
                dve.wait_ge(S["d_top"], base + 5)
                dve.tensor_scalar(first[:], rank[:], 0.0, None, ALU.is_equal).then_inc(S["d_top"], 1)
                yield
                dve.wait_ge(S["d_top"], base + 6)
                dve.scalar_tensor_tensor(second_first[:], rank[:], 1.0, first[:], ALU.is_equal, ALU.subtract).then_inc(S["d_top"], 1)
                yield
                dve.wait_ge(S["d_top"], base + 7)
                dve.scalar_tensor_tensor(chosen[:], second_first[:], -1.0, values, ALU.mult, ALU.mult).then_inc(S["d_top"], 1)
                yield
                dve.wait_ge(S["d_top"], base + 8)
                dve.tensor_reduce(gap[:, ts], chosen[:], AX.X, ALU.add).then_inc(S["d_top"], 1)
                yield
                dve.wait_ge(S["a_tanh"], h + 1)
                dve.tensor_tensor(mix_w[:], second_first[:], gap_t[:, ts].unsqueeze(2).to_broadcast(part), ALU.mult).then_inc(S["d_top"], 1)
                yield
                dve.tensor_scalar(chosen[:], rank[:], 1.5, None, ALU.is_lt).then_inc(S["d_top"], 1)
                yield
                dve.wait_ge(S["d_top"], base + 11)
                dve.tensor_tensor(mix_w[:], chosen[:], mix_w[:], ALU.subtract).then_inc(S["d_top"], 1)
                yield
                dve.wait_ge(S["d_top"], base + 12)
                for col in (0, 32):
                    dve.tensor_scalar(w_pad[:, ts, col:col + NX], mix_w[:], 0.5, None, ALU.mult).then_inc(S["d_pad"], 1)
                yield

            def weights_low(c):
                cs = slice(c * CH, (c + 1) * CH)
                dve.wait_ge(S["a_wth"], c + 1)
                dve.tensor_tensor(wt[32:64, cs], ps[32:64, c if c < 2 else 7, :], wt[32:64, cs], ALU.subtract).then_inc(S["d_wl"], 1)

            dve.wait_ge(S["l_x"], 16)
            residual(0)
            residual(1)
            for _ in norms(0):
                pass
            residual(2)
            residual(3)
            dve.memset(w_pad[:], 0.0).then_inc(S["d_pad"], 1)
            dve.wait_ge(S["l_small"], 16 * N_SMALL)
            add_gate_bias(0)
            dve.wait_ge(S["c_bef"], 2)
            dve.wait_ge(S["d_pad"], 1)
            for _ in choose(0):
                pass
            input_low(0)
            input_low(1)
            dve.tensor_scalar(gcb_half[:], gcb, 0.5, None, ALU.mult).then_inc(S["d_gc"], 1)
            dve.wait_ge(S["a_vec"], 1)
            dve.tensor_copy(gc_wide[:], gc_col.unsqueeze(2).to_broadcast([P, 2, P])).then_inc(S["d_gc"], 1)
            dve.wait_ge(S["a_eb"], 1)
            dve.tensor_tensor(eb2_lo[:], eb2_rows[:], eb2_hi[:], ALU.subtract).then_inc(S["d_wl"], 1)
            for c in range(2):
                weights_low(c)

            def section(c, cur, prev, first=False, second=False):
                rest, choice = norms(1), choose(1)
                for j in range(NB):
                    if second and j in LOW_AT:
                        input_low(LOW_AT[j])
                    if second and j == CHOOSE_AT:
                        add_gate_bias(1)
                    if second and 0 <= j - CHOOSE_AT < len(CHOOSE_STEPS):
                        for _ in range(CHOOSE_STEPS[j - CHOOSE_AT]):
                            next(choice, None)
                    if second and j in WEIGHTS_LOW_AT:
                        weights_low(WEIGHTS_LOW_AT[j])
                    if first and j == max(PRODUCT_AT) + 2:
                        dve.wait_ge(S["a_rh"], 1)
                        dve.tensor_tensor(rot_lo[:], product(0)[:, 0, :], rot_hi[:], ALU.subtract).then_inc(S["d_rl"], 1)
                    for _ in range(5 if first else 0):
                        next(rest, None)
                    if cur and j >= NA:
                        n = j - NA
                        dve.wait_ge(S["a_g"], c * NB + (j + 1))
                        dve.wait_ge(S["f_wb"], c * NX + (n // NXB + 1))
                        dve.tensor_tensor(hid[:, j % RING, :], hid[:, j % RING, :], ps[:, 2 + n // NXB % 2, :], ALU.mult).then_inc(S["d_hw"], 1)
                    if prev and j == T_SPLIT:
                        dve.wait_ge(S["a_mh"], c)
                        dve.tensor_tensor(moe_lo[:], ps[:, 5, :], moe_hi[:], ALU.subtract).then_inc(S["d_ml"], 1)
                    if prev and j == T_MIX:
                        base = (c - 1) * 3
                        dve.wait_ge(S["a_no"], c)
                        dve.wait_ge(S["a_ab"], c)
                        wait(dve, S["d_mix"], base)
                        dve.tensor_tensor(delta[:], nonabel[:], abel[:], ALU.subtract).then_inc(S["d_mix"], 1)
                        dve.wait_ge(S["a_th"], c)
                        dve.wait_ge(S["d_mix"], base + 1)
                        dve.scalar_tensor_tensor(delta[:], gate[:], 1.0, delta[:], ALU.add, ALU.mult).then_inc(S["d_mix"], 1)
                        dve.wait_ge(S["d_mix"], base + 2)
                        wait(dve, S["f_out"], c - 1)
                        dve.scalar_tensor_tensor(mixed[:], delta[:], 0.5, abel[:], ALU.mult, ALU.add).then_inc(S["d_mix"], 1)
                    if prev and j == T_NORM:
                        dve.wait_ge(S["f_out"], c)
                        ts = bass.ds((c - 1) * TPC, TPC)
                        wait(dve, S["d_ln3"], ln_steps(TPC) * (c - 1))
                        dve.scalar_tensor_tensor(last_sum[:], y1[:, ts, :], 2.0, ps[:, 6, :].rearrange("p (t e) -> p t e", e=E),
                                                 ALU.mult, ALU.add).then_inc(S["d_v"], 1)
                        dve.wait_ge(S["d_v"], c)
                        norm = layer_norm(dve, S["d_ln3"], ln_steps(TPC) * (c - 1), last_sum[:], y2[:, ts, :], ln_buf, TPC)
                    if prev and j >= T_NORM:
                        for _ in range(NORM_STEPS[j - T_NORM]):
                            next(norm)

            section(0, True, False, first=True)
            section(1, True, True, second=True)
            with dve.Fori(2, NC) as c:
                section(c, True, True)
            section(NC, False, True)

        @block.tensor
        def _(pe):
            for c in range(NC):
                for t in range(TPC):
                    last = pe.transpose(ps[:, c, t * P:(t + 1) * P], acc[:, (c * TPC + t) * P:(c * TPC + t + 1) * P], ident[:])
                last.then_inc(S["f_u"], 1)
            pe.wait_ge(S["l_gens"], 16)

            def turn(src, h, signal):
                for i in range(HALF):
                    last = pe.transpose(turn_bank(h)[:, i, :], src[:, HALF * h + i, :], ident[:])
                last.then_inc(S[signal], 1)

            def multiply(into, left_t, right, h):
                for i in range(HALF):
                    last = pe.matmul(into[:, i, :], left_t[:, HALF * h + i, :], right[:, HALF * h + i, :], start=True, stop=True)
                return last

            for h in range(2):
                turn(gens_sb, h, "f_gt")
            for h in range(2):
                pe.wait_ge(S["a_b"], 1)
                pe.wait_ge(S["a_gt"], h + 1)
                multiply(product(h), gen_t, gen, h)
                multiply(turn_bank(h), gen, gen_t, h).then_inc(S["f_b2"], 1)
            for h in range(2):
                pe.wait_ge(S["g_q"], h + 2)
                for i in range(HALF):
                    r = HALF * h + i
                    pe.matmul(product(h)[:, i, :], gen2_t[:, r, :], series[:, r, :], start=True, stop=False)
                    last = pe.matmul(product(h)[:, i, :], gen_t[:, r, :], ident[:], start=False, stop=True)
                last.then_inc(S["f_e"], 1)

            def turn_e(k):
                for h in range(2):
                    if k == 0:
                        pe.wait_ge(S["a_e"], h + 1)
                    else:
                        pe.wait_ge(S["a_sq"], 2 * (k - 1) + h + 1)
                    for i in range(HALF):
                        pe.matmul(turn_bank(h)[:, i, :], e_sum[:, HALF * h + i, :], ident[:], start=True, stop=False)
                        last = pe.matmul(turn_bank(h)[:, i, :], eyes[:, 0, :], eyes[:, 0 if k == SQUARINGS else 1, :],
                                         start=False, stop=True)
                    last.then_inc(S["f_sqt"], 1)

            def square(k):
                for h in range(2):
                    pe.wait_ge(S["a_t"], 2 * k + h + 1)
                    multiply(product(h), e_turn, e_sum, h).then_inc(S["f_sq"], 1)

            def to_features(c):
                pe.wait_ge(S["d_ln"], 2 * ln_steps(NT // 2) * (c // 2 + 1))
                bank = c if c < 2 else 7
                if c == 2:
                    pe.wait_ge(S["f_r"], 3)
                if c == 3:
                    pe.wait_ge(S["a_x"], 2 * c)
                for t in range(TPC):
                    last = pe.transpose(ps[:, bank, t * P:(t + 1) * P], n2[:, c * TPC + t, :], ident[:])
                last.then_inc(S["f_n"], 1)

            def gate_logits(c):
                pe.wait_ge(S["a_x"], 2 * c + 1 if c < 2 else 2 * NC)
                for t in range(c * TPC, (c + 1) * TPC):
                    last = pe.matmul(ps[:, LOGIT_BANK[c // 2], t * NX:(t + 1) * NX], xn[:, t * P:(t + 1) * P], gw, start=True, stop=True)
                last.then_inc(S["f_log"], 1)

            pe.wait_ge(S["c_eye"], 3)
            for k in range(EARLY):
                turn_e(k)
                square(k)
                if k == 0:
                    pe.wait_ge(S["l_small"], 16 * N_SMALL)
                    pe.transpose(ps[:, 5, P:P + N_VEC], vec_rows, ident[0:N_VEC, 0:N_VEC]).then_inc(S["f_vec"], 1)
                if k == EARLY_FEATURES:
                    to_features(0)
                    to_features(1)
                if k == EARLY_FEATURES + 1:
                    gate_logits(0)
                    gate_logits(1)

            def weights_turned(c):
                bank = c if c < 2 else 7
                pe.wait_ge(S["d_pad"], 3 if c < 2 else 5)
                if c == 0:
                    pe.wait_ge(S["a_x"], 4)
                if c == 2:
                    pe.wait_ge(S["a_th"], 1)
                if c == 3:
                    pe.wait_ge(S["d_wl"], 1 + c)
                for t in range(TPC):
                    last = pe.transpose(ps[0:64, bank, t * P:(t + 1) * P], w_pad[:, c * TPC + t, :], ident[:])
                last.then_inc(S["f_wt"], 1)

            for c in range(2):
                weights_turned(c)

            def chunk(a, c):
                return a[:, bass.ds(c * CH, CH)]

            def layer2(c, j):
                into = ps[:, 4 if j < NA else 5, :]
                pe.wait_ge(S["g_hl"], c * NB + (j + 1))
                if j == 0:
                    wait(pe, S["a_ab"], c)
                if j == NA:
                    wait(pe, S["d_ml"], c)
                w = slice(LAYER2[j], LAYER2[j] + P)
                r = j % RING
                end = j in (NA - 1, NB - 1)
                for k, (a, h) in enumerate(((w_hi, hid_hi), (w_lo, hid_hi), (w_hi, hid_lo))):
                    last = pe.matmul(into, a[:, w], h[:, r, :], start=(k == 0 and j in (0, NA)), stop=(end and k == 2 and j < NA))
                last.then_inc(S["f_y"], 1)

            def section(c, cur, prev, first=False, second=False):
                for j in range(NB):
                    if cur:
                        wait(pe, S["a_hh"] if j in range(2, NA + 2) else S["a_g"], c * NB + (j - 1))
                        w = slice(LAYER1[j], LAYER1[j] + P)
                        for k, (a, h) in enumerate(((w_hi, xn_hi), (w_lo, xn_hi), (w_hi, xn_lo))):
                            last = pe.matmul(ps[:, j % 2, :], a[:, w], chunk(h, c), start=(k == 0), stop=(k == 2))
                        last.then_inc(S["f_h"], 1)
                        if j >= NA and (j - NA) % NXB == 0:
                            e = (j - NA) // NXB
                            wait(pe, S["d_hw"], c * (NB - NA) + NXB * (e - 1))
                            pe.matmul(ps[:, 2 + e % 2, :], pick[:, e, :], chunk(wt, c), start=True, stop=True).then_inc(S["f_wb"], 1)
                    if cur and j >= LAG:
                        layer2(c, j - LAG)
                    if second and j in FEATURES_AT:
                        to_features(FEATURES_AT[j])
                    if second and j == LOGITS_AT:
                        gate_logits(2)
                        gate_logits(3)
                    if second and j in WEIGHTS_AT:
                        weights_turned(WEIGHTS_AT[j])
                    if first and j in TURN_AT:
                        turn_e(TURN_AT[j])
                    if first and j in SQUARE_AT:
                        square(SQUARE_AT[j])
                    if first and j in PRODUCT_AT:
                        k = PRODUCT_AT[j]
                        if k == 0:
                            pe.wait_ge(S["g_m"], 1)
                            pe.wait_ge(S["a_t"], 2 * (SQUARINGS + 1))
                        else:
                            pe.wait_ge(S["a_r"], k)
                        pe.matmul(product(0)[:, 0, :], e_turn[:, NROT - 2 - k, :], rot[:, k - 1, :] if k else e_last[:],
                                  start=True, stop=True).then_inc(S["f_r"], 1)
                    if prev and j < LAG:
                        layer2(c - 1, NB - LAG + j)
                        if j == LAG - 1:
                            pe.matmul(ps[:, 5, :], eb2_hi[:], chunk(wt, c - 1), start=False, stop=False)
                            pe.matmul(ps[:, 5, :], eb2_lo[:], chunk(wt, c - 1), start=False, stop=True).then_inc(S["f_ym"], 1)
                    if prev and j == T_ROTATE:
                        pe.wait_ge(S["d_rl"], 1)
                        pe.wait_ge(S["d_ml"], c)
                        wait(pe, S["d_v"], c - 1)
                        for k, (a, m) in enumerate(((rot_hi, moe_hi), (rot_lo, moe_hi), (rot_hi, moe_lo))):
                            last = pe.matmul(ps[:, 6, :], a[:], m[:], start=(k == 0), stop=(k == 2))
                        last.then_inc(S["f_rot"], 1)
                    if prev and j == T_GATE:
                        pe.wait_ge(S["a_no"], c)
                        pe.wait_ge(S["a_ab"], c)
                        pe.wait_ge(S["d_log"], 2)
                        wait(pe, S["a_th"], c - 1)
                        pe.matmul(ps[:, 7, :], gc_wide[:, 0, :], abel[:], start=True, stop=False)
                        pe.matmul(ps[:, 7, :], gc_wide[:, 1, :], nonabel[:], start=False, stop=True).then_inc(S["f_gate"], 1)
                    if prev and j == T_TURN:
                        pe.wait_ge(S["d_mix"], 3 * c)
                        for t in range(TPC):
                            last = pe.transpose(ps[:, 6, t * P:(t + 1) * P], mixed[:, t * P:(t + 1) * P], ident[:])
                        last.then_inc(S["f_out"], 1)

            pe.wait_ge(S["d_wl"], 1 + 2)
            pe.wait_ge(S["d_u"], NC)
            pe.wait_ge(S["d_xl"], 2)
            pe.wait_ge(S["g_wl"], W_PARTS)
            pe.wait_ge(S["d_log"], 1)
            pe.wait_ge(S["c_pick"], 1)
            pe.wait_ge(S["c_wt"], 1)
            section(0, True, False, first=True)
            section(1, True, True, second=True)
            pe.wait_ge(S["d_wl"], 1 + NC)
            pe.wait_ge(S["d_xl"], NC)
            with pe.Fori(2, NC) as c:
                section(c, True, True)
            section(NC, False, True)


def transformer_block(nc, x, w_qkv, w_o, ln_g, ln_b, aw1, ab1, aw2, ab2, gate_w, gate_b, ew1, eb1, ew2, eb2,
                      gens, gc_w, gc_b, pe2, out):
    ffn_arrays = (x, ln_g, ln_b, aw1, ab1, aw2, ab2, gate_w, gate_b, ew1, eb1, ew2, eb2, gens, gc_w, gc_b)
    with ExitStack() as ctx:
        def sb(name, shape):
            return ctx.enter_context(nc.sbuf_tensor(name, shape, F32))

        acc = sb("acc", [P, T])
        ident = sb("ident", [P, P])
        pos = sb("pos", [P, T])
        qk = sb("qk", [P, 2, CH])
        v_all = sb("v_all", [P, H, NT, D])
        loaded = {name: ctx.enter_context(nc.semaphore(name)) for name in ("l_x", "l_gens", "l_small", "l_w")}
        early = Early(pos, qk, v_all, loaded)
        attention(nc, acc, ident, pos, qk, v_all, x, w_qkv, w_o, pe2, lambda sp: early.load(sp, *ffn_arrays))
        feed_forward(nc, early, acc, ident, eb2, out)


_INS = ["L0_attn_x", "L0_attn_Wqkv", "L0_attn_Wo", "L0_ffn_ln_g", "L0_ffn_ln_b", "L0_ffn_aw1", "L0_ffn_ab1",
        "L0_ffn_aw2", "L0_ffn_ab2", "L0_ffn_gate_w", "L0_ffn_gate_b", "L0_ffn_ew1", "L0_ffn_eb1", "L0_ffn_ew2",
        "L0_ffn_eb2", "L0_ffn_gens", "L0_ffn_gc_w", "L0_ffn_gc_b"]


def position_table():
    import numpy as np

    pos = np.arange(T, dtype=np.float32)[:, None]
    div = np.exp(np.arange(0, D, 2, dtype=np.float32) * np.float32(-np.log(10000.0) / D))
    angle = pos * div
    table = np.stack([np.sin(angle), np.cos(angle)], axis=-1).reshape(T, D).astype(np.float32)
    return np.ascontiguousarray(np.concatenate([table.T, table.T], axis=0))


def kernel(**inputs):
    import concourse.bacc as bacc
    import numpy as np
    from concourse.bass_utils import run_bass_kernel_spmd

    nc = bacc.Bacc("TRN2", target_bir_lowering=False, num_devices=1)
    arrays = {name: np.ascontiguousarray(inputs[name]) for name in _INS}
    arrays["positions"] = position_table()
    args = [nc.dram_tensor(name, a.shape, F32, kind="ExternalInput").ap() for name, a in arrays.items()]
    args.append(nc.dram_tensor("out", (1, T, E), F32, kind="ExternalOutput").ap())
    transformer_block(nc, *args)
    result = run_bass_kernel_spmd(nc, [arrays], core_ids=[0])
    return result.results[0]["out"]
```

```python
from contextlib import ExitStack

import concourse.bass as bass
from concourse import mybir

F32 = mybir.dt.float32
F32R = mybir.dt.float32r
BF16 = mybir.dt.bfloat16
I32 = mybir.dt.int32
ALU = mybir.AluOpType
ACT = mybir.ActivationFunctionType
AX = mybir.AxisListType

P = 128
T = 2048
E = 128
H = 8
D = 64
CH = 512
NC = T // CH
NT = T // P
TPC = CH // P
NEG = -1e30
LEAD = 22

PAIRS = [2 * (c + 1) for c in range(NC)]
PAIR0 = [sum(PAIRS[:c]) for c in range(NC + 1)]
NP = PAIR0[NC]
UNIT0 = [sum(TPC * (b + 1) for b in range(c)) for c in range(NC + 1)]
NU = UNIT0[NC]

EPS = 1e-5

NA = 4
NX = 6
NXB = 2
NB = NA + NX * NXB
N_SMALL = 9
N_VEC = 5 + NB
NROT = 4
SQUARINGS = 10
HALF = NROT // 2
EARLY = 5
CHOOSE = 12
CHOOSE_TANH = 9
LOGIT_BANK = (5, 7)
EARLY_FEATURES = 3
LAG = 3
RING = 4
NORM_STEPS = (3, 5, 5, 12)

LAYER1 = [P * j if j < NA else 2 * NA * P + P * (j - NA) for j in range(NB)]
LAYER2 = [NA * P + P * j if j < NA else 2 * NA * P + NX * NXB * P + P * (j - NA) for j in range(NB)]
W_COLS = 2 * NB * P
W_PARTS = 8

TURN_AT = {1: 5, 3: 6, 5: 7, 7: 8, 9: 9, 11: 10}
SQUARE_AT = {2: 5, 4: 6, 6: 7, 8: 8, 10: 9}
PRODUCT_AT = {12: 0, 13: 1, 14: 2}
FIRST_TANH_AT = 1
FIRST_WEIGHTS_AT = 3
FEATURES_AT = {0: 2, 2: 3}
LOW_AT = {1: 2, 3: 3}
LOGITS_AT, CHOOSE_AT = 4, 5
CHOOSE_STEPS = (5, 4, 0, 4)
WEIGHTS_AT = {10: 2, 12: 3}
WEIGHTS_LOW_AT = {11: 2, 13: 3}
T_ABEL, T_SPLIT, T_ROTATE, T_NONABEL, T_GATE, T_TANH, T_MIX, T_TURN, T_NORM = 1, 3, 5, 6, 7, 8, 9, 11, 12


def ln_steps(n):
    return 3 * n + 13


def chunk_of(starts, n):
    return max(c for c in range(NC) if starts[c] <= n)


def at(g, per, local):
    i, offset = g
    return i * (2 * per) + (offset * per + local)


def plus(g, n):
    return (g[0], g[1] + n)


def index(g):
    return g[0] * 2 + g[1]


def wait(eng, sem, value):
    if not isinstance(value, int) or value > 0:
        eng.wait_ge(sem, value)


PROJECT = {4: (0, 1), 7: (1, 1), 10: (2, 1), 17: (3, 1)}
TURN = {1: (2, 0), 9: (3, 0), 11: (0, 1), 15: (1, 1)}
OUTPUT = {6: (3, -1), 12: (0, 0), 14: (1, 0), 19: (2, 0)}


def due(table, p, after, cur, nxt, prev):
    for slot, (c, ahead) in table.items():
        if (slot + after) % NP == p:
            ahead -= (slot + after) // NP
            if (nxt if ahead > 0 else prev if ahead < 0 else cur):
                return [(c, ahead)]
    return []


V_LOW = (16, 18)

DONE = {PAIR0[c + 1] + 2: (c, 0) for c in range(NC)}


def attention(nc, acc, ident, pos, qk, v_all, x, w_qkv, w_o, pe2, load_early):
    with ExitStack() as ctx:
        def sb(name, shape, dt=F32):
            return ctx.enter_context(nc.sbuf_tensor(name, shape, dt))

        def psum(name, shape, dt=F32):
            return ctx.enter_context(nc.psum_tensor(name, shape, dt))

        def sem(name):
            return ctx.enter_context(nc.semaphore(name))

        xh = sb("xh", [P, T], F32R)
        xl = sb("xl", [P, T], F32R)
        wth = sb("wth", [P, H, 2, D], F32R)
        wtl = sb("wtl", [P, H, 2, D], F32R)
        woh = sb("woh", [P, H, E], F32R)
        wol = sb("wol", [P, H, E], F32R)
        w_head = sb("w_head", [P, 2, P], F32R)
        wo_head = sb("wo_head", [P, 2, 2, E], F32R)
        v1 = sb("v1", [P, 2, NT, 2 * D], F32R)
        v2 = sb("v2", [P, 2, NT, D], F32R)
        q1 = sb("q1", [P, T], F32R)
        q2 = sb("q2", [P, T], F32R)
        k1 = sb("k1", [P, 2, T], F32R)
        k2 = sb("k2", [P, 2, T], F32R)
        probs = sb("probs", [P, 2, 2, CH])
        probs_h = sb("probs_h", [P, 4, 2, CH], F32R)
        probs_l = sb("probs_l", [P, 2, 2, CH], F32R)
        oh = sb("oh", [P, 2, CH], F32R)
        o_sum = sb("o_sum", [P, CH])
        l_both = sb("l_both", [P, CH])
        l_rows, l_cols = l_both[0:D, :], l_both[D:P, :]
        l_inv = sb("l_inv", [P, CH // 32])
        o_norm = sb("o_norm", [D, 2, CH])
        m_part = sb("m_part", [P, TPC, NC])
        m_max = sb("m_max", [P, 2, TPC])
        m_row = sb("m_row", [TPC, P], F32R)
        ident_b = sb("ident_b", [P, P], BF16)
        mask_kq = sb("mask_kq", [P, 2 * P], BF16)
        mask_qk = sb("mask_qk", [P, P], BF16)
        wvh, wvl = k1[:, 1, 0:CH], k1[:, 1, CH:2 * CH]
        x_tok = probs[:].rearrange("p b j q -> p (b j q)").rearrange("p (n e) -> p n e", e=E)
        wq_raw = acc[:, 0:12 * P].rearrange("p (n e) -> p n e", n=12)
        wo_raw = v_all[:, 0, :, :].rearrange("p t d -> p (t d)").rearrange("p (h r d) -> p h r d", h=H, r=2)

        scores = psum("scores", [P, 2, 2, CH])
        o_ps = psum("o_ps", [P, CH])
        max_ps = psum("max_ps", [P, 2, CH])
        side_ps = psum("side_ps", [P, CH])

        names = """loaded_w_qkv loaded_w_o loaded_x loaded_positions identity_made masks_made ones_beside_v_made
            rows_beside_qk_made sum_cleared setup_turned setup_high_ready setup_low_ready v_projected
            v_copied qk_projected max_scores_ready maxima_turned output_projected scores_ready pv_done
            probs_ready probs_high_ready k_high_ready q_high_ready q_high_doubled head_weights_ready
            head_wo_ready v_high_ready head_out_high_ready head_out_taken probs_low_ready qk_positioned
            q_low_ready k_low_ready tile_max_ready row_max_ready max_row_ready sums_turned sums_inverted
            inverse_spread inverse_turned head_out_normalised head_out_low_ready output_added v_low_ready
            max_row_moved""".split()
        S = {n: sem(n) for n in names}
        block = ctx.enter_context(nc.Block())

        def units(p, cur, nxt):
            for n in (2 * p + LEAD, 2 * p + LEAD + 1):
                if n < NU and cur:
                    yield 0, n
                if n >= NU and nxt:
                    yield 1, n - NU

        def unit_place(u):
            c = chunk_of(UNIT0, u)
            r, j = divmod(u - UNIT0[c], c + 1)
            return c, r, j, (CH if j < c else P * (r + 1))

        def group(n, hi):
            if n < 3:
                if n == 2:
                    return wvh if hi else wvl
                return (wth if hi else wtl)[:, 4 * n:4 * (n + 1), :, :].rearrange("p h s d -> p (h s d)")
            if n < 7:
                return (xh if hi else xl)[:, (n - 3) * CH:(n - 2) * CH]
            return (woh if hi else wol)[:, 4 * (n - 7):4 * (n - 6), :].rearrange("p h e -> p (h e)")

        GROUPS = 3 + 4 + 2

        @block.sync
        def _(sp):
            w_rows = w_qkv.rearrange("(h s d) e -> s d h e", h=H, s=3)
            for s in range(2):
                sp.dma_start(wq_raw[s * D:(s + 1) * D, 0:H, :], w_rows[s]).then_inc(S["loaded_w_qkv"], 16)
            v_rows = w_rows[2].rearrange("d (n r) e -> r d n e", r=2)
            for r in range(2):
                sp.dma_start(wq_raw[r * D:(r + 1) * D, H:H + H // 2, :], v_rows[r]).then_inc(S["loaded_w_qkv"], 16)
            sp.dma_start(x_tok, x.rearrange("b (n p) e -> p (b n) e", p=P)).then_inc(S["loaded_x"], 16)
            for r in range(2):
                sp.dma_start(wo_raw[:, :, r, :], w_o.rearrange("e (h d) -> e h d", d=D)).then_inc(S["loaded_w_o"], 16)
            sp.dma_start(pos[:], pe2).then_inc(S["loaded_positions"], 16)

            def section(g, cur, nxt):
                for p in range(NP):
                    for c, ahead in due(TURN, p, 0, cur, nxt, False):
                        h = plus(g, ahead)
                        wait(sp, S["max_row_ready"], at(h, NC, c + 1))
                        sp.dma_start(q2[D:D + 1, c * CH:(c + 1) * CH].bitcast(F32), m_row[:].bitcast(F32)).then_inc(S["max_row_moved"], 16)

            sp.wait_ge(S["rows_beside_qk_made"], 3)
            section((0, -1), False, True)
            section((0, 0), True, True)
            with sp.Fori(0, (H - 2) // 2) as i:
                for o in (1, 2):
                    section((i, o), True, True)
            section((0, H - 1), True, False)
            for signal, per_head in (("qk_positioned", NC), ("q_low_ready", NC), ("k_low_ready", NC), ("q_high_doubled", NC), ("k_high_ready", 2 * NC), ("v_low_ready", 2)):
                sp.wait_ge(S[signal], H * per_head)
            load_early(sp)

        @block.gpsimd
        def _(pool):
            pool.memset(ident[:], 0.0).then_inc(S["identity_made"], 1)
            pool.wait_ge(S["identity_made"], 1)
            pool.affine_select(out=ident[:], in_=ident[:], compare_op=ALU.not_equal, fill=1.0, base=0,
                               pattern=[[-1, P]], channel_multiplier=1).then_inc(S["identity_made"], 1)
            pool.memset(ident_b[:], 0.0).then_inc(S["masks_made"], 1)
            pool.memset(mask_kq[:], 0.0).then_inc(S["masks_made"], 1)
            pool.memset(mask_qk[:], 0.0).then_inc(S["masks_made"], 1)
            pool.wait_ge(S["masks_made"], 3)
            pool.affine_select(out=ident_b[:], in_=ident_b[:], compare_op=ALU.not_equal, fill=1.0, base=0,
                               pattern=[[-1, P]], channel_multiplier=1).then_inc(S["masks_made"], 1)
            pool.affine_select(out=mask_kq[:], in_=mask_kq[:], compare_op=ALU.is_ge, fill=NEG, base=-P,
                               pattern=[[1, 2 * P]], channel_multiplier=-1).then_inc(S["masks_made"], 1)
            pool.affine_select(out=mask_qk[:], in_=mask_qk[:], compare_op=ALU.is_ge, fill=NEG, base=0,
                               pattern=[[-1, P]], channel_multiplier=1).then_inc(S["masks_made"], 1)
            pool.wait_ge(S["masks_made"], 6)
            pool.memset(q2[D:P, :].bitcast(F32), 0.0).then_inc(S["rows_beside_qk_made"], 1)
            pool.memset(k2[D:P, :, :].bitcast(F32), 0.0).then_inc(S["rows_beside_qk_made"], 1)
            pool.wait_ge(S["rows_beside_qk_made"], 2)
            pool.memset(k2[D:D + 1, :, :].bitcast(F32), 1.0).then_inc(S["rows_beside_qk_made"], 1)
            pool.wait_ge(S["rows_beside_qk_made"], 3)
            for b in range(2):
                pool.memset(v1[:, b, :, D:2 * D].bitcast(F32), 1.0).then_inc(S["ones_beside_v_made"], 1)

            def section(g, cur, nxt):
                for p in range(NP):
                    if cur:
                        c = chunk_of(PAIR0, p)
                        lo = CH // 2 if p == PAIR0[c + 1] - 1 else 0
                        wait(pool, S["probs_high_ready"], at(g, NP, p + 1))
                        wait(pool, S["pv_done"], at(g, NP, p - 1))
                        pool.tensor_tensor(probs_l[:, p % 2, :, lo:CH], probs[:, p % 2, :, lo:CH],
                                           probs_h[:, p % 4, :, lo:CH], ALU.subtract).then_inc(S["probs_low_ready"], 1)

            section((0, -1), False, True)
            section((0, 0), True, True)
            with pool.Fori(0, (H - 2) // 2) as i:
                for o in (1, 2):
                    section((i, o), True, True)
            section((0, H - 1), True, False)

        @block.scalar
        def _(act):
            for n in range(GROUPS):
                act.wait_ge(S["setup_turned"], n + 1)
                act.activation(group(n, True), scores[:, n % 4 // 2, n % 2, :], ACT.Copy).then_inc(S["setup_high_ready"], 1)

            def w_copy(g):
                wait(act, S["qk_projected"], at(g, NC, 0))
                for part, w in enumerate((wth, wtl)):
                    act.activation(w_head[:, part, :], w[:, bass.ds(index(g), 1), :, :].rearrange("p h s d -> p (h s d)"),
                                   ACT.Copy).then_inc(S["head_weights_ready"], 1)

            def wo_copy(g):
                wait(act, S["output_projected"], at(g, NC, -NC))
                for part, w in enumerate((woh, wol)):
                    act.activation(wo_head[:, g[1] % 2, part, :], w[:, bass.ds(index(g), 1), :].rearrange("p h e -> p (h e)"),
                                   ACT.Copy).then_inc(S["head_wo_ready"], 1)

            def v_high(g):
                b = g[1] % 2
                wait(act, S["pv_done"], at(g, NP, -NP))
                act.wait_ge(S["v_copied"], NT)
                act.activation(v1[:, b, :, 0:D], v_all[:, bass.ds(index(g), 1), :, :].rearrange("p h t d -> p (h t) d"),
                               ACT.Copy).then_inc(S["v_high_ready"], 1)

            def section(g, cur, nxt, prev, first=False):
                for p in range(NP):
                    for c, ahead in due(DONE, p, 0, cur, nxt, prev):
                        h = plus(g, ahead)
                        act.wait_ge(S["pv_done"], at(h, NP, PAIR0[c + 1]))
                        wait(act, S["head_out_normalised"], at(h, NC, c))
                        act.activation(o_sum[:], o_ps[:], ACT.Copy).then_inc(S["head_out_taken"], 1)
                    if cur:
                        c = chunk_of(PAIR0, p)
                        lo = CH // 2 if p == PAIR0[c + 1] - 1 else 0
                        act.wait_ge(S["scores_ready"], at(g, NP, p + 1))
                        wait(act, S["probs_low_ready"], at(g, NP, p - 1))
                        act.activation(probs[:, p % 2, :, lo:CH], scores[:, p % 2, :, lo:CH], ACT.Exp,
                                       scale=D ** -0.5).then_inc(S["probs_ready"], 1)
                        wait(act, S["pv_done"], at(g, NP, p - 3))
                        act.activation(probs_h[:, p % 4, :, lo:CH], scores[:, p % 2, :, lo:CH], ACT.Exp,
                                       scale=D ** -0.5).then_inc(S["probs_high_ready"], 1)
                    if p == 1 and nxt:
                        w_copy(plus(g, 1))
                    for c, ahead in due(PROJECT, p, 1, cur, nxt, prev):
                        h = plus(g, ahead)
                        ks = slice(c * CH, (c + 1) * CH)
                        act.wait_ge(S["qk_positioned"], at(h, NC, c + 1))
                        for rows in (slice(0, D), slice(D, P)):
                            act.activation(k1[rows, h[1] % 2, ks], qk[D:P, c % 2, :], ACT.Copy).then_inc(S["k_high_ready"], 1)
                    for c, ahead in due(PROJECT, p, 2, cur, nxt, prev):
                        h = plus(g, ahead)
                        qs = slice(c * CH, (c + 1) * CH)
                        wait(act, S["scores_ready"], at(h, NP, PAIR0[c + 1] - NP))
                        act.activation(q1[0:D, qs], qk[0:D, c % 2, :], ACT.Copy).then_inc(S["q_high_ready"], 1)
                        act.activation(q2[0:D, qs], qk[0:D, c % 2, :], ACT.Copy).then_inc(S["q_high_doubled"], 1)
                    if first and p < NT:
                        act.wait_ge(S["v_projected"], p + 1)
                        act.activation(v_all[:, :, p, :], scores[:, p % 4 // 2, p % 2, :].rearrange("p (h d) -> p h d", h=H),
                                       ACT.Copy).then_inc(S["v_copied"], 1)
                    if p == 9 and nxt:
                        wo_copy(plus(g, 1))
                    if p == 15 and nxt:
                        v_high(plus(g, 1))
                    for c, ahead in due(DONE, p, 2, cur, nxt, prev):
                        h = plus(g, ahead)
                        act.wait_ge(S["head_out_normalised"], at(h, NC, c + 1))
                        wait(act, S["output_projected"], at(h, NC, c - 1))
                        act.activation(oh[0:D, c % 2, :], o_norm[:, c % 2, :], ACT.Copy).then_inc(S["head_out_high_ready"], 1)

            section((0, -1), False, True, False, first=True)
            section((0, 0), True, True, False)
            with act.Fori(0, (H - 2) // 2) as i:
                for o in (1, 2):
                    section((i, o), True, True, True)
            section((0, H - 1), True, False, True)
            section((0, H), False, False, True)

        @block.vector
        def _(dve):
            for n in range(GROUPS):
                dve.wait_ge(S["setup_high_ready"], n + 1)
                dve.tensor_tensor(group(n, False), scores[:, n % 4 // 2, n % 2, :], group(n, True), ALU.subtract).then_inc(S["setup_low_ready"], 1)
            dve.memset(acc[:], 0.0).then_inc(S["sum_cleared"], 1)
            dve.wait_ge(S["sum_cleared"], 1)

            def v_low(g, part):
                dve.wait_ge(S["v_high_ready"], at(g, 1, 1))
                b, ts = g[1] % 2, slice(part * NT // 2, (part + 1) * NT // 2)
                dve.tensor_tensor(v2[:, b, ts, :], v_all[:, bass.ds(index(g), 1), ts, :].rearrange("p h t d -> p (h t) d"),
                                  v1[:, b, ts, 0:D], ALU.subtract).then_inc(S["v_low_ready"], 1)

            def section(g, cur, nxt, prev):
                for p in range(NP):
                    for ahead, u in units(p, cur, nxt):
                        h = plus(g, ahead)
                        c, r, j, width = unit_place(u)
                        if u == UNIT0[c]:
                            wait(dve, S["row_max_ready"], at(h, NC, c))
                        dve.wait_ge(S["max_scores_ready"], at(h, NU, u + 1))
                        dve.tensor_reduce(m_part[:, r, j:j + 1], max_ps[:, u % 2, 0:width], AX.X, ALU.max).then_inc(S["tile_max_ready"], 1)
                        if u + 1 == UNIT0[c + 1]:
                            dve.wait_ge(S["tile_max_ready"], at(h, NU, u + 1))
                            wait(dve, S["maxima_turned"], at(h, NC, c - 1))
                            dve.tensor_reduce(m_max[:, c % 2, :], m_part[:, :, 0:c + 1], AX.X, ALU.max).then_inc(S["row_max_ready"], 1)
                    for c, ahead in due(OUTPUT, p, 0, cur, nxt, prev):
                        h = plus(g, ahead)
                        qs = slice(c * CH, (c + 1) * CH)
                        wait(dve, S["output_added"], at(h, NC, c))
                        dve.wait_ge(S["output_projected"], at(h, NC, c + 1))
                        dve.tensor_tensor(acc[:, qs], acc[:, qs], side_ps[:], ALU.add).then_inc(S["output_added"], 1)
                    for c, ahead in due(TURN, p, 0, cur, nxt, prev):
                        h = plus(g, ahead)
                        wait(dve, S["scores_ready"], at(h, NP, PAIR0[c + 1] - NP))
                        wait(dve, S["max_row_moved"], at(h, 16 * NC, 16 * c))
                        dve.wait_ge(S["maxima_turned"], at(h, NC, c + 1))
                        dve.tensor_scalar(m_row[:], side_ps[0:TPC, 0:P], -1.0, None, ALU.mult).then_inc(S["max_row_ready"], 1)
                    for c, ahead in due(PROJECT, p, 0, cur, nxt, prev):
                        h = plus(g, ahead)
                        wait(dve, S["q_low_ready"], at(h, NC, c - 1))
                        wait(dve, S["k_low_ready"], at(h, NC, c - 1))
                        wait(dve, S["q_high_doubled"], at(h, NC, c - 1))
                        wait(dve, S["k_high_ready"], at(h, 2 * NC, 2 * (c - 1)))
                        dve.wait_ge(S["qk_projected"], at(h, NC, c + 1))
                        dve.tensor_tensor(qk[:, c % 2, :], side_ps[:], pos[:, c * CH:(c + 1) * CH], ALU.add).then_inc(S["qk_positioned"], 1)
                    for c, ahead in due(DONE, p, 0, cur, nxt, prev):
                        h = plus(g, ahead)
                        wait(dve, S["inverse_turned"], at(h, NC, c))
                        dve.wait_ge(S["head_out_taken"], at(h, NC, c + 1))
                        dve.transpose(l_cols, o_sum[D:P, :]).then_inc(S["sums_turned"], 1)
                    for c, ahead in due(PROJECT, p, 2, cur, nxt, prev):
                        h = plus(g, ahead)
                        b, ks = h[1] % 2, slice(c * CH, (c + 1) * CH)
                        dve.wait_ge(S["k_high_ready"], at(h, 2 * NC, 2 * (c + 1)))
                        dve.tensor_tensor(k2[0:D, b, ks], qk[D:P, c % 2, :], k1[D:P, b, ks], ALU.subtract).then_inc(S["k_low_ready"], 1)
                    for c, ahead in due(PROJECT, p, 3, cur, nxt, prev):
                        h = plus(g, ahead)
                        qs = slice(c * CH, (c + 1) * CH)
                        dve.wait_ge(S["q_high_doubled"], at(h, NC, c + 1))
                        dve.tensor_tensor(q1[D:P, qs], qk[0:D, c % 2, :], q1[0:D, qs], ALU.subtract).then_inc(S["q_low_ready"], 1)
                    for c, ahead in due(DONE, p, 0, cur, nxt, prev):
                        h = plus(g, ahead)
                        dve.wait_ge(S["sums_turned"], at(h, NC, c + 1))
                        dve.reciprocal(l_inv[D:P, :], l_cols.rearrange("p (b j) -> p b j", j=32)[:, :, 0]).then_inc(S["sums_inverted"], 1)
                        dve.wait_ge(S["sums_inverted"], at(h, NC, c + 1))
                        dve.tensor_copy(l_cols.rearrange("p (b j) -> p b j", j=32),
                                        l_inv[D:P, :].unsqueeze(2).to_broadcast([D, CH // 32, 32])).then_inc(S["inverse_spread"], 1)
                        dve.wait_ge(S["inverse_spread"], at(h, NC, c + 1))
                        wait(dve, S["head_out_normalised"], at(h, NC, c))
                        dve.transpose(l_rows, l_cols).then_inc(S["inverse_turned"], 1)
                    for c, ahead in due(DONE, p, 1, cur, nxt, prev):
                        h = plus(g, ahead)
                        dve.wait_ge(S["inverse_turned"], at(h, NC, c + 1))
                        wait(dve, S["head_out_low_ready"], at(h, NC, c - 1))
                        dve.tensor_tensor(o_norm[:, c % 2, :], o_sum[0:D, :], l_rows, ALU.mult).then_inc(S["head_out_normalised"], 1)
                    if p in V_LOW and nxt:
                        v_low(plus(g, 1), V_LOW.index(p))
                    for c, ahead in due(DONE, p, 3, cur, nxt, prev):
                        h = plus(g, ahead)
                        dve.wait_ge(S["head_out_high_ready"], at(h, NC, c + 1))
                        dve.tensor_tensor(oh[D:P, c % 2, :], o_norm[:, c % 2, :], oh[0:D, c % 2, :], ALU.subtract).then_inc(S["head_out_low_ready"], 1)

            dve.wait_ge(S["loaded_positions"], 16)
            section((0, -1), False, True, False)
            section((0, 0), True, True, False)
            with dve.Fori(0, (H - 2) // 2) as i:
                for o in (1, 2):
                    section((i, o), True, True, True)
            section((0, H - 1), True, False, True)
            section((0, H), False, False, True)

        @block.tensor
        def _(pe):
            pe.wait_ge(S["identity_made"], 2)
            for n in range(GROUPS):
                if n >= 4:
                    pe.wait_ge(S["setup_low_ready"], n - 3)
                if n == 0:
                    pe.wait_ge(S["loaded_w_qkv"], 64)
                if n == 3:
                    pe.wait_ge(S["loaded_x"], 16)
                if n == 7:
                    pe.wait_ge(S["loaded_w_o"], 32)
                for j in range(4):
                    if n < 3:
                        src = wq_raw[:, 4 * n + j, :]
                    elif n < 7:
                        src = x_tok[:, 4 * (n - 3) + j, :]
                    else:
                        src = wo_raw[:, 4 * (n - 7) + j, :, :].rearrange("p r d -> p (r d)")
                    last = pe.transpose(scores[:, n % 4 // 2, n % 2, j * P:(j + 1) * P], src, ident[:])
                last.then_inc(S["setup_turned"], 1)

            def v_tile(n):
                if n == 0:
                    pe.wait_ge(S["setup_low_ready"], GROUPS)
                if n >= 4:
                    pe.wait_ge(S["v_copied"], n - 3)
                ts = slice(n * P, (n + 1) * P)
                for k, (a, w) in enumerate(((xh, wvh), (xh, wvl), (xl, wvh))):
                    last = pe.matmul(scores[:, n % 4 // 2, n % 2, :], a[:, ts], w, start=(k == 0), stop=(k == 2))
                last.then_inc(S["v_projected"], 1)

            def project(h, c):
                xs = slice(c * CH, (c + 1) * CH)
                for k, (w, a) in enumerate(((0, xh), (0, xl), (1, xh))):
                    last = pe.matmul(side_ps[:], w_head[:, w, :], a[:, xs], start=(k == 0), stop=(k == 2))
                last.then_inc(S["qk_projected"], 1)

            def maximum(h, u):
                c, r, j, width = unit_place(u)
                b = h[1] % 2
                if u == UNIT0[c]:
                    pe.wait_ge(S["q_low_ready"], at(h, NC, c + 1))
                    pe.wait_ge(S["k_high_ready"], at(h, 2 * NC, 2 * (c + 1)))
                wait(pe, S["tile_max_ready"], at(h, NU, u - 1))
                n = max(width, 2 * P)
                ks = slice(j * CH, j * CH + n)
                tile = (c * TPC + r) * P
                last = pe.matmul(max_ps[:, u % 2, 0:n], q1[:, tile:tile + P], k1[:, b, ks], start=True, stop=(j < c))
                if j == c:
                    last = pe.matmul(max_ps[:, u % 2, width - P:width], ident_b[:], mask_qk[:], start=False, stop=True)
                last.then_inc(S["max_scores_ready"], 1)

            def turn(h, c):
                pe.wait_ge(S["row_max_ready"], at(h, NC, c + 1))
                pe.transpose(side_ps[0:TPC, 0:P], m_max[:, c % 2, :], ident[:]).then_inc(S["maxima_turned"], 1)

            def output(h, c):
                pe.wait_ge(S["head_out_low_ready"], at(h, NC, c + 1))
                if c == 0:
                    pe.wait_ge(S["head_wo_ready"], at(h, 2, 2))
                for part in range(2):
                    last = pe.matmul(side_ps[:], wo_head[:, h[1] % 2, part, :], oh[:, c % 2, :], start=(part == 0), stop=(part == 1))
                last.then_inc(S["output_projected"], 1)

            def score_pair(h, p):
                c = chunk_of(PAIR0, p)
                b = h[1] % 2
                if p == PAIR0[c]:
                    pe.wait_ge(S["max_row_moved"], at(h, 16 * NC, 16 * (c + 1)))
                    pe.wait_ge(S["k_low_ready"], at(h, NC, c + 1))
                wait(pe, S["probs_high_ready"], at(h, NP, p - 1))
                for j in range(2):
                    kb = 2 * (p - PAIR0[c]) + j
                    diag = kb - TPC * c
                    lo = P * min(diag, 2) if diag > 0 else 0
                    ks = slice(kb * P, (kb + 1) * P)
                    qs = slice(c * CH + lo, (c + 1) * CH)
                    into = scores[:, p % 2, j, lo:CH]
                    pe.matmul(into, k1[:, b, ks], q1[:, qs], start=True, stop=False)
                    last = pe.matmul(into, k2[:, b, ks], q2[:, qs], start=False, stop=(diag < 0))
                    if diag >= 0:
                        m0 = 0 if diag == 3 else P
                        last = pe.matmul(scores[:, p % 2, j, (diag + 1) * P - (2 * P - m0):(diag + 1) * P], ident_b[:],
                                         mask_kq[:, m0:2 * P], start=False, stop=True)
                last.then_inc(S["scores_ready"], 1)

            def pv_pair(h, p):
                c = chunk_of(PAIR0, p)
                b = h[1] % 2
                pe.wait_ge(S["probs_low_ready"], at(h, NP, p + 1))
                if p == PAIR0[c]:
                    wait(pe, S["head_out_taken"], at(h, NC, c))
                if p == 0:
                    pe.wait_ge(S["v_low_ready"], at(h, 2, 2))
                for j in range(2):
                    kb = 2 * (p - PAIR0[c]) + j
                    diag = kb - TPC * c
                    lo = P * min(diag, 2) if diag > 0 else 0
                    hi_v = v1[:, b, kb, :]
                    lo_v = v2[:, b, kb, :]
                    for k, (v, rows, pr) in enumerate(((hi_v, P, probs_h[:, p % 4, j, lo:CH]),
                                                       (lo_v, D, probs_h[:, p % 4, j, lo:CH]),
                                                       (hi_v, P, probs_l[:, p % 2, j, lo:CH]))):
                        last = pe.matmul(o_ps[0:rows, lo:CH], v, pr, start=(p == PAIR0[c] and j == 0 and k == 0),
                                         stop=(p == PAIR0[c + 1] - 1 and j == 1 and k == 2))
                last.then_inc(S["pv_done"], 1)

            def section(g, cur, nxt, prev, first=False):
                before = [("output_added", at(plus(g, -1), NC, NC - 1))] if prev else [("qk_positioned", at(g, NC, NC))] if cur else []

                def side_bank(evacuated, value):
                    if before:
                        wait(pe, S[before[0][0]], before[0][1])
                    before[:] = [(evacuated, value)]

                for p in range(NP):
                    if cur:
                        score_pair(g, p)
                    for ahead, u in units(p, cur, nxt):
                        maximum(plus(g, ahead), u)
                    for c, ahead in due(OUTPUT, p, 0, cur, nxt, prev):
                        side_bank("output_added", at(plus(g, ahead), NC, c + 1))
                        output(plus(g, ahead), c)
                    for c, ahead in due(TURN, p, 0, cur, nxt, prev):
                        side_bank("max_row_ready", at(plus(g, ahead), NC, c + 1))
                        turn(plus(g, ahead), c)
                    for c, ahead in due(PROJECT, p, 0, cur, nxt, prev):
                        if c == 0:
                            pe.wait_ge(S["head_weights_ready"], at(plus(g, ahead), 2, 2))
                        side_bank("qk_positioned", at(plus(g, ahead), NC, c + 1))
                        project(plus(g, ahead), c)
                    if first and p < NT:
                        v_tile(p)
                    if p >= 2 and cur:
                        pv_pair(g, p - 2)
                    if p < 2 and prev:
                        pv_pair(plus(g, -1), NP - 2 + p)

            pe.wait_ge(S["masks_made"], 6)
            section((0, -1), False, True, False, first=True)
            pe.wait_ge(S["ones_beside_v_made"], 2)
            pe.wait_ge(S["rows_beside_qk_made"], 3)
            section((0, 0), True, True, False)
            with pe.Fori(0, (H - 2) // 2) as i:
                for o in (1, 2):
                    section((i, o), True, True, True)
            section((0, H - 1), True, False, True)
            section((0, H), False, False, True)


def layer_norm(dve, sem, base, src, dst, buf, n):
    stats, mean_var, s, pause = buf
    var, half, guess, t, bits = (s[:, i, 0:n] for i in range(5))
    if not isinstance(base, int) or base > 0:
        dve.wait_ge(sem, base)
    for i in range(n):
        dve.bn_stats(stats[:, i, :], src[:, i, :]).then_inc(sem, 1)
        yield
    dve.wait_ge(sem, base + n)
    dve.memset(pause, 0.0).then_inc(sem, 1)
    yield
    base = base + 1
    for i in range(n):
        dve.bn_aggr(mean_var[:, i, :], stats[:, i, :]).then_inc(sem, 1)
        yield
    dve.wait_ge(sem, base + 2 * n)
    dve.tensor_scalar(var, mean_var[:, 0:n, 1], EPS, None, ALU.add).then_inc(sem, 1)
    yield
    base = base + 2 * n
    dve.wait_ge(sem, base + 1)
    dve.tensor_scalar(bits.bitcast(I32), var.bitcast(I32), 1, None, ALU.logical_shift_right).then_inc(sem, 1)
    yield
    dve.wait_ge(sem, base + 2)
    dve.tensor_scalar(guess.bitcast(I32), bits.bitcast(I32), -1, 0x5F3759DF, ALU.mult, ALU.add).then_inc(sem, 1)
    yield
    for k in range(3):
        dve.wait_ge(sem, base + 3 + 3 * k)
        dve.tensor_tensor(t, guess, guess, ALU.mult).then_inc(sem, 1)
        yield
        dve.wait_ge(sem, base + 4 + 3 * k)
        dve.scalar_tensor_tensor(half, var, -0.5, t, ALU.mult, ALU.mult).then_inc(sem, 1)
        yield
        dve.wait_ge(sem, base + 5 + 3 * k)
        dve.scalar_tensor_tensor(guess, half, 1.5, guess, ALU.add, ALU.mult).then_inc(sem, 1)
        yield
    dve.wait_ge(sem, base + 12)
    for i in range(n):
        dve.tensor_scalar(dst[:, i, :], src[:, i, :], mean_var[:, i, 0:1], guess[:, i:i + 1],
                          ALU.subtract, ALU.mult).then_inc(sem, 1)
        yield


class Early:

    def __init__(self, pos, qk, v_all, sems):
        self.x_in = pos[:].rearrange("p (n e) -> p n e", e=E)
        self.gens = qk[:, 0, :].rearrange("p (r j) -> p r j", r=NROT)
        small = qk[:, 1, :]
        self.vec_rows = small[0:N_VEC, 0:P]
        self.gw, self.gb, self.gcb = small[:, P:P + NX], small[:, P + NX:P + 2 * NX], small[:, P + 2 * NX:P + 2 * NX + 1]
        free = v_all[:].rearrange("p h t d -> p (h t d)")
        self.w_raw = free[:, 0:W_COLS]
        self.n2, self.y2 = (free[:, a:a + T].rearrange("p (n e) -> p n e", e=E) for a in (W_COLS, W_COLS + T))
        self.sems = sems

    def load(self, sp, x, ln_g, ln_b, aw1, ab1, aw2, ab2, gate_w, gate_b, ew1, eb1, ew2, eb2, gens, gc_w, gc_b):
        S = self.sems

        def row(a, n=1):
            return self.vec_rows[a:a + n, :]

        sp.dma_start(self.x_in, x.rearrange("b (n p) e -> p (b n) e", p=P)).then_inc(S["early_x_loaded"], 16)
        sp.dma_start(self.gens, gens.rearrange("r i j -> i r j")).then_inc(S["early_generators_loaded"], 16)
        small = [(self.gw, gate_w), (self.gb, gate_b.partition_broadcast(P)), (self.gcb, gc_b.partition_broadcast(P)),
                 (row(0), ln_g.rearrange("(o d) -> o d", o=1)), (row(1), ln_b.rearrange("(o d) -> o d", o=1)),
                 (row(2), ab2.rearrange("(o d) -> o d", o=1)), (row(3, 2), gc_w.rearrange("(o d) u -> o (d u)", o=2)),
                 (row(5, NA), ab1.rearrange("(m p) -> m p", p=P)),
                 (row(5 + NA, NX * NXB), eb1.rearrange("e (k p) -> (e k) p", p=P))]
        assert len(small) == N_SMALL
        for dst, src in small:
            sp.dma_start(dst, src).then_inc(S["early_small_loaded"], 16)
        A, X = NA * P, NX * NXB * P
        sp.dma_start(self.w_raw[:, 0:A], aw1).then_inc(S["early_weights_loaded"], 16)
        sp.dma_start(self.w_raw[:, A:2 * A].rearrange("p (m d) -> p m d", m=NA), aw2.rearrange("(m p) d -> p m d", p=P)).then_inc(S["early_weights_loaded"], 16)
        sp.dma_start(self.w_raw[:, 2 * A:2 * A + X].rearrange("p (e h) -> p e h", e=NX), ew1.rearrange("e d h -> d e h")).then_inc(S["early_weights_loaded"], 16)
        sp.dma_start(self.w_raw[:, 2 * A + X:].rearrange("p (e k d) -> p e k d", e=NX, k=NXB),
                     ew2.rearrange("e (k p) d -> p e k d", p=P)).then_inc(S["early_weights_loaded"], 16)


def feed_forward(nc, early, acc, ident, eb2, out):
    with ExitStack() as ctx:
        def sb(name, shape, dt=F32):
            return ctx.enter_context(nc.sbuf_tensor(name, shape, dt))

        def sem(name):
            return ctx.enter_context(nc.semaphore(name))

        w_hi = sb("w_hi", [P, W_COLS], F32R)
        w_lo = sb("w_lo", [P, W_COLS], F32R)
        x_in, gens_sb, vec_rows, w_raw = early.x_in, early.gens, early.vec_rows, early.w_raw
        n2, y2 = early.n2, early.y2
        gw, gb, gcb = early.gw, early.gb, early.gcb
        y1 = sb("y1", [P, NT, E])
        u = sb("u", [P, NT, E])
        ln_buf = (sb("ln_stats", [P, NT // 2, 6])[:], sb("ln_mean_var", [P, NT // 2, 2])[:], sb("ln_small", [P, 5, NT // 2])[:],
                  sb("ln_pause", [P, 1])[:])
        xn = sb("xn", [P, T])
        xn_hi = sb("xn_hi", [P, T], F32R)
        xn_lo = sb("xn_lo", [P, T], F32R)
        gen = sb("gen", [P, NROT, P])
        gen_t = sb("gen_t", [P, NROT, P])
        gen2_t = sb("gen2_t", [P, NROT, P])
        series = sb("series", [P, NROT, P])
        e_sum = sb("e_sum", [P, NROT, P])
        e_turn = sb("e_turn", [P, NROT, P])
        e_last = sb("e_last", [P, P])
        half_eye = sb("half_eye", [P, P])
        eyes = sb("eyes", [P, 2, P], BF16)
        rot = sb("rot", [P, 2, P])
        rot_hi = sb("rot_hi", [P, P], F32R)
        rot_lo = sb("rot_lo", [P, P], F32R)
        vec_cols = sb("vec_cols", [P, N_VEC])
        g_col, b_col, ab2_col, gc_col = (vec_cols[:, a:b] for a, b in ((0, 1), (1, 2), (2, 3), (3, 5)))
        ab1_col, eb1_col = vec_cols[:, 5:5 + NA], vec_cols[:, 5 + NA:N_VEC]
        eb2_rows = sb("eb2_rows", [P, E])
        eb2_hi = sb("eb2_hi", [P, E], F32R)
        eb2_lo = sb("eb2_lo", [P, E], F32R)
        gc_wide = sb("gc_wide", [P, 2, P])
        gcb_half = sb("gcb_half", [P, 1])
        pick = sb("pick", [P, NX, P], F32R)
        logits = sb("logits", [P, NT, NX])
        before = sb("before", [P, NX, NX])
        gt = sb("gt", [P, NT // 2, NX, NX])
        eq = sb("eq", [P, NT // 2, NX, NX])
        rank = sb("rank", [P, NT // 2, NX])
        first = sb("first", [P, NT // 2, NX])
        second_first = sb("second_first", [P, NT // 2, NX])
        chosen = sb("chosen", [P, NT // 2, NX])
        gap = sb("gap", [P, NT])
        gap_t = sb("gap_t", [P, NT])
        mix_w = sb("mix_w", [P, NT // 2, NX])
        w_pad = sb("w_pad", [P, NT, 64])
        wt = sb("wt", [P, T], F32R)
        hid = sb("hid", [P, RING, CH])
        hid_hi = sb("hid_hi", [P, RING, CH], F32R)
        hid_lo = sb("hid_lo", [P, RING, CH], F32R)
        abel = sb("abel", [P, CH])
        moe_hi = sb("moe_hi", [P, CH], F32R)
        moe_lo = sb("moe_lo", [P, CH], F32R)
        nonabel = sb("nonabel", [P, CH])
        gate = sb("gate", [P, CH])
        delta = sb("delta", [P, CH])
        mixed = sb("mixed", [P, CH])
        last_sum = sb("last_sum", [P, TPC, E])

        ps = ctx.enter_context(nc.psum_tensor("ps_ffn", [P, 8, CH], F32))

        names = """loaded_eb2 eb2_cleared pick_made before_made identities_made weights_cleared attention_turned
            generator_turned generator_squared series_multiplied exponential_squared exponential_turned
            vectors_turned features_turned logits_ready expert_weights_turned rotation_multiplied
            hidden_scores_ready expert_weight_spread second_layer_done moe_summed moe_rotated gate_summed
            mixed_turned generator_scaled generator_turned_taken generator_square_taken exponential_taken
            turned_exponential_taken squared_exponential_taken vectors_ready weights_high_ready
            features_ready expert_weights_high_ready rotation_taken rotation_high_ready gap_tanh_ready
            eb2_high_ready hidden_ready hidden_high_ready abel_ready moe_high_ready nonabel_ready
            gate_tanh_ready residual_ready first_norms_steps features_low_ready logits_biased choice_steps
            expert_weights_low_ready gate_constants_ready hidden_weighted dense_high_ready moe_low_ready
            mix_steps second_residual_ready last_norm_steps padded_weights_ready rotation_low_ready
            series_steps last_exponential_ready weights_low_ready hidden_low_ready output_stored""".split()
        S = {n: sem("ffn_" + n) for n in names}
        S.update(early.sems)
        block = ctx.enter_context(nc.Block())

        def tiles(h):
            return slice(h * NT // 2, (h + 1) * NT // 2)

        def half(h):
            return slice(HALF * h, HALF * (h + 1))

        def product(h):
            return ps[:, 6 + h, 0:HALF * P].rearrange("p (r j) -> p r j", r=HALF)

        def turn_bank(h):
            return ps[:, 6 + h, HALF * P:2 * HALF * P].rearrange("p (r j) -> p r j", r=HALF)

        @block.sync
        def _(sp):
            sp.wait_ge(S["eb2_cleared"], 1)
            for row in (0, 32):
                sp.dma_start(eb2_rows[row:row + NX, :], eb2).then_inc(S["loaded_eb2"], 16)
            o_v = out.rearrange("b (n p) e -> p (b n) e", p=P)
            for c in range(NC):
                sp.wait_ge(S["last_norm_steps"], ln_steps(TPC) * (c + 1))
                sp.dma_start(o_v[:, TPC * c:TPC * (c + 1), :], y2[:, TPC * c:TPC * (c + 1), :]).then_inc(S["output_stored"], 16)
            sp.wait_ge(S["output_stored"], 16 * NC)

        PART = W_COLS // W_PARTS

        @block.gpsimd
        def _(pool):
            pool.tensor_scalar(half_eye[:], ident[:], 0.5, None, ALU.mult).then_inc(S["identities_made"], 1)
            for n in range(2):
                pool.tensor_scalar(eyes[:, n, :], ident[:], n + 1.0, None, ALU.mult).then_inc(S["identities_made"], 1)

            pool.wait_ge(S["identities_made"], 1)
            pool.wait_ge(S["generator_scaled"], 2)
            pool.tensor_tensor(series[:], series[:], half_eye[:].unsqueeze(1).to_broadcast([P, NROT, P]), ALU.add).then_inc(S["series_steps"], 1)
            for h in range(2):
                hs = half(h)
                pool.wait_ge(S["series_steps"], h + 1)
                pool.wait_ge(S["generator_square_taken"], 2 * (h + 1))
                pool.tensor_tensor(series[:, hs, :], series[:, hs, :], e_turn[:, hs, :], ALU.add).then_inc(S["series_steps"], 1)
            pool.tensor_tensor(pick[:], ident[:, 0:NX].unsqueeze(2).to_broadcast([P, NX, P]),
                               ident[:, 32:32 + NX].unsqueeze(2).to_broadcast([P, NX, P]), ALU.add).then_inc(S["pick_made"], 1)
            pool.memset(before[:], 1.0).then_inc(S["before_made"], 1)
            pool.wait_ge(S["before_made"], 1)
            pool.affine_select(out=before[:], in_=before[:], compare_op=ALU.is_gt, fill=0.0, base=0,
                               pattern=[[1, NX], [-1, NX]], channel_multiplier=0).then_inc(S["before_made"], 1)

            for k in range(W_PARTS):
                cols = slice(k * PART, (k + 1) * PART)
                pool.wait_ge(S["weights_high_ready"], k + 1)
                pool.tensor_tensor(w_lo[:, cols], w_raw[:, cols], w_hi[:, cols], ALU.subtract).then_inc(S["weights_low_ready"], 1)

            def section(c, first=False):
                for j in range(NB):
                    if first and j + 1 == min(PRODUCT_AT):
                        pool.wait_ge(S["squared_exponential_taken"], 2 * SQUARINGS)
                        pool.tensor_tensor(e_last[:], e_sum[:, NROT - 1, :], ident[:], ALU.add).then_inc(S["last_exponential_ready"], 1)
                    if j < NA:
                        pool.wait_ge(S["dense_high_ready"], c * NA + (j + 1))
                    else:
                        pool.wait_ge(S["hidden_high_ready"], c * (NB - NA) + (j - NA + 1))
                    wait(pool, S["second_layer_done"], c * NB + (j - RING + 1))
                    r = j % RING
                    pool.tensor_tensor(hid_lo[:, r, :], hid[:, r, :], hid_hi[:, r, :], ALU.subtract).then_inc(S["hidden_low_ready"], 1)

            section(0, first=True)
            with pool.Fori(1, NC) as c:
                section(c)

        @block.scalar
        def _(act):
            scale = 2.0 ** -SQUARINGS
            act.wait_ge(S["early_generators_loaded"], 16)
            act.activation(gen[:], gens_sb, ACT.Copy, scale=scale).then_inc(S["generator_scaled"], 1)
            act.activation(series[:], gens_sb, ACT.Copy, scale=scale / 6).then_inc(S["generator_scaled"], 1)
            for h in range(2):
                act.wait_ge(S["generator_turned"], h + 1)
                act.activation(gen_t[:, half(h), :], turn_bank(h), ACT.Copy, scale=scale).then_inc(S["generator_turned_taken"], 1)
            for h in range(2):
                act.wait_ge(S["generator_squared"], h + 1)
                act.activation(gen2_t[:, half(h), :], turn_bank(h), ACT.Copy).then_inc(S["generator_square_taken"], 1)
                act.activation(e_turn[:, half(h), :], product(h), ACT.Copy, scale=1 / 24).then_inc(S["generator_square_taken"], 1)

            for h in range(2):
                act.wait_ge(S["series_multiplied"], h + 1)
                act.activation(e_sum[:, half(h), :], product(h), ACT.Copy).then_inc(S["exponential_taken"], 1)

            def turned(k):
                for h in range(2):
                    act.wait_ge(S["exponential_turned"], 2 * k + h + 1)
                    act.activation(e_turn[:, half(h), :], turn_bank(h), ACT.Copy).then_inc(S["turned_exponential_taken"], 1)

            def squared(k):
                for h in range(2):
                    act.wait_ge(S["exponential_squared"], 2 * k + h + 1)
                    act.activation(e_sum[:, half(h), :], product(h), ACT.Copy).then_inc(S["squared_exponential_taken"], 1)

            def to_features(c):
                cs = slice(c * CH, (c + 1) * CH)
                act.wait_ge(S["vectors_ready"], 1)
                act.wait_ge(S["features_turned"], c + 1)
                src = ps[:, c if c < 2 else 7, :]
                act.activation(xn[:, cs], src, ACT.Identity, scale=g_col, bias=b_col).then_inc(S["features_ready"], 1)
                act.activation(xn_hi[:, cs], src, ACT.Identity, scale=g_col, bias=b_col).then_inc(S["features_ready"], 1)

            def gap_tanh(h):
                act.wait_ge(S["choice_steps"], CHOOSE * h + CHOOSE_TANH)
                act.activation(gap_t[:, tiles(h)], gap[:, tiles(h)], ACT.Tanh, scale=0.5).then_inc(S["gap_tanh_ready"], 1)

            def weights_high(c):
                act.wait_ge(S["expert_weights_turned"], c + 1)
                act.activation(wt[0:64, c * CH:(c + 1) * CH], ps[0:64, 2 + c if c < 2 else 7, :], ACT.Copy).then_inc(S["expert_weights_high_ready"], 1)

            def weight_high(part):
                cols = slice(part * PART, (part + 1) * PART)
                act.wait_ge(S["early_weights_loaded"], 16 * 4)
                act.activation(w_hi[:, cols], w_raw[:, cols], ACT.Copy).then_inc(S["weights_high_ready"], 1)

            weight_high(0)
            for k in range(EARLY):
                turned(k)
                squared(k)
                weight_high(k + 1)
                if k == 0:
                    act.wait_ge(S["vectors_turned"], 1)
                    act.activation(vec_cols[:], ps[:, 5, P:P + N_VEC], ACT.Copy).then_inc(S["vectors_ready"], 1)
                if k == EARLY_FEATURES:
                    to_features(0)
                    to_features(1)
            act.wait_ge(S["loaded_eb2"], 32)
            act.activation(eb2_hi[:], eb2_rows[:], ACT.Copy).then_inc(S["eb2_high_ready"], 1)
            for part in range(EARLY + 1, W_PARTS):
                weight_high(part)

            def high(c, j):
                r = j % RING
                wait(act, S["second_layer_done"], c * NB + (j - RING + 1))
                act.wait_ge(S["hidden_weighted"], c * (NB - NA) + (j - NA + 1))
                act.activation(hid_hi[:, r, :], hid[:, r, :], ACT.Copy).then_inc(S["hidden_high_ready"], 1)

            def section(c, cur, prev, first=False, second=False):
                for j in range(NB):
                    if cur:
                        bias = ab1_col[:, j:j + 1] if j < NA else eb1_col[:, j - NA:j - NA + 1]
                        act.wait_ge(S["hidden_scores_ready"], c * NB + (j + 1))
                        wait(act, S["hidden_low_ready"], c * NB + (j - RING + 1))
                        act.activation(hid[:, j % RING, :], ps[:, j % 2, :], ACT.Gelu, bias=bias).then_inc(S["hidden_ready"], 1)
                        if j > NA:
                            high(c, j - 1)
                    if first and j == FIRST_TANH_AT:
                        gap_tanh(0)
                    if first and j == FIRST_WEIGHTS_AT:
                        for n in range(2):
                            weights_high(n)
                    if second and j in FEATURES_AT:
                        to_features(FEATURES_AT[j])
                    if second and j == CHOOSE_AT + 2:
                        gap_tanh(1)
                    if second and j in WEIGHTS_AT:
                        weights_high(WEIGHTS_AT[j])
                    if first and j in TURN_AT:
                        turned(TURN_AT[j])
                    if first and j in SQUARE_AT:
                        squared(SQUARE_AT[j])
                    if first and j in PRODUCT_AT:
                        k = PRODUCT_AT[j]
                        act.wait_ge(S["rotation_multiplied"], k + 1)
                        if k < HALF:
                            act.activation(rot[:, k, :], product(0)[:, 0, :], ACT.Copy).then_inc(S["rotation_taken"], 1)
                        else:
                            act.activation(rot_hi[:], product(0)[:, 0, :], ACT.Copy).then_inc(S["rotation_high_ready"], 1)
                    if prev and j == T_ABEL:
                        act.wait_ge(S["second_layer_done"], (c - 1) * NB + NA)
                        wait(act, S["mix_steps"], (c - 1) * 3)
                        act.activation(abel[:], ps[:, 4, :], ACT.Identity, bias=ab2_col).then_inc(S["abel_ready"], 1)
                    if prev and j == T_SPLIT:
                        act.wait_ge(S["moe_summed"], c)
                        wait(act, S["moe_rotated"], c - 1)
                        act.activation(moe_hi[:], ps[:, 5, :], ACT.Copy).then_inc(S["moe_high_ready"], 1)
                    if prev and j == T_NONABEL:
                        act.wait_ge(S["moe_rotated"], c)
                        wait(act, S["gate_summed"], c - 1)
                        wait(act, S["mix_steps"], (c - 1) * 3)
                        act.activation(nonabel[:], ps[:, 6, :], ACT.Copy).then_inc(S["nonabel_ready"], 1)
                    if prev and j == T_TANH:
                        act.wait_ge(S["gate_summed"], c)
                        wait(act, S["mix_steps"], (c - 1) * 3)
                        act.activation(gate[:], ps[:, 7, :], ACT.Tanh, scale=0.5, bias=gcb_half[:]).then_inc(S["gate_tanh_ready"], 1)
                if cur:
                    high(c, NB - 1)

            section(0, True, False, first=True)
            act.wait_ge(S["gate_constants_ready"], 2)
            section(1, True, True, second=True)
            with act.Fori(2, NC) as c:
                section(c, True, True)
            section(NC, False, True)

        @block.vector
        def _(dve):
            dve.memset(eb2_rows[:], 0.0).then_inc(S["eb2_cleared"], 1)
            dve.memset(wt[64:P, :].bitcast(F32), 0.0).then_inc(S["weights_cleared"], 1)

            def residual(c):
                dve.wait_ge(S["attention_turned"], c + 1)
                dve.tensor_tensor(u[:, TPC * c:TPC * (c + 1), :], ps[:, c, :].rearrange("p (t e) -> p t e", e=E),
                                  x_in[:, TPC * c:TPC * (c + 1), :], ALU.add).then_inc(S["residual_ready"], 1)

            def norms(h):
                n = NT // 2
                dve.wait_ge(S["residual_ready"], 2 * h + 2)
                yield from layer_norm(dve, S["first_norms_steps"], 2 * h * ln_steps(n), u[:, tiles(h), :], y1[:, tiles(h), :], ln_buf, n)
                yield from layer_norm(dve, S["first_norms_steps"], (2 * h + 1) * ln_steps(n), y1[:, tiles(h), :], n2[:, tiles(h), :], ln_buf, n)

            def input_low(c):
                cs = slice(c * CH, (c + 1) * CH)
                dve.wait_ge(S["features_ready"], 2 * (c + 1))
                dve.tensor_tensor(xn_lo[:, cs], xn[:, cs], xn_hi[:, cs], ALU.subtract).then_inc(S["features_low_ready"], 1)

            def add_gate_bias(h):
                n = NT // 2
                dve.wait_ge(S["logits_ready"], 2 * h + 2)
                dve.tensor_tensor(logits[:, tiles(h), :],
                                  ps[:, LOGIT_BANK[h], h * n * NX:(h + 1) * n * NX].rearrange("p (t e) -> p t e", e=NX),
                                  gb.unsqueeze(1).to_broadcast([P, n, NX]), ALU.add).then_inc(S["logits_biased"], 1)

            def choose(h):
                n, ts, base = NT // 2, tiles(h), CHOOSE * h
                full, part = [P, n, NX, NX], [P, n, NX]
                values = logits[:, ts, :]
                other, own = values.unsqueeze(2).to_broadcast(full), values.unsqueeze(3).to_broadcast(full)
                dve.wait_ge(S["logits_biased"], h + 1)
                if h:
                    dve.wait_ge(S["choice_steps"], base)
                dve.tensor_tensor(gt[:], other, own, ALU.is_gt).then_inc(S["choice_steps"], 1)
                yield
                dve.tensor_tensor(eq[:], other, own, ALU.is_equal).then_inc(S["choice_steps"], 1)
                yield
                dve.wait_ge(S["choice_steps"], base + 2)
                dve.tensor_tensor(eq[:], eq[:], before[:].unsqueeze(1).to_broadcast(full), ALU.mult).then_inc(S["choice_steps"], 1)
                yield
                dve.wait_ge(S["choice_steps"], base + 3)
                dve.tensor_tensor(gt[:], gt[:], eq[:], ALU.add).then_inc(S["choice_steps"], 1)
                yield
                dve.wait_ge(S["choice_steps"], base + 4)
                dve.tensor_reduce(rank[:], gt[:], AX.X, ALU.add).then_inc(S["choice_steps"], 1)
                yield
                dve.wait_ge(S["choice_steps"], base + 5)
                dve.tensor_scalar(first[:], rank[:], 0.0, None, ALU.is_equal).then_inc(S["choice_steps"], 1)
                yield
                dve.wait_ge(S["choice_steps"], base + 6)
                dve.scalar_tensor_tensor(second_first[:], rank[:], 1.0, first[:], ALU.is_equal, ALU.subtract).then_inc(S["choice_steps"], 1)
                yield
                dve.wait_ge(S["choice_steps"], base + 7)
                dve.scalar_tensor_tensor(chosen[:], second_first[:], -1.0, values, ALU.mult, ALU.mult).then_inc(S["choice_steps"], 1)
                yield
                dve.wait_ge(S["choice_steps"], base + 8)
                dve.tensor_reduce(gap[:, ts], chosen[:], AX.X, ALU.add).then_inc(S["choice_steps"], 1)
                yield
                dve.wait_ge(S["gap_tanh_ready"], h + 1)
                dve.tensor_tensor(mix_w[:], second_first[:], gap_t[:, ts].unsqueeze(2).to_broadcast(part), ALU.mult).then_inc(S["choice_steps"], 1)
                yield
                dve.tensor_scalar(chosen[:], rank[:], 1.5, None, ALU.is_lt).then_inc(S["choice_steps"], 1)
                yield
                dve.wait_ge(S["choice_steps"], base + 11)
                dve.tensor_tensor(mix_w[:], chosen[:], mix_w[:], ALU.subtract).then_inc(S["choice_steps"], 1)
                yield
                dve.wait_ge(S["choice_steps"], base + 12)
                for col in (0, 32):
                    dve.tensor_scalar(w_pad[:, ts, col:col + NX], mix_w[:], 0.5, None, ALU.mult).then_inc(S["padded_weights_ready"], 1)
                yield

            def weights_low(c):
                cs = slice(c * CH, (c + 1) * CH)
                dve.wait_ge(S["expert_weights_high_ready"], c + 1)
                dve.tensor_tensor(wt[32:64, cs], ps[32:64, 2 + c if c < 2 else 7, :], wt[32:64, cs], ALU.subtract).then_inc(S["expert_weights_low_ready"], 1)

            dve.wait_ge(S["early_x_loaded"], 16)
            residual(0)
            residual(1)
            for _ in norms(0):
                pass
            residual(2)
            residual(3)
            dve.memset(w_pad[:], 0.0).then_inc(S["padded_weights_ready"], 1)
            input_low(0)
            input_low(1)
            dve.wait_ge(S["early_small_loaded"], 16 * N_SMALL)
            add_gate_bias(0)
            dve.wait_ge(S["before_made"], 2)
            dve.wait_ge(S["padded_weights_ready"], 1)
            first_choice = choose(0)
            for _ in range(CHOOSE_TANH):
                next(first_choice)
            dve.tensor_scalar(gcb_half[:], gcb, 0.5, None, ALU.mult).then_inc(S["gate_constants_ready"], 1)
            dve.wait_ge(S["vectors_ready"], 1)
            dve.tensor_copy(gc_wide[:], gc_col.unsqueeze(2).to_broadcast([P, 2, P])).then_inc(S["gate_constants_ready"], 1)
            dve.wait_ge(S["eb2_high_ready"], 1)
            dve.tensor_tensor(eb2_lo[:], eb2_rows[:], eb2_hi[:], ALU.subtract).then_inc(S["expert_weights_low_ready"], 1)

            def section(c, cur, prev, first=False, second=False):
                rest, choice = norms(1), choose(1)
                for j in range(NB):
                    if second and j in LOW_AT:
                        input_low(LOW_AT[j])
                    if second and j == CHOOSE_AT:
                        add_gate_bias(1)
                    if second and 0 <= j - CHOOSE_AT < len(CHOOSE_STEPS):
                        for _ in range(CHOOSE_STEPS[j - CHOOSE_AT]):
                            next(choice, None)
                    if second and j in WEIGHTS_LOW_AT:
                        weights_low(WEIGHTS_LOW_AT[j])
                    if first and j == max(PRODUCT_AT) + 1:
                        dve.wait_ge(S["rotation_high_ready"], 1)
                        dve.tensor_tensor(rot_lo[:], product(0)[:, 0, :], rot_hi[:], ALU.subtract).then_inc(S["rotation_low_ready"], 1)
                    for _ in range(5 if first else 0):
                        next(rest, None)
                    if cur and j < NA:
                        r = j % RING
                        dve.wait_ge(S["hidden_ready"], c * NB + (j + 1))
                        wait(dve, S["second_layer_done"], c * NB + (j - RING + 1))
                        dve.tensor_copy(hid_hi[:, r, :], hid[:, r, :]).then_inc(S["dense_high_ready"], 1)
                    if first and j == FIRST_TANH_AT:
                        for _ in first_choice:
                            pass
                    if first and j == FIRST_WEIGHTS_AT:
                        for n in range(2):
                            weights_low(n)
                    if cur and j >= NA:
                        n = j - NA
                        dve.wait_ge(S["hidden_ready"], c * NB + (j + 1))
                        dve.wait_ge(S["expert_weight_spread"], c * NX + (n // NXB + 1))
                        dve.tensor_tensor(hid[:, j % RING, :], hid[:, j % RING, :], ps[:, 2 + n // NXB % 2, :], ALU.mult).then_inc(S["hidden_weighted"], 1)
                    if prev and j == T_SPLIT:
                        dve.wait_ge(S["moe_high_ready"], c)
                        dve.tensor_tensor(moe_lo[:], ps[:, 5, :], moe_hi[:], ALU.subtract).then_inc(S["moe_low_ready"], 1)
                    if prev and j == T_MIX:
                        base = (c - 1) * 3
                        dve.wait_ge(S["nonabel_ready"], c)
                        dve.wait_ge(S["abel_ready"], c)
                        wait(dve, S["mix_steps"], base)
                        dve.tensor_tensor(delta[:], nonabel[:], abel[:], ALU.subtract).then_inc(S["mix_steps"], 1)
                        dve.wait_ge(S["gate_tanh_ready"], c)
                        dve.wait_ge(S["mix_steps"], base + 1)
                        dve.scalar_tensor_tensor(delta[:], gate[:], 1.0, delta[:], ALU.add, ALU.mult).then_inc(S["mix_steps"], 1)
                        dve.wait_ge(S["mix_steps"], base + 2)
                        wait(dve, S["mixed_turned"], c - 1)
                        dve.scalar_tensor_tensor(mixed[:], delta[:], 0.5, abel[:], ALU.mult, ALU.add).then_inc(S["mix_steps"], 1)
                    if prev and j == T_NORM:
                        dve.wait_ge(S["mixed_turned"], c)
                        ts = bass.ds((c - 1) * TPC, TPC)
                        wait(dve, S["last_norm_steps"], ln_steps(TPC) * (c - 1))
                        dve.scalar_tensor_tensor(last_sum[:], y1[:, ts, :], 2.0, ps[:, 6, :].rearrange("p (t e) -> p t e", e=E),
                                                 ALU.mult, ALU.add).then_inc(S["second_residual_ready"], 1)
                        dve.wait_ge(S["second_residual_ready"], c)
                        norm = layer_norm(dve, S["last_norm_steps"], ln_steps(TPC) * (c - 1), last_sum[:], y2[:, ts, :], ln_buf, TPC)
                    if prev and j >= T_NORM:
                        for _ in range(NORM_STEPS[j - T_NORM]):
                            next(norm)

            section(0, True, False, first=True)
            section(1, True, True, second=True)
            with dve.Fori(2, NC) as c:
                section(c, True, True)
            section(NC, False, True)

        @block.tensor
        def _(pe):
            for c in range(NC):
                for t in range(TPC):
                    last = pe.transpose(ps[:, c, t * P:(t + 1) * P], acc[:, (c * TPC + t) * P:(c * TPC + t + 1) * P], ident[:])
                last.then_inc(S["attention_turned"], 1)
            pe.wait_ge(S["early_generators_loaded"], 16)

            def turn(src, h, signal):
                for i in range(HALF):
                    last = pe.transpose(turn_bank(h)[:, i, :], src[:, HALF * h + i, :], ident[:])
                last.then_inc(S[signal], 1)

            def multiply(into, left_t, right, h):
                for i in range(HALF):
                    last = pe.matmul(into[:, i, :], left_t[:, HALF * h + i, :], right[:, HALF * h + i, :], start=True, stop=True)
                return last

            for h in range(2):
                turn(gens_sb, h, "generator_turned")
            for h in range(2):
                pe.wait_ge(S["generator_scaled"], 1)
                pe.wait_ge(S["generator_turned_taken"], h + 1)
                multiply(product(h), gen_t, gen, h)
                multiply(turn_bank(h), gen, gen_t, h).then_inc(S["generator_squared"], 1)
            for h in range(2):
                pe.wait_ge(S["series_steps"], h + 2)
                for i in range(HALF):
                    r = HALF * h + i
                    pe.matmul(product(h)[:, i, :], gen2_t[:, r, :], series[:, r, :], start=True, stop=False)
                    last = pe.matmul(product(h)[:, i, :], gen_t[:, r, :], ident[:], start=False, stop=True)
                last.then_inc(S["series_multiplied"], 1)

            def turn_e(k):
                for h in range(2):
                    if k == 0:
                        pe.wait_ge(S["exponential_taken"], h + 1)
                    else:
                        pe.wait_ge(S["squared_exponential_taken"], 2 * (k - 1) + h + 1)
                    for i in range(HALF):
                        pe.matmul(turn_bank(h)[:, i, :], e_sum[:, HALF * h + i, :], ident[:], start=True, stop=False)
                        last = pe.matmul(turn_bank(h)[:, i, :], eyes[:, 0, :], eyes[:, 0 if k == SQUARINGS else 1, :],
                                         start=False, stop=True)
                    last.then_inc(S["exponential_turned"], 1)

            def square(k):
                for h in range(2):
                    pe.wait_ge(S["turned_exponential_taken"], 2 * k + h + 1)
                    multiply(product(h), e_turn, e_sum, h).then_inc(S["exponential_squared"], 1)

            def to_features(c):
                pe.wait_ge(S["first_norms_steps"], 2 * ln_steps(NT // 2) * (c // 2 + 1))
                bank = c if c < 2 else 7
                if c == 2:
                    pe.wait_ge(S["rotation_multiplied"], 3)
                if c == 3:
                    pe.wait_ge(S["features_ready"], 2 * c)
                for t in range(TPC):
                    last = pe.transpose(ps[:, bank, t * P:(t + 1) * P], n2[:, c * TPC + t, :], ident[:])
                last.then_inc(S["features_turned"], 1)

            def gate_logits(c):
                pe.wait_ge(S["features_ready"], 2 * c + 1 if c < 2 else 2 * NC)
                for t in range(c * TPC, (c + 1) * TPC):
                    last = pe.matmul(ps[:, LOGIT_BANK[c // 2], t * NX:(t + 1) * NX], xn[:, t * P:(t + 1) * P], gw, start=True, stop=True)
                last.then_inc(S["logits_ready"], 1)

            pe.wait_ge(S["identities_made"], 3)
            for k in range(EARLY):
                turn_e(k)
                square(k)
                if k == 0:
                    pe.wait_ge(S["early_small_loaded"], 16 * N_SMALL)
                    pe.transpose(ps[:, 5, P:P + N_VEC], vec_rows, ident[0:N_VEC, 0:N_VEC]).then_inc(S["vectors_turned"], 1)
                if k == EARLY_FEATURES:
                    to_features(0)
                    to_features(1)
                if k == EARLY_FEATURES + 1:
                    gate_logits(0)
                    gate_logits(1)

            def weights_turned(c):
                bank = 2 + c if c < 2 else 7
                pe.wait_ge(S["padded_weights_ready"], 3 if c < 2 else 5)
                if c == 2:
                    pe.wait_ge(S["gate_tanh_ready"], 1)
                if c == 3:
                    pe.wait_ge(S["expert_weights_low_ready"], 1 + c)
                for t in range(TPC):
                    last = pe.transpose(ps[0:64, bank, t * P:(t + 1) * P], w_pad[:, c * TPC + t, :], ident[:])
                last.then_inc(S["expert_weights_turned"], 1)

            def chunk(a, c):
                return a[:, bass.ds(c * CH, CH)]

            def layer2(c, j):
                into = ps[:, 4 if j < NA else 5, :]
                pe.wait_ge(S["hidden_low_ready"], c * NB + (j + 1))
                if j == 0:
                    wait(pe, S["abel_ready"], c)
                if j == NA:
                    wait(pe, S["moe_low_ready"], c)
                w = slice(LAYER2[j], LAYER2[j] + P)
                r = j % RING
                end = j in (NA - 1, NB - 1)
                for k, (a, h) in enumerate(((w_hi, hid_hi), (w_lo, hid_hi), (w_hi, hid_lo))):
                    last = pe.matmul(into, a[:, w], h[:, r, :], start=(k == 0 and j in (0, NA)), stop=(end and k == 2 and j < NA))
                last.then_inc(S["second_layer_done"], 1)

            def section(c, cur, prev, first=False, second=False):
                for j in range(NB):
                    if cur:
                        wait(pe, S["hidden_ready"], c * NB + (j - 1))
                        w = slice(LAYER1[j], LAYER1[j] + P)
                        for k, (a, h) in enumerate(((w_hi, xn_hi), (w_lo, xn_hi), (w_hi, xn_lo))):
                            last = pe.matmul(ps[:, j % 2, :], a[:, w], chunk(h, c), start=(k == 0), stop=(k == 2))
                        last.then_inc(S["hidden_scores_ready"], 1)
                        if j >= NA and (j - NA) % NXB == 0:
                            e = (j - NA) // NXB
                            if first and e == 0:
                                pe.wait_ge(S["expert_weights_low_ready"], 1 + 2)
                            wait(pe, S["hidden_weighted"], c * (NB - NA) + NXB * (e - 1))
                            pe.matmul(ps[:, 2 + e % 2, :], pick[:, e, :], chunk(wt, c), start=True, stop=True).then_inc(S["expert_weight_spread"], 1)
                    if first and j == NA + LAG:
                        pe.wait_ge(S["logits_biased"], 1)
                        pe.wait_ge(S["weights_low_ready"], W_PARTS)
                    if cur and j >= LAG:
                        layer2(c, j - LAG)
                    if first and j == FIRST_WEIGHTS_AT:
                        for n in range(2):
                            weights_turned(n)
                    if second and j in FEATURES_AT:
                        to_features(FEATURES_AT[j])
                    if second and j == LOGITS_AT:
                        gate_logits(2)
                        gate_logits(3)
                    if second and j in WEIGHTS_AT:
                        weights_turned(WEIGHTS_AT[j])
                    if first and j in TURN_AT:
                        turn_e(TURN_AT[j])
                    if first and j in SQUARE_AT:
                        square(SQUARE_AT[j])
                    if first and j in PRODUCT_AT:
                        k = PRODUCT_AT[j]
                        if k == 0:
                            pe.wait_ge(S["last_exponential_ready"], 1)
                            pe.wait_ge(S["turned_exponential_taken"], 2 * (SQUARINGS + 1))
                        else:
                            pe.wait_ge(S["rotation_taken"], k)
                        pe.matmul(product(0)[:, 0, :], e_turn[:, NROT - 2 - k, :], rot[:, k - 1, :] if k else e_last[:],
                                  start=True, stop=True).then_inc(S["rotation_multiplied"], 1)
                    if prev and j < LAG:
                        layer2(c - 1, NB - LAG + j)
                        if j == LAG - 1:
                            pe.matmul(ps[:, 5, :], eb2_hi[:], chunk(wt, c - 1), start=False, stop=False)
                            pe.matmul(ps[:, 5, :], eb2_lo[:], chunk(wt, c - 1), start=False, stop=True).then_inc(S["moe_summed"], 1)
                    if prev and j == T_ROTATE:
                        pe.wait_ge(S["rotation_low_ready"], 1)
                        pe.wait_ge(S["moe_low_ready"], c)
                        wait(pe, S["second_residual_ready"], c - 1)
                        for k, (a, m) in enumerate(((rot_hi, moe_hi), (rot_lo, moe_hi), (rot_hi, moe_lo))):
                            last = pe.matmul(ps[:, 6, :], a[:], m[:], start=(k == 0), stop=(k == 2))
                        last.then_inc(S["moe_rotated"], 1)
                    if prev and j == T_NONABEL:
                        pe.wait_ge(S["abel_ready"], c)
                        pe.wait_ge(S["logits_biased"], 2)
                        wait(pe, S["gate_tanh_ready"], c - 1)
                        pe.matmul(ps[:, 7, :], gc_wide[:, 0, :], abel[:], start=True, stop=False)
                    if prev and j == T_GATE:
                        pe.wait_ge(S["nonabel_ready"], c)
                        pe.matmul(ps[:, 7, :], gc_wide[:, 1, :], nonabel[:], start=False, stop=True).then_inc(S["gate_summed"], 1)
                    if prev and j == T_TURN:
                        pe.wait_ge(S["mix_steps"], 3 * c)
                        for t in range(TPC):
                            last = pe.transpose(ps[:, 6, t * P:(t + 1) * P], mixed[:, t * P:(t + 1) * P], ident[:])
                        last.then_inc(S["mixed_turned"], 1)

            pe.wait_ge(S["residual_ready"], NC)
            pe.wait_ge(S["features_low_ready"], 2)
            pe.wait_ge(S["weights_low_ready"], LAYER2[NA] // PART)
            pe.wait_ge(S["features_ready"], 4)
            pe.wait_ge(S["pick_made"], 1)
            pe.wait_ge(S["weights_cleared"], 1)
            section(0, True, False, first=True)
            section(1, True, True, second=True)
            pe.wait_ge(S["expert_weights_low_ready"], 1 + NC)
            pe.wait_ge(S["features_low_ready"], NC)
            with pe.Fori(2, NC) as c:
                section(c, True, True)
            section(NC, False, True)


def transformer_block(nc, x, w_qkv, w_o, ln_g, ln_b, aw1, ab1, aw2, ab2, gate_w, gate_b, ew1, eb1, ew2, eb2,
                      gens, gc_w, gc_b, pe2, out):
    ffn_arrays = (x, ln_g, ln_b, aw1, ab1, aw2, ab2, gate_w, gate_b, ew1, eb1, ew2, eb2, gens, gc_w, gc_b)
    with ExitStack() as ctx:
        def sb(name, shape):
            return ctx.enter_context(nc.sbuf_tensor(name, shape, F32))

        acc = sb("acc", [P, T])
        ident = sb("ident", [P, P])
        pos = sb("pos", [P, T])
        qk = sb("qk", [P, 2, CH])
        v_all = sb("v_all", [P, H, NT, D])
        loaded = {name: ctx.enter_context(nc.semaphore(name)) for name in ("early_x_loaded", "early_generators_loaded",
                                                                     "early_small_loaded", "early_weights_loaded")}
        early = Early(pos, qk, v_all, loaded)
        attention(nc, acc, ident, pos, qk, v_all, x, w_qkv, w_o, pe2, lambda sp: early.load(sp, *ffn_arrays))
        feed_forward(nc, early, acc, ident, eb2, out)


_INS = ["L0_attn_x", "L0_attn_Wqkv", "L0_attn_Wo", "L0_ffn_ln_g", "L0_ffn_ln_b", "L0_ffn_aw1", "L0_ffn_ab1",
        "L0_ffn_aw2", "L0_ffn_ab2", "L0_ffn_gate_w", "L0_ffn_gate_b", "L0_ffn_ew1", "L0_ffn_eb1", "L0_ffn_ew2",
        "L0_ffn_eb2", "L0_ffn_gens", "L0_ffn_gc_w", "L0_ffn_gc_b"]


def position_table():
    import numpy as np

    pos = np.arange(T, dtype=np.float32)[:, None]
    div = np.exp(np.arange(0, D, 2, dtype=np.float32) * np.float32(-np.log(10000.0) / D))
    angle = pos * div
    table = np.stack([np.sin(angle), np.cos(angle)], axis=-1).reshape(T, D).astype(np.float32)
    return np.ascontiguousarray(np.concatenate([table.T, table.T], axis=0))


def kernel(**inputs):
    import concourse.bacc as bacc
    import numpy as np
    from concourse.bass_utils import run_bass_kernel_spmd

    nc = bacc.Bacc("TRN2", target_bir_lowering=False, num_devices=1)
    arrays = {name: np.ascontiguousarray(inputs[name]) for name in _INS}
    arrays["positions"] = position_table()
    args = [nc.dram_tensor(name, a.shape, F32, kind="ExternalInput").ap() for name, a in arrays.items()]
    args.append(nc.dram_tensor("out", (1, T, E), F32, kind="ExternalOutput").ap())
    transformer_block(nc, *args)
    result = run_bass_kernel_spmd(nc, [arrays], core_ids=[0])
    return result.results[0]["out"]
```
